# Optimizing a Trainium2 kernel written in Bass

```python
import numpy as np
import jax
import jax.numpy as jnp

def _softmax(x, axis=-1):
    return jax.nn.softmax(x, axis=axis)

def _gelu(x):
    return jax.nn.gelu(x, approximate=True)

def _silu(x):
    return jax.nn.silu(x)

def _sigmoid(x):
    return jax.nn.sigmoid(x)

def _layernorm(x, axis=-1, eps=1e-05):
    m = jnp.mean(x, axis=axis, keepdims=True)
    v = jnp.var(x, axis=axis, keepdims=True)
    return (x - m) / jnp.sqrt(v + eps)

def _scatter_add(tgt, idx, src, axis=0):
    return tgt.at[idx].add(src)

def _segment_sum(src, seg, n):
    return jax.ops.segment_sum(src, seg, n)
kernel_name = 'mk_perceiver_d1_seqx_r2_e221ca'

def setup_inputs(seed: int=0):
    np.random.seed(seed)
    _w = jnp.asarray

    def _rec_inputs():
        import jax
        import jax.numpy as jnp
        _rk = jax.random.key(seed)
        x = -0.0003929 + 0.9999 * jax.random.normal(jax.random.fold_in(_rk, 1), (32, 64, 512), jnp.float32)
        _lenS = 64 - jax.random.randint(jax.random.fold_in(_rk, 7), (32,), 0, max(1, 64 // 4) + 1, jnp.int32)
        _lenS2 = 512 - jax.random.randint(jax.random.fold_in(_rk, 8), (32,), 0, max(1, 512 // 4) + 1, jnp.int32)
        _ctx_768P = jax.random.normal(jax.random.fold_in(_rk, 11), (32, 16, 384), jnp.float32)
        _ctx_768c = jax.random.dirichlet(jax.random.fold_in(_rk, 511), 0.3 * jnp.ones((16,), jnp.float32), (32, 512))
        _ctx_768t = jnp.einsum('bsk,bkd->bsd', _ctx_768c, _ctx_768P)
        _ctx_768t = _ctx_768t * jax.lax.rsqrt(jnp.mean(jnp.square(_ctx_768t)) + 1e-12) * 0.953939
        ctx_768 = 0.00095986 + 0.999812 * (_ctx_768t + 0.3 * jax.random.normal(jax.random.fold_in(_rk, 611), (32, 512, 384), jnp.float32))
        _validS = jnp.arange(64)[None, :] < _lenS[:, None]
        _validS2 = jnp.arange(512)[None, :] < _lenS2[:, None]
        _causal = jnp.tril(jnp.ones((64, 64), dtype=bool))
        mask_BxS2_bf1 = jnp.ones((32, 512), dtype=bool)
        return (x, ctx_768, mask_BxS2_bf1)
    x, ctx_768, mask_BxS2_bf1 = _rec_inputs()

    def _L0_xattn_setup():
        import jax, jax.numpy as jnp
        import numpy as np
        DIM = 512
        CTX_DIM = 384
        HEADS = 16
        key = jax.random.key(seed)
        ks = jax.random.split(key, 7)
        B, N, M = (4, 2048, 128)
        x = jax.random.normal(ks[0], (B, N, DIM), dtype=jnp.float32)
        context = jax.random.normal(ks[1], (B, M, CTX_DIM), dtype=jnp.float32)
        context_mask = jnp.ones((B, M), dtype=bool)
        s_d = 1.0 / np.sqrt(DIM)
        s_c = 1.0 / np.sqrt(CTX_DIM)
        Wq = jax.random.normal(ks[2], (DIM, DIM), dtype=jnp.float32) * s_d
        Wk = jax.random.normal(ks[3], (CTX_DIM, DIM), dtype=jnp.float32) * s_c
        Wv = jax.random.normal(ks[4], (CTX_DIM, DIM), dtype=jnp.float32) * s_c
        Wo = jax.random.normal(ks[5], (DIM, DIM), dtype=jnp.float32) * s_d
        return {'x': x, 'context': context, 'context_mask': context_mask, 'Wq': Wq, 'Wk': Wk, 'Wv': Wv, 'Wo': Wo}
    _L0_xattn_all = _L0_xattn_setup()
    _L0_xattn_in = {k: v for k, v in _L0_xattn_all.items() if k in ('Wq', 'Wk', 'Wv', 'Wo')}
    del _L0_xattn_all

    def _L0_attn_setup():
        import jax, jax.numpy as jnp
        import numpy as np
        D_MODEL = 512
        NUM_HEADS = 16
        D_K = 512
        D_V = 512
        D_IN = 512
        THETA = 10000.0
        B, S = (2, 1024)

        def _rope(t, theta):
            hd = t.shape[-1]
            inv_freq = 1.0 / theta ** (jnp.arange(0, hd, 2, dtype=jnp.float32) / hd)
            pos = jnp.arange(t.shape[-2], dtype=jnp.float32)
            ang = pos[:, None] * inv_freq[None, :]
            cos, sin = (jnp.cos(ang), jnp.sin(ang))
            tp = t.reshape(t.shape[:-1] + (hd // 2, 2))
            t0, t1 = (tp[..., 0], tp[..., 1])
            out = jnp.stack([t0 * cos - t1 * sin, t0 * sin + t1 * cos], axis=-1)
            return out.reshape(t.shape)
        key = jax.random.key(seed)
        k1, k2, k3, k4, k5 = jax.random.split(key, 5)
        std_qkv = (2.0 / (D_IN + D_K)) ** 0.5
        std_o = (2.0 / (D_V + D_MODEL)) ** 0.5
        x = jax.random.normal(k1, (B, S, D_IN), jnp.float32)
        wq = jax.random.normal(k2, (D_IN, D_K), jnp.float32) * std_qkv
        wk = jax.random.normal(k3, (D_IN, D_K), jnp.float32) * std_qkv
        wv = jax.random.normal(k4, (D_IN, D_V), jnp.float32) * std_qkv
        wo = jax.random.normal(k5, (D_V, D_MODEL), jnp.float32) * std_o
        return {'x': x, 'wq': wq, 'wk': wk, 'wv': wv, 'wo': wo}
    _L0_attn_all = _L0_attn_setup()
    _L0_attn_in = {k: v for k, v in _L0_attn_all.items() if k in ('wq', 'wk', 'wv', 'wo')}
    del _L0_attn_all

    def _L0_ffn_setup():
        import jax, jax.numpy as jnp
        import numpy as np
        CAPACITY_FACTOR = 0.5
        key = jax.random.key(seed)
        ks = jax.random.split(key, 5)
        B, S, D, F = (4, 2048, 512, 2048)
        scale_in = 1.0 / np.sqrt(D)
        scale_ff = 1.0 / np.sqrt(F)
        return {'hidden_states': jax.random.normal(ks[0], (B, S, D), dtype=jnp.float32), 'w_router': jax.random.normal(ks[1], (D,), dtype=jnp.float32) * scale_in, 'W1': jax.random.normal(ks[2], (D, F), dtype=jnp.float32) * scale_in, 'b1': jnp.zeros((F,), dtype=jnp.float32), 'W2': jax.random.normal(ks[3], (F, D), dtype=jnp.float32) * scale_ff, 'b2': jnp.zeros((D,), dtype=jnp.float32)}
    _L0_ffn_all = _L0_ffn_setup()
    _L0_ffn_in = {k: v for k, v in _L0_ffn_all.items() if k in ('w_router', 'W1', 'b1', 'W2', 'b2')}
    del _L0_ffn_all
    return {'x': x, 'ctx_768': ctx_768, 'mask_BxS2_bf1': mask_BxS2_bf1, 'L0_xattn_Wq': _L0_xattn_in['Wq'], 'L0_xattn_Wk': _L0_xattn_in['Wk'], 'L0_xattn_Wv': _L0_xattn_in['Wv'], 'L0_xattn_Wo': _L0_xattn_in['Wo'], 'L0_attn_wq': _L0_attn_in['wq'], 'L0_attn_wk': _L0_attn_in['wk'], 'L0_attn_wv': _L0_attn_in['wv'], 'L0_attn_wo': _L0_attn_in['wo'], 'L0_ffn_w_router': _L0_ffn_in['w_router'], 'L0_ffn_W1': _L0_ffn_in['W1'], 'L0_ffn_b1': _L0_ffn_in['b1'], 'L0_ffn_W2': _L0_ffn_in['W2'], 'L0_ffn_b2': _L0_ffn_in['b2']}

def reference(x, ctx_768, mask_BxS2_bf1, L0_xattn_Wq, L0_xattn_Wk, L0_xattn_Wv, L0_xattn_Wo, L0_attn_wq, L0_attn_wk, L0_attn_wv, L0_attn_wo, L0_ffn_w_router, L0_ffn_W1, L0_ffn_b1, L0_ffn_W2, L0_ffn_b2):
    import jax
    import jax.numpy as jnp

    def _L0_xattn_ref(x, context, context_mask, Wq, Wk, Wv, Wo):
        import jax, jax.numpy as jnp
        import numpy as np
        DIM = 512
        CTX_DIM = 384
        HEADS = 16
        B, N, _ = x.shape
        M = context.shape[1]
        hd = DIM // HEADS
        scale = hd ** (-0.5)
        q = (x @ Wq).reshape(B, N, HEADS, hd).transpose(0, 2, 1, 3)
        k = (context @ Wk).reshape(B, M, HEADS, hd).transpose(0, 2, 1, 3)
        v = (context @ Wv).reshape(B, M, HEADS, hd).transpose(0, 2, 1, 3)
        scores = jnp.einsum('bhid,bhjd->bhij', q, k) * scale
        max_neg = -jnp.finfo(scores.dtype).max
        scores = jnp.where(context_mask[:, None, None, :], scores, max_neg)
        attn = jax.nn.softmax(scores, axis=-1)
        out = jnp.einsum('bhij,bhjd->bhid', attn, v)
        out = out.transpose(0, 2, 1, 3).reshape(B, N, DIM)
        return out @ Wo

    def _L0_attn_ref(x, wq, wk, wv, wo):
        import jax, jax.numpy as jnp
        import numpy as np
        D_MODEL = 512
        NUM_HEADS = 16
        D_K = 512
        D_V = 512
        D_IN = 512
        THETA = 10000.0
        B, S = (2, 1024)

        def _rope(t, theta):
            hd = t.shape[-1]
            inv_freq = 1.0 / theta ** (jnp.arange(0, hd, 2, dtype=jnp.float32) / hd)
            pos = jnp.arange(t.shape[-2], dtype=jnp.float32)
            ang = pos[:, None] * inv_freq[None, :]
            cos, sin = (jnp.cos(ang), jnp.sin(ang))
            tp = t.reshape(t.shape[:-1] + (hd // 2, 2))
            t0, t1 = (tp[..., 0], tp[..., 1])
            out = jnp.stack([t0 * cos - t1 * sin, t0 * sin + t1 * cos], axis=-1)
            return out.reshape(t.shape)
        b, s, _ = x.shape
        hd = D_K // NUM_HEADS
        hdv = D_V // NUM_HEADS
        q = jnp.einsum('bsd,de->bse', x, wq).reshape(b, s, NUM_HEADS, hd).transpose(2, 0, 1, 3)
        k = jnp.einsum('bsd,de->bse', x, wk).reshape(b, s, NUM_HEADS, hd).transpose(2, 0, 1, 3)
        v = jnp.einsum('bsd,de->bse', x, wv).reshape(b, s, NUM_HEADS, hdv).transpose(2, 0, 1, 3)
        q = _rope(q, THETA)
        k = _rope(k, THETA)
        scale = 1.0 / jnp.sqrt(jnp.asarray(hd, jnp.float32))
        scores = jnp.einsum('hbqd,hbkd->hbqk', q, k) * scale
        causal = jnp.tril(jnp.ones((s, s), dtype=bool))
        scores = jnp.where(causal, scores, -jnp.inf)
        attn = jax.nn.softmax(scores, axis=-1)
        o = jnp.einsum('hbqk,hbkd->hbqd', attn, v)
        o = o.transpose(1, 2, 0, 3).reshape(b, s, D_V)
        return jnp.einsum('bsd,de->bse', o, wo)

    def _L0_ffn_ref(hidden_states, w_router, W1, b1, W2, b2):
        import jax, jax.numpy as jnp
        import numpy as np
        CAPACITY_FACTOR = 0.5
        'Mixture-of-Depths block: route top-k tokens through an FFN inner block,\n            scatter back with sigmoid router weights; bypassed tokens pass through.'
        B, S, D = hidden_states.shape
        k = int(S * CAPACITY_FACTOR)
        scores = jnp.einsum('bsd,d->bs', hidden_states, w_router)
        top_scores, top_idx = jax.lax.top_k(scores, k)
        weights = jax.nn.sigmoid(top_scores)
        selected = jnp.take_along_axis(hidden_states, top_idx[:, :, None], axis=1)
        h = jax.nn.gelu(jnp.einsum('bkd,df->bkf', selected, W1) + b1)
        processed = jnp.einsum('bkf,fd->bkd', h, W2) + b2
        update = weights[:, :, None] * processed

        def scatter_one(xb, ib, ub):
            return xb.at[ib].add(ub)
        output = jax.vmap(scatter_one)(hidden_states, top_idx, update)
        return output
    x = x + _L0_xattn_ref(_layernorm(x, axis=-1), ctx_768, mask_BxS2_bf1, L0_xattn_Wq, L0_xattn_Wk, L0_xattn_Wv, L0_xattn_Wo)
    x = x + _L0_attn_ref(_layernorm(x, axis=-1), L0_attn_wq, L0_attn_wk, L0_attn_wv, L0_attn_wo)
    x = x + _L0_ffn_ref(_layernorm(x, axis=-1), L0_ffn_w_router, L0_ffn_W1, L0_ffn_b1, L0_ffn_W2, L0_ffn_b2)
    return x

_drawn_inputs = setup_inputs


def setup_inputs(seed=0):
    import zlib

    import numpy as np

    out = dict(_drawn_inputs(seed))
    spreads = {'L0_ffn_b1': (0.0, 0.571), 'L0_ffn_b2': (0.0, 0.398)}
    factors = {}
    for name, (base, spread) in spreads.items():
        noise = np.random.default_rng([zlib.crc32(name.encode()), seed]).standard_normal(out[name].shape)
        drawn = base * np.exp(spread * noise) if base else spread * noise
        out[name] = jnp.asarray(drawn.astype(out[name].dtype))
    for name, factor in factors.items():
        out[name] = (out[name] * factor).astype(out[name].dtype)
    return out
```

```python
from contextlib import ExitStack

import numpy as np

import concourse.bass as bass
from concourse import mybir

F32 = mybir.dt.float32
F32R = mybir.dt.float32r
U8 = mybir.dt.uint8
ALU = mybir.AluOpType
ACT = mybir.ActivationFunctionType
AX_X = mybir.AxisListType.X

P = 128
HEADS = 16
BIG = 1.0e30
LN_EPS = 1e-5


class Map:

    def __init__(self, nc, start):
        self.nc, self.at = nc, (start + 63) // 64 * 64

    def __call__(self, name, shape, dt):
        size = 1 if dt == U8 else 4
        for n in shape[1:]:
            size *= n
        t = self.nc.alloc_sbuf_tensor_at(name, shape, dt, offset=self.at)
        self.at += (size + 63) // 64 * 64
        return t


def perceiver_layer(nc, x, ctxT, mask, wq, wk, wv, wo, aq, ak, av, ao, router, w1, b1, w2, b2,
                    cos_tab, sin_tab, causal, same_in, before_in, slot_in, out, stop_after=None):
    B, SQ, D = x.shape
    _, C, SK = ctxT.shape
    HD = D // HEADS
    DT, CT, KT = D // P, C // P, SK // P
    G = B * SQ // P
    BPG = P // SQ
    CH = 4
    NCH = G // CH
    PAIRS = HEADS // 2
    SCALE = float(HD) ** -0.5
    xt = x.rearrange("b s d -> (b s) d").rearrange("(g p) d -> p g d", p=P)
    outt = out.rearrange("b s d -> (b s) d").rearrange("(g p) d -> p g d", p=P)

    stack = ExitStack()
    with stack:
        def sem(name):
            return stack.enter_context(nc.semaphore(name))

        s_stood = sem("stood")

        def settle(eng):
            eng.sem_inc(s_stood, 1)

        psum = stack.enter_context(nc.psum_tensor("psum", [P, 8, 512], F32))
        bank = [psum[:, i, :] for i in range(8)]

        def at_least(eng, sem, value):
            if not isinstance(value, int) or value > 0:
                eng.wait_ge(sem, value)

        always = Map(nc, nc.sbuf_base)
        tok = always("tok", [P, G, D], F32)
        ident = always("ident", [P, P], F32)
        epsb = always("epsb", [P, 1], F32)
        stats = always("stats", [P, CH, 6], F32)
        mv = always("mv", [P, CH, 2], F32)
        rstd = always("rstd", [P, CH], F32)
        base = always.at

        m = Map(nc, base)
        wk_h, wk_l = m("wk_h", [P, CT, D], F32R), m("wk_l", [P, CT, D], F32R)
        wv_h, wv_l = m("wv_h", [P, CT, D], F32R), m("wv_l", [P, CT, D], F32R)
        wo_h, wo_l = m("wo_h", [P, DT, D], F32R), m("wo_l", [P, DT, D], F32R)
        after_xw = m.at
        wq_r = m("wq_r", [P, DT, D], F32)
        wq_h, wq_l = m("wq_h", [P, DT, D], F32R), m("wq_l", [P, DT, D], F32R)
        wk_r, wv_r = m("wk_r", [P, CT, D], F32), m("wv_r", [P, CT, D], F32)
        wo_r = m("wo_r", [P, DT, D], F32)
        xn = m("xn", [P, CH, D], F32)
        xnT_h, xnT_l = m("xnT_h", [P, DT, CH * P], F32R), m("xnT_l", [P, DT, CH * P], F32R)

        s_w = sem("p1_w")
        s_wkv = [sem(f"p1_w{i}") for i in range(3)]
        s_x = [sem(f"p1_x{i}") for i in range(NCH)]
        s_id = sem("p1_id")
        s_eps = sem("p1_eps")
        s_st, s_var, s_sd, s_rs, s_xn = sem("p1_st"), sem("p1_var"), sem("p1_sd"), sem("p1_rs"), sem("p1_xn")
        s_tr, s_hi, s_lo, s_q, s_qe = sem("p1_tr"), sem("p1_hi"), sem("p1_lo"), sem("p1_q"), sem("p1_qe")
        s_wh, s_wl = sem("p1_wh"), sem("p1_wl")
        s_pw = sem("p1_pw")

        with nc.Block() as block:
            @block.sync
            def _(sp):
                for c in range(NCH):
                    sp.dma_start(tok[:, c * CH:(c + 1) * CH, :], xt[:, c * CH:(c + 1) * CH, :]).then_inc(s_x[c], 16)
                    if c == 0:
                        sp.dma_start(wq_r[:], wq.rearrange("(t p) n -> p t n", p=P)).then_inc(s_w, 16)
                for i, (r, w) in enumerate(((wk_r, wk), (wv_r, wv), (wo_r, wo))):
                    sp.dma_start(r[:], w.rearrange("(t p) n -> p t n", p=P)).then_inc(s_wkv[i], 16)

            @block.gpsimd
            def _(pool):
                pool.memset(ident[:], 0.0).then_inc(s_id, 1)
                pool.memset(epsb[:], LN_EPS).then_inc(s_eps, 1)
                pool.wait_ge(s_id, 1)
                pool.affine_select(out=ident[:], in_=ident[:], compare_op=ALU.not_equal, fill=1.0, base=0,
                                   pattern=[[-1, P]], channel_multiplier=1).then_inc(s_id, 1)
                n = 0
                for i, (r, h, l) in enumerate(((wk_r, wk_h, wk_l), (wv_r, wv_h, wv_l), (wo_r, wo_h, wo_l))):
                    pool.wait_ge(s_wkv[i], 16)
                    pool.tensor_scalar(h[:], r[:], 1.0, None, ALU.mult).then_inc(s_pw, 1)
                    n += 1
                    pool.wait_ge(s_pw, n)
                    pool.tensor_tensor(l[:], r[:], h[:].bitcast(F32), ALU.subtract).then_inc(s_pw, 1)
                    n += 1
                pool.wait_ge(s_pw, n)

            @block.vector
            def _(dve):
                for c in range(NCH):
                    dve.wait_ge(s_x[c], 16)
                    if c >= 1:
                        dve.wait_ge(s_xn, 4 * c)
                    for t in range(CH):
                        dve.bn_stats(stats[:, t, :], tok[:, c * CH + t, :]).then_inc(s_st, 1)
                    for t in range(CH):
                        dve.wait_ge(s_st, CH * c + t + 1)
                        dve.bn_aggr(mv[:, t, :], stats[:, t, :]).then_inc(s_var, 1)
                    dve.wait_ge(s_sd, c + 1)
                    dve.reciprocal(rstd[:], rstd[:]).then_inc(s_rs, 1)
                    dve.wait_ge(s_rs, c + 1)
                    if c >= 1:
                        dve.wait_ge(s_tr, DT * c)
                    for t in range(CH):
                        dve.tensor_scalar(xn[:, t, :], tok[:, c * CH + t, :], mv[:, t, 0:1], rstd[:, t:t + 1],
                                          ALU.subtract, ALU.mult).then_inc(s_xn, 1)
                    if c == 0:
                        dve.wait_ge(s_wh, 1)
                        dve.tensor_tensor(wq_l[:], wq_r[:], wq_h[:].bitcast(F32), ALU.subtract).then_inc(s_wl, 1)
                    for k in range(DT):
                        dve.wait_ge(s_hi, DT * c + k + 1)
                        dve.tensor_tensor(xnT_l[:, k, :], bank[k][:], xnT_h[:, k, :].bitcast(F32),
                                          ALU.subtract).then_inc(s_lo, 1)

            @block.scalar
            def _(act):
                act.wait_ge(s_eps, 1)
                act.wait_ge(s_w, 16)
                act.activation(wq_h[:], wq_r[:], ACT.Copy).then_inc(s_wh, 1)
                for c in range(NCH):
                    act.wait_ge(s_var, CH * (c + 1))
                    if c >= 1:
                        act.wait_ge(s_xn, CH * c)
                    act.activation(rstd[:], mv[:, :, 1], ACT.Sqrt, bias=epsb[:]).then_inc(s_sd, 1)
                    if c >= 1:
                        act.wait_ge(s_q, DT * c)
                    for k in range(DT):
                        act.wait_ge(s_tr, DT * c + k + 1)
                        act.activation(xnT_h[:, k, :], bank[k][:], ACT.Copy).then_inc(s_hi, 1)
                    act.wait_ge(s_xn, CH * (c + 1))
                    for mt in range(DT):
                        act.wait_ge(s_q, DT * c + mt + 1)
                        act.activation(
                            tok[:, c * CH:(c + 1) * CH, mt * P:(mt + 1) * P],
                            bank[4 + mt][:].rearrange("p (t n) -> p t n", t=CH), ACT.Copy).then_inc(s_qe, 1)
                act.wait_ge(s_qe, DT * NCH)

            @block.tensor
            def _(pe):
                pe.wait_ge(s_id, 2)
                for c in range(NCH):
                    pe.wait_ge(s_xn, CH * (c + 1))
                    if c >= 1:
                        pe.wait_ge(s_lo, DT * c)
                    for k in range(DT):
                        for t in range(CH):
                            i = pe.transpose(bank[k][:, t * P:(t + 1) * P], xn[:, t, k * P:(k + 1) * P], ident[:])
                        i.then_inc(s_tr, 1)
                    if c == 0:
                        pe.wait_ge(s_wl, 1)
                    pe.wait_ge(s_lo, DT * (c + 1))
                    for mt in range(DT):
                        if c >= 1:
                            pe.wait_ge(s_qe, DT * (c - 1) + mt + 1)
                        for k in range(DT):
                            for w, y in ((wq_h, xnT_h), (wq_h, xnT_l), (wq_l, xnT_h)):
                                i = pe.matmul(bank[4 + mt][:], w[:, k, mt * P:(mt + 1) * P], y[:, k, :],
                                              start=(k == 0 and w is wq_h and y is xnT_h),
                                              stop=(k == DT - 1 and w is wq_l))
                        i.then_inc(s_q, 1)

        m = Map(nc, after_xw)
        xres = m("xres", [P, 1, D], F32)
        KT_h, KT_l = m("KT_h", [P, DT, SK], F32R), m("KT_l", [P, DT, SK], F32R)
        V_h, V_l = m("V_h", [P, 2, KT, D], F32R), m("V_l", [P, 2, KT, D], F32R)
        ctx_r = m("ctx_r", [P, CT, SK], F32)
        ctx_h, ctx_l = m("ctx_h", [P, 2, CT, SK], F32R), m("ctx_l", [P, 2, CT, SK], F32R)
        qz_h, qz_l = m("qz_h", [P, DT, 2, 2, SQ], F32R), m("qz_l", [P, DT, 2, 2, SQ], F32R)
        prob = m("prob", [P, 2, SK], F32)
        PT_h, PT_l = m("PT_h", [P, 2, KT, 2, P], F32R), m("PT_l", [P, 2, KT, 2, P], F32R)
        OT_h, OT_l = m("OT_h", [P, DT, BPG, SQ], F32R), m("OT_l", [P, DT, BPG, SQ], F32R)
        mask8 = m("mask8", [P, BPG, SK], U8)
        mbias = m("mbias", [P, BPG, SK], F32)
        mx, nmx = m("mx", [P, 4], F32), m("nmx", [P, 4], F32)
        rsum, rinv = m("rsum", [P, 4], F32), m("rinv", [P, 4], F32)
        assert m.at <= nc.sbuf_usable_end, m.at

        s_raw = sem("p2_ctx")
        s_mraw = [sem(f"p2_mask{i}") for i in range(BPG)]
        s_xr = sem("p2_xres")
        s_z = sem("p2_zero")
        s_cx = sem("p2_cx")
        s_qz = sem("p2_qz")
        s_mb = sem("p2_mb")
        s_S, s_KV, s_T, s_PV, s_Wo = sem("p2_S"), sem("p2_KV"), sem("p2_T"), sem("p2_PV"), sem("p2_Wo")
        s_mx, s_nm, s_ex, s_ri, s_pn = sem("p2_mx"), sem("p2_nm"), sem("p2_ex"), sem("p2_ri"), sem("p2_pn")
        s_Th, s_Tl, s_KVh, s_KVl = sem("p2_Th"), sem("p2_Tl"), sem("p2_KVh"), sem("p2_KVl")
        s_Oh, s_Ol = sem("p2_Oh"), sem("p2_Ol")
        s_x1 = sem("p2_x1")
        S_bank, KV_bank, T_bank, PV_bank, Wo_bank = bank[0:2], bank[2:4], bank[4], bank[5], bank[6]

        SPT = BPG * PAIRS
        AHEAD = 6
        TILES = KT + DT
        KV_ORDER = [("V", 0), ("K", 0), ("V", 1), ("K", 1), ("V", 2), ("V", 3), ("K", 2), ("K", 3)]
        K_READY = [2, 4, 7, 8]
        GROUPS = BPG * DT
        PRODUCTS = 3

        def group(j, lag):
            n = (j - lag) // 2
            return n, n % DT, (n % GROUPS) // DT

        def kv_tile(k, low):
            kind, t = KV_ORDER[k % TILES]
            if kind == "K":
                return (KT_l if low else KT_h)[:, t, :]
            return (V_l if low else V_h)[:, (k // TILES) % 2, t, :]

        def pt_half(j, low):
            return (PT_l if low else PT_h)[:, (j // 2) % 2, :, j % 2, :]

        def heads_of(psum, r):
            return psum[r * HD:(r + 1) * HD, r * SQ:(r + 1) * SQ]

        def pe_kv(pe, g, k, first):
            b, t = k // TILES, KV_ORDER[k % TILES][1]
            if k % TILES == 0:
                pe.wait_ge(s_cx, g * (2 * BPG) + 2 * b + 2)
            if not (first and k < 2):
                pe.wait_ge(s_KVl, g * SPT + (k - 1))
            for c in range(CT):
                if KV_ORDER[k % TILES][0] == "K":
                    parts = ((wk_h, ctx_h), (wk_l, ctx_h), (wk_h, ctx_l))
                    ops = [(w[:, c, t * P:(t + 1) * P], y[:, b % 2, c, :]) for w, y in parts]
                else:
                    parts = ((ctx_h, wv_h), (ctx_h, wv_l), (ctx_l, wv_h))
                    ops = [(y[:, b % 2, c, t * P:(t + 1) * P], w[:, c, :]) for y, w in parts]
                for i, (stat, mov) in enumerate(ops):
                    ins = pe.matmul(KV_bank[k % 2][:], stat, mov, start=(c == 0 and i == 0),
                                    stop=(c == CT - 1 and i == PRODUCTS - 1))
            ins.then_inc(s_KV, 1)

        def pe_slot(pe, g, j, first=False, last=False, tail=False):
            s = g * SPT + j
            b, p = j // PAIRS, j % PAIRS
            if not tail:
                if p % 4 == 0:
                    pe.wait_ge(s_qz, g * (BPG * 16) + b * 16 + (p // 4 + 1) * 8)
                if p % 2 == 0:
                    pe.wait_ge(s_KVl, g * SPT + b * TILES + K_READY[p // 2])
                if not (first and j < 2):
                    pe.wait_ge(s_mx, s - 1)
                for i, (q, k) in enumerate(((qz_h, KT_h), (qz_h, KT_l), (qz_l, KT_h))):
                    ins = pe.matmul(S_bank[j % 2][:], q[:, p // 2, p % 2, :, :].rearrange("p a b -> p (a b)"),
                                    k[:, p // 2, :], start=(i == 0), stop=(i == PRODUCTS - 1))
                ins.then_inc(s_S, 1)
                if not (last and j + AHEAD >= SPT):
                    pe_kv(pe, g, j + AHEAD, first)
            if j == 2 and not first:
                pe.wait_ge(s_Ol, g * (4 * GROUPS))
                pe.wait_ge(s_x1, g)
                for n in range(DT):
                    for i, (o, w) in enumerate(((OT_h, wo_h), (OT_l, wo_h), (OT_h, wo_l))):
                        ins = pe.matmul(Wo_bank[:], o[:, n, :, :].rearrange("p a b -> p (a b)"), w[:, n, :],
                                        start=(n == 0 and i == 0), stop=(n == DT - 1 and i == PRODUCTS - 1))
                ins.then_inc(s_Wo, 1)
            if not (first and j == 0) and not (tail and j > 0):
                pe.wait_ge(s_pn, s)
                if not (first and j == 1):
                    pe.wait_ge(s_Tl, s - 1)
                for kt in range(KT):
                    ins = pe.transpose(T_bank[:, kt * P:(kt + 1) * P],
                                       prob[:, (j - 1) % 2, kt * P:(kt + 1) * P], ident[:])
                ins.then_inc(s_T, 1)
            if j % 2 == 1 and not (first and j == 1) and not (tail and j > 1):
                n, quarter, odd = group(j, 3)
                pe.wait_ge(s_Tl, s - 1)
                if not (first and n == 0):
                    pe.wait_ge(s_Ol, g * (4 * GROUPS) + 4 * n)
                for kt in range(KT):
                    for i, (v, t) in enumerate(((V_h, PT_h), (V_h, PT_l), (V_l, PT_h))):
                        ins = pe.matmul(PV_bank[:, 0:2 * P], v[:, odd, kt, quarter * P:(quarter + 1) * P],
                                        t[:, n % 2, kt, :, :].rearrange("p a b -> p (a b)"),
                                        start=(kt == 0 and i == 0), stop=(kt == KT - 1 and i == PRODUCTS - 1))
                ins.then_inc(s_PV, 1)

        def act_kv(act, g, k):
            act.wait_ge(s_KV, g * SPT + k + 1)
            act.activation(kv_tile(k, False), KV_bank[k % 2][:], ACT.Copy).then_inc(s_KVh, 1)

        def dve_kv(dve, g, k):
            dve.wait_ge(s_KVh, g * SPT + k + 1)
            dve.tensor_tensor(kv_tile(k, True), KV_bank[k % 2][:], kv_tile(k, False).bitcast(F32),
                              ALU.subtract).then_inc(s_KVl, 1)

        def act_slot(act, g, j, first=False, last=False, tail=False):
            s = g * SPT + j
            if not (first and j < 2) and not (tail and j > 1):
                act.wait_ge(s_T, s - 1)
                if not (first and j < 6):
                    act.wait_ge(s_PV, g * GROUPS + (j - 2) // 2 - 1)
                act.activation(pt_half(j - 2, False), T_bank[:].rearrange("p (k n) -> p k n", k=KT),
                               ACT.Copy).then_inc(s_Th, 1)
            if j % 2 == 0 and not (first and j < 4) and not (tail and j > 2):
                n, quarter, odd = group(j, 4)
                act.wait_ge(s_PV, g * GROUPS + n + 1)
                if n == 0 and not first:
                    act.wait_ge(s_Wo, g)
                for r in range(4):
                    act.activation(OT_h[r * HD:(r + 1) * HD, quarter, odd, :], heads_of(PV_bank, r),
                                   ACT.Copy).then_inc(s_Oh, 1)
            if tail:
                return
            if not (last and j - 1 + AHEAD >= SPT) and not (first and j == 0):
                act_kv(act, g, j - 1 + AHEAD)
            c = slice(j % 4, j % 4 + 1)
            act.wait_ge(s_nm, s + 1)
            act.activation(prob[:, j % 2, :], prob[:, j % 2, :], ACT.Exp, bias=nmx[:, c], scale=SCALE,
                           accum_out=rsum[:, c]).then_inc(s_ex, 1)
            act.wait_ge(s_ri, s + 1)
            act.activation(prob[:, j % 2, :], prob[:, j % 2, :], ACT.Copy, scale=rinv[:, c]).then_inc(s_pn, 1)

        def dve_slot(dve, g, j, first=False, last=False, tail=False):
            s = g * SPT + j
            c = slice(j % 4, j % 4 + 1)
            if not tail:
                dve.wait_ge(s_S, s + 1)
                if not (first and j < 2):
                    dve.wait_ge(s_T, s - 1)
                if j % PAIRS == 0:
                    dve.wait_ge(s_mb, g * BPG + j // PAIRS + 1)
                settle(dve)
                dve.tensor_tensor_reduce(prob[:, j % 2, :], S_bank[j % 2][:], mbias[:, j // PAIRS, :], 1.0,
                                         -3.0e38, ALU.add, ALU.max, mx[:, c]).then_inc(s_mx, 1)
                dve.wait_ge(s_mx, s + 1)
                dve.tensor_scalar(nmx[:, c], mx[:, c], -SCALE, None, ALU.mult).then_inc(s_nm, 1)
            if not (first and j < 2) and not (tail and j > 1):
                dve.wait_ge(s_Th, s - 1)
                dve.tensor_tensor(pt_half(j - 2, True), T_bank[:].rearrange("p (k n) -> p k n", k=KT),
                                  pt_half(j - 2, False).bitcast(F32), ALU.subtract).then_inc(s_Tl, 1)
            if j % 2 == 0 and not (first and j < 4) and not (tail and j > 2):
                n, quarter, odd = group(j, 4)
                dve.wait_ge(s_Oh, g * (4 * GROUPS) + 4 * n + 4)
                for r in range(4):
                    rows = slice(r * HD, (r + 1) * HD)
                    dve.tensor_tensor(OT_l[rows, quarter, odd, :], heads_of(PV_bank, r),
                                      OT_h[rows, quarter, odd, :].bitcast(F32), ALU.subtract).then_inc(s_Ol, 1)
            if j == 3 and not first:
                dve.wait_ge(s_Wo, g)
                dve.wait_ge(s_xr, g * 16)
                dve.tensor_tensor(tok[:, bass.ds(g - 1, 1), :], Wo_bank[:].rearrange("p (a n) -> p a n", a=1),
                                  xres[:], ALU.add).then_inc(s_x1, 1)
            if tail:
                return
            dve.wait_ge(s_ex, s + 1)
            dve.reciprocal(rinv[:, c], rsum[:, c]).then_inc(s_ri, 1)
            if not (last and j - 1 + AHEAD >= SPT) and not (first and j == 0):
                dve_kv(dve, g, j - 1 + AHEAD)

        def sp_tile(sp, g, first=False, last=False):
            for b in range(BPG):
                n = g * BPG + b
                if not (first and b == 0):
                    sp.wait_ge(s_cx, n * 2)
                settle(sp)
                sp.dma_start(ctx_r[:], ctxT[bass.ds(n, 1), :, :].rearrange("a (t p) n -> p (a t) n", p=P))\
                    .then_inc(s_raw, 16)
                if not first:
                    sp.wait_ge(s_mb, n - 1)
                settle(sp)
                sp.dma_start(mask8[:, b, :], mask[bass.ds(n, 1), :].broadcast_to([P, SK])).then_inc(s_mraw[b], 16)
            if not first:
                sp.wait_ge(s_x1, g + 1)
            settle(sp)
            sp.dma_start(xres[:], xt[:, bass.ds(g, 1), :]).then_inc(s_xr, 16)

        def pool_ctx(pool, g, b, first):
            n = g * BPG + b
            pool.wait_ge(s_raw, n * 16 + 16)
            if not (first and b == 0):
                pool.wait_ge(s_qz, (n - 1) * 16 + 8)
            if not (first and b < 2):
                pool.wait_ge(s_KV, (n - 1) * TILES)
            settle(pool)
            pool.tensor_scalar(ctx_h[:, b % 2, :, :], ctx_r[:], 1.0, None, ALU.mult).then_inc(s_cx, 1)
            pool.wait_ge(s_cx, n * 2 + 1)
            settle(pool)
            pool.tensor_tensor(ctx_l[:, b % 2, :, :], ctx_r[:], ctx_h[:, b % 2, :, :].bitcast(F32),
                               ALU.subtract).then_inc(s_cx, 1)

        def pool_q(pool, g, b, half, first, last):
            n = g * BPG + b
            if not (first and b == 0):
                pool.wait_ge(s_S, n * PAIRS - 4 + 4 * half)
            qt = tok[:, bass.ds(g, 1), :].rearrange("p a (n b q) -> p (a n) b q", n=DT, b=BPG)
            t = slice(2 * half, 2 * half + 2)
            for low in (0, 1):
                for r in range(4):
                    rows = slice(r * HD, (r + 1) * HD)
                    src, dst = qt[rows, t, b, :], qz_h[rows, t, r // 2, r % 2, :]
                    if low or r:
                        pool.wait_ge(s_qz, n * 16 + half * 8 + 4 * low + r)
                    elif half == 0:
                        pool.wait_ge(s_mb, n + 1)
                    elif not last or b < BPG - 1:
                        pool.wait_ge(s_cx, n * 2 + 4)
                    settle(pool)
                    if low:
                        ins = pool.tensor_tensor(qz_l[rows, t, r // 2, r % 2, :], src, dst.bitcast(F32), ALU.subtract)
                    else:
                        ins = pool.tensor_copy(dst, src)
                    ins.then_inc(s_qz, 1)

        def pool_mask(pool, g, b, first):
            n = g * BPG + b
            pool.wait_ge(s_mraw[b], g * 16 + 16)
            if not first:
                pool.wait_ge(s_mx, (n - 1) * PAIRS)
            if not (first and b == 0):
                pool.wait_ge(s_qz, n * 16)
            settle(pool)
            pool.tensor_scalar(mbias[:, b, :], mask8[:, b, :], -1.0, BIG, ALU.add, ALU.mult).then_inc(s_mb, 1)

        def pool_tile(pool, g, first=False, last=False):
            for b in range(BPG):
                pool_mask(pool, g, b, first)
                pool_q(pool, g, b, 0, first, last)
                if not (last and b == BPG - 1):
                    pool_ctx(pool, g, b + 1, first)
                pool_q(pool, g, b, 1, first, last)

        def tiles(eng, tile):
            tile(0, True, False)
            with eng.Fori(1, G - 1) as g:
                tile(g, False, False)
            tile(G - 1, False, True)

        with nc.Block() as block:
            @block.sync
            def _(sp):
                tiles(sp, lambda g, first, last: sp_tile(sp, g, first, last))

            @block.gpsimd
            def _(pool):
                pool.memset(qz_h[:].bitcast(F32), 0.0).then_inc(s_z, 1)
                pool.memset(qz_l[:].bitcast(F32), 0.0).then_inc(s_z, 1)
                pool_ctx(pool, 0, 0, True)
                pool.wait_ge(s_z, 2)
                tiles(pool, lambda g, first, last: pool_tile(pool, g, first, last))

            @block.tensor
            def _(pe):
                def tile(g, first, last):
                    for j in range(SPT):
                        pe_slot(pe, g, j, first, last)
                for k in range(AHEAD):
                    pe_kv(pe, 0, k, True)
                tiles(pe, tile)
                for j in range(4):
                    pe_slot(pe, G, j, tail=True)

            @block.scalar
            def _(act):
                def tile(g, first, last):
                    for j in range(SPT):
                        act_slot(act, g, j, first, last)
                for k in range(AHEAD):
                    act_kv(act, 0, k)
                tiles(act, tile)
                for j in range(4):
                    act_slot(act, G, j, tail=True)

            @block.vector
            def _(dve):
                def tile(g, first, last):
                    for j in range(SPT):
                        dve_slot(dve, g, j, first, last)
                dve.sem_inc(s_x1, 1)
                for k in range(AHEAD):
                    dve_kv(dve, 0, k)
                tiles(dve, tile)
                for j in range(4):
                    dve_slot(dve, G, j, tail=True)

        if stop_after == 2:
            s_dbg = sem("dbg")
            with nc.Block() as block:
                @block.sync
                def _(sp):
                    sp.dma_start(outt, tok[:]).then_inc(s_dbg, 16)
                    sp.wait_ge(s_dbg, 16)
            return

        m = Map(nc, base)
        qw_h, qw_l = m("aq_h", [P, DT, D], F32R), m("aq_l", [P, DT, D], F32R)
        kw_h, kw_l = m("ak_h", [P, DT, D], F32R), m("ak_l", [P, DT, D], F32R)
        vw_h, vw_l = m("av_h", [P, DT, D], F32R), m("av_l", [P, DT, D], F32R)
        ow = m("ao_sb", [P, DT, D], F32)
        raw3 = m("raw3", [P, 3, DT, D], F32)
        st3, mv3 = m("st3", [P, G, 6], F32), m("mv3", [P, G, 2], F32)
        rs3 = m("rs3", [P, G], F32)
        cur = m("cur", [P, 3], F32)
        xn3 = m("xn3", [P, D], F32)
        x3_h, x3_l = m("x3_h", [P, 2, DT, P], F32R), m("x3_l", [P, 2, DT, P], F32R)
        rope = m("rope", [P, 2, HD], F32)
        r_cos, r_sin = m("r_cos", [P, D], F32), m("r_sin", [P, D], F32)
        q_r, k_r = m("q_r", [P, D], F32), m("k_r", [P, D], F32)
        v_sb = m("v_sb", [P, 2, D], F32)
        qb = m("qb", [P, DT, BPG, 4, SQ], F32)
        k_T = m("k_T", [P, DT, P], F32)
        cmask = m("cmask", [P, SQ], F32)
        sm = m("sm", [P, 2, DT, 2, BPG, SQ], F32)
        mx3, rc3 = m("mx3", [P, HEADS], F32), m("rc3", [P, 2, HEADS], F32)
        pb = m("pb", [P, DT, BPG, 2, P], F32)
        o_T = m("o_T", [P, DT, BPG, SQ], F32)
        assert m.at <= nc.sbuf_usable_end, m.at

        s3_w = [sem(f"p3_w{i}") for i in range(4)]
        s3_c = sem("p3_const")
        s3_ws = sem("p3_ws")
        s3_z = sem("p3_z")
        s3_st, s3_mv, s3_sd, s3_rs = sem("p3_st"), sem("p3_mv"), sem("p3_sd"), sem("p3_rs")
        s3_cu, s3_xn, s3_XT, s3_xh, s3_xl = sem("p3_cu"), sem("p3_xn"), sem("p3_XT"), sem("p3_xh"), sem("p3_xl")
        s3_Q, s3_K, s3_V, s3_Tq, s3_Tk = sem("p3_Q"), sem("p3_K"), sem("p3_V"), sem("p3_Tq"), sem("p3_Tk")
        s3_rq, s3_rk, s3_aq, s3_ak = sem("p3_rq"), sem("p3_rk"), sem("p3_aq"), sem("p3_ak")
        s3_v = sem("p3_v")
        s3_qa, s3_qd, s3_kT = sem("p3_qa"), sem("p3_qd"), sem("p3_kT")
        s3_S, s3_ms, s3_mx, s3_su, s3_ex = sem("p3_S"), sem("p3_ms"), sem("p3_mx"), sem("p3_su"), sem("p3_ex")
        s3_sm, s3_rc, s3_pn = sem("p3_sum"), sem("p3_rc"), sem("p3_pn")
        s3_PT, s3_pa, s3_pd = sem("p3_PT"), sem("p3_pa"), sem("p3_pd")
        s3_PV, s3_oa, s3_od, s3_Wo, s3_x = sem("p3_PV"), sem("p3_oa"), sem("p3_od"), sem("p3_Wo"), sem("p3_x")

        def has(t):
            return not isinstance(t, int) or 0 <= t < G

        def one_tile(t):
            return tok[:, bass.ds(t, 1), :].rearrange("p a n -> p (a n)")

        def project(pe, b, y_h, y_l, w_h, w_l):
            for k in range(DT):
                for i, (y, w) in enumerate(((y_h, w_h), (y_h, w_l), (y_l, w_h))):
                    ins = pe.matmul(b, y[:, k, :], w[:, k, :], start=(k == 0 and i == 0),
                                    stop=(k == DT - 1 and i == PRODUCTS - 1))
            return ins

        def pe3(pe, t, par):
            nxt = 1 - par
            if has(t):
                pe.wait_ge(s3_aq, t + 1)
                at_least(pe, s3_xl, t + 2 if not isinstance(t, int) else min(t + 2, G))
                for n in range(DT):
                    ins = pe.transpose(bank[0][:, n * P:(n + 1) * P], q_r[:, n * P:(n + 1) * P], ident[:])
                ins.then_inc(s3_Tq, 1)
                pe.wait_ge(s3_ak, t + 1)
                for n in range(DT):
                    ins = pe.transpose(bank[1][:, n * P:(n + 1) * P], k_r[:, n * P:(n + 1) * P], ident[:])
                ins.then_inc(s3_Tk, 1)
            if has(t + 1):
                at_least(pe, s3_xl, t + 2)
                at_least(pe, s3_v, t + 1)
                if isinstance(t, int) and t == -1:
                    pe.wait_ge(s3_ws, 2)
                project(pe, bank[2], x3_h[:, nxt, :, :], x3_l[:, nxt, :, :], qw_h, qw_l).then_inc(s3_Q, 1)
            if has(t):
                pe.wait_ge(s3_kT, t + 1)
                pe.wait_ge(s3_qa, 2 * t + 2)
                pe.wait_ge(s3_qd, 2 * t + 2)
                for n in range(DT):
                    if n < 2:
                        at_least(pe, s3_oa, 4 * t - 4)
                        at_least(pe, s3_od, 4 * t - 4)
                    else:
                        pe.wait_ge(s3_ms, 4 * t + n - 1)
                    for b in range(BPG):
                        for pl in range(2):
                            at = pl * 2 * P + b * SQ
                            ins = pe.matmul(bank[4 + n % 2][:, at:at + P],
                                            qb[:, n, b, 2 * pl:2 * pl + 2, :].rearrange("p a b -> p (a b)"), k_T[:, n, :],
                                            start=True, stop=True)
                    ins.then_inc(s3_S, 1)
            if has(t + 1):
                at_least(pe, s3_x, t - 1)
                if isinstance(t, int) and t == -1:
                    pe.wait_ge(s3_ws, 4)
                project(pe, bank[3], x3_h[:, nxt, :, :], x3_l[:, nxt, :, :], kw_h, kw_l).then_inc(s3_K, 1)
            if has(t - 1):
                pe.wait_ge(s3_pn, t)
                for h in range(2):
                    for i in range(4):
                        n, pl = 2 * h + i // 2, i % 2
                        ins = pe.transpose(bank[h][:, i * P:(i + 1) * P],
                                           sm[:, nxt, n, pl, :, :].rearrange("p b k -> p (b k)"), ident[:])
                    ins.then_inc(s3_PT, 1)
                pe.wait_ge(s3_v, t)
                for n in range(DT):
                    if n % 2 == 0:
                        pe.wait_ge(s3_pa, 2 * t - 1 + n // 2)
                        pe.wait_ge(s3_pd, 2 * t - 1 + n // 2)
                    if n == 0:
                        at_least(pe, s3_oa, 4 * (t - 1) - 2)
                        at_least(pe, s3_od, 4 * (t - 1) - 2)
                    if n == 2 and has(t):
                        pe.wait_ge(s3_ms, 4 * t + 4)
                    ins = pe.matmul(bank[(6, 7, 4, 5)[n]], v_sb[:, nxt, n * P:(n + 1) * P],
                                    pb[:, n, :, :, :].rearrange("p a b c -> p (a b c)"), start=True, stop=True)
                    if n % 2:
                        ins.then_inc(s3_PV, 1)
            if has(t + 2):
                at_least(pe, s3_xn, t + 3)
                if has(t - 1):
                    pe.wait_ge(s3_pa, 2 * t)
                    pe.wait_ge(s3_pd, 2 * t)
                for k in range(DT):
                    ins = pe.transpose(bank[0][:, k * P:(k + 1) * P], xn3[:, k * P:(k + 1) * P], ident[:])
                ins.then_inc(s3_XT, 1)
            if has(t + 1):
                pe.wait_ge(s3_rq, 2 * t + 4)
                if isinstance(t, int) and t == -1:
                    pe.wait_ge(s3_ws, 6)
                project(pe, bank[2], x3_h[:, nxt, :, :], x3_l[:, nxt, :, :], vw_h, vw_l).then_inc(s3_V, 1)
            if has(t - 1):
                pe.wait_ge(s3_oa, 4 * t)
                pe.wait_ge(s3_od, 4 * t)
                if has(t + 1):
                    pe.wait_ge(s3_rk, 2 * t + 4)
                if isinstance(t, int) and t == 1:
                    pe.wait_ge(s3_w[3], 16)
                for n in range(DT):
                    ins = pe.matmul(bank[3], o_T[:, n, :, :].rearrange("p b q -> p (b q)"), ow[:, n, :],
                                    start=(n == 0), stop=(n == DT - 1))
                ins.then_inc(s3_Wo, 1)

        def head_rows(r):
            return slice(r * HD, (r + 1) * HD)

        def q_blocks(eng_copy, r):
            return eng_copy(qb[head_rows(r), :, :, r, :],
                            bank[0][head_rows(r), :].rearrange("p (n b q) -> p n b q", n=DT, b=BPG))

        def o_blocks(eng_copy, pair, r):
            src = (psum[:, 6:8, :] if pair == 0 else psum[:, 4:6, :])[head_rows(r), :, :]
            src = src.rearrange("p n (b h q) -> p n b h q", b=BPG, h=4)[:, :, :, r, :]
            return eng_copy(o_T[head_rows(r), 2 * pair:2 * pair + 2, :, :], src)

        def p_block(eng_copy, h, b):
            rows = slice(b * SQ, (b + 1) * SQ)
            return eng_copy(pb[rows, 2 * h:2 * h + 2, b, :, :],
                            bank[h][rows, :].rearrange("p (n l c) -> p n l c", n=2, l=2))

        def act3(act, t, par):
            nxt = 1 - par
            copy = lambda o, i: act.activation(o, i, ACT.Copy)
            if has(t):
                act.wait_ge(s3_Tq, t + 1)
                at_least(act, s3_S, 4 * t)
                for r in range(2):
                    q_blocks(copy, r).then_inc(s3_qa, 1)
                act.wait_ge(s3_Tk, t + 1)
                copy(k_T[:].rearrange("p n c -> p (n c)"), bank[1]).then_inc(s3_kT, 1)
            if has(t - 1):
                at_least(act, s3_PV, 2 * t - 2)
                for h in range(2):
                    act.wait_ge(s3_PT, 2 * t - 1 + h)
                    p_block(copy, h, 0).then_inc(s3_pa, 1)
            if has(t):
                act.wait_ge(s3_su, t + 1)
                s_ = sm[:, par].rearrange("p a b c d -> p (a b c d)")
                act.activation(s_, s_, ACT.Exp).then_inc(s3_ex, 1)
            if has(t - 1):
                at_least(act, s3_Wo, t - 1)
                for pair in range(2):
                    act.wait_ge(s3_PV, 2 * t - 1 + pair)
                    for r in range(2):
                        o_blocks(copy, pair, r).then_inc(s3_oa, 1)
            if has(t + 2):
                act.wait_ge(s3_XT, t + 3)
                at_least(act, s3_V, t + 1)
                copy(x3_h[:, par].rearrange("p n c -> p (n c)"), bank[0]).then_inc(s3_xh, 1)
            if has(t + 1):
                act.wait_ge(s3_V, t + 2)
                copy(v_sb[:, nxt, :], bank[2]).then_inc(s3_v, 1)

        def rotate_parts(dve, psum_bank, done, pool_sem, pool_count):
            at_least(dve, pool_sem, pool_count)
            p4 = psum_bank.rearrange("p (h i) -> p h i", h=HEADS)
            dve.tensor_tensor(r_cos[:].rearrange("p (h i) -> p h i", h=HEADS), p4,
                              rope[:, 0:1, :].broadcast_to([P, HEADS, HD]), ALU.mult).then_inc(done, 1)
            for e in range(2):
                swapped = psum_bank.rearrange("p (h i e) -> p h i e", h=HEADS, e=2)[:, :, :, 1 - e]
                o = r_sin[:].rearrange("p (h i e) -> p h i e", h=HEADS, e=2)[:, :, :, e]
                w = rope[:, 1:2, e::2].broadcast_to([P, HEADS, HD // 2])
                ins = dve.tensor_tensor(o, swapped, w, ALU.mult)
            ins.then_inc(done, 1)

        def dve3(dve, t, par):
            nxt = 1 - par
            copy = dve.tensor_copy
            if has(t + 2):
                at_least(dve, s3_xn, t + 2)
                dve.tensor_copy(cur[:, 0:2], mv3[:, bass.ds(t + 2, 1), :].rearrange("p a b -> p (a b)"))
                dve.tensor_copy(cur[:, 2:3], rs3[:, bass.ds(t + 2, 1)]).then_inc(s3_cu, 1)
                dve.wait_ge(s3_cu, t + 3)
                at_least(dve, s3_XT, t + 2)
                dve.tensor_scalar(xn3[:], one_tile(t + 2), cur[:, 0:1], cur[:, 2:3],
                                  ALU.subtract, ALU.mult).then_inc(s3_xn, 1)
            if has(t):
                dve.wait_ge(s3_Tq, t + 1)
                at_least(dve, s3_S, 4 * t)
                for r in range(2, 4):
                    q_blocks(copy, r).then_inc(s3_qd, 1)
            if has(t + 1):
                dve.wait_ge(s3_Q, t + 2)
                rotate_parts(dve, bank[2], s3_rq, s3_ak, t + 1)
            if has(t):
                at_least(dve, s3_PT, 2 * t - 2)
                for n in range(DT):
                    dve.wait_ge(s3_S, 4 * t + n + 1)
                    src = bank[4 + n % 2].rearrange("p (u w) -> p u w", w=P)[:, :, 0:SQ]
                    dve.scalar_tensor_tensor(out=sm[:, par, n].rearrange("p l b k -> p (l b) k"), in0=src,
                                             scalar=SCALE, in1=cmask[:].rearrange("p (a k) -> p a k", a=1)
                                             .broadcast_to([P, 4, SQ]), op0=ALU.mult, op1=ALU.add).then_inc(s3_ms, 1)
                dve.wait_ge(s3_ms, 4 * t + 4)
                at_least(dve, s3_su, t)
                dve.tensor_reduce(mx3[:], sm[:, par].rearrange("p n l b k -> p (n l b) k"), AX_X,
                                  ALU.max).then_inc(s3_mx, 1)
            if has(t + 1):
                dve.wait_ge(s3_K, t + 2)
                rotate_parts(dve, bank[3], s3_rk, s3_aq, t + 2)
            if has(t - 1):
                at_least(dve, s3_PV, 2 * t - 2)
                for h in range(2):
                    dve.wait_ge(s3_PT, 2 * t - 1 + h)
                    p_block(copy, h, 1).then_inc(s3_pd, 1)
                at_least(dve, s3_Wo, t - 1)
                for pair in range(2):
                    dve.wait_ge(s3_PV, 2 * t - 1 + pair)
                    for r in range(2, 4):
                        o_blocks(copy, pair, r).then_inc(s3_od, 1)
            if has(t):
                dve.wait_ge(s3_ex, t + 1)
                dve.tensor_reduce(rc3[:, 0, :], sm[:, par].rearrange("p n l b k -> p (n l b) k"), AX_X,
                                  ALU.add).then_inc(s3_sm, 1)
                dve.wait_ge(s3_sm, t + 1)
                at_least(dve, s3_pn, t)
                dve.reciprocal(rc3[:, 1, :], rc3[:, 0, :]).then_inc(s3_rc, 1)
            if has(t + 2):
                dve.wait_ge(s3_xh, t + 3)
                dve.tensor_tensor(x3_l[:, par].rearrange("p n c -> p (n c)"), bank[0],
                                  x3_h[:, par].rearrange("p n c -> p (n c)").bitcast(F32),
                                  ALU.subtract).then_inc(s3_xl, 1)
            if has(t - 1):
                dve.wait_ge(s3_Wo, t)
                dve.tensor_tensor(one_tile(t - 1), bank[3], one_tile(t - 1), ALU.add).then_inc(s3_x, 1)

        def pool3(pool, t, par):
            if has(t + 1):
                pool.wait_ge(s3_rq, 2 * t + 4)
                at_least(pool, s3_Tq, t + 1)
                settle(pool)
                pool.tensor_tensor(q_r[:], r_cos[:], r_sin[:], ALU.add).then_inc(s3_aq, 1)
            if has(t):
                pool.wait_ge(s3_mx, t + 1)
                settle(pool)
                s_ = sm[:, par].rearrange("p n l b k -> p (n l b) k")
                pool.tensor_tensor(s_, s_, mx3[:].rearrange("p (u a) -> p u a", a=1).broadcast_to([P, HEADS, SQ]),
                                   ALU.subtract).then_inc(s3_su, 1)
            if has(t + 1):
                pool.wait_ge(s3_rk, 2 * t + 4)
                at_least(pool, s3_Tk, t + 1)
                settle(pool)
                pool.tensor_tensor(k_r[:], r_cos[:], r_sin[:], ALU.add).then_inc(s3_ak, 1)
            if has(t):
                pool.wait_ge(s3_rc, t + 1)
                settle(pool)
                s_ = sm[:, par].rearrange("p n l b k -> p (n l b) k")
                pool.tensor_tensor(s_, s_, rc3[:, 1, :].rearrange("p (u a) -> p u a", a=1)
                                   .broadcast_to([P, HEADS, SQ]), ALU.mult).then_inc(s3_pn, 1)

        def steps(eng, step):
            for t in range(-2, 2):
                step(eng, t, t % 2)
            with eng.Fori(1, G // 2 - 1) as h:
                step(eng, 2 * h, 0)
                step(eng, 2 * h + 1, 1)
            for t in range(G - 2, G + 1):
                step(eng, t, t % 2)

        with nc.Block() as block:
            @block.sync
            def _(sp):
                for i, w in enumerate((aq, ak, av)):
                    sp.dma_start(raw3[:, i], w.rearrange("(t p) n -> p t n", p=P)).then_inc(s3_w[i], 16)
                sp.dma_start(ow[:], ao.rearrange("(t p) n -> p t n", p=P)).then_inc(s3_w[3], 16)
                for i in range(BPG):
                    rows = slice(i * SQ, (i + 1) * SQ)
                    sp.dma_start(rope[rows, 0, :], cos_tab).then_inc(s3_c, 16)
                    sp.dma_start(rope[rows, 1, :], sin_tab).then_inc(s3_c, 16)
                    sp.dma_start(cmask[rows, :], causal).then_inc(s3_c, 16)

            @block.gpsimd
            def _(pool):
                pool.memset(qb[:], 0.0).then_inc(s3_z, 1)
                pool.memset(pb[:], 0.0).then_inc(s3_z, 1)
                for i, (h, l) in enumerate(((qw_h, qw_l), (kw_h, kw_l), (vw_h, vw_l))):
                    pool.wait_ge(s3_w[i], 16)
                    pool.tensor_scalar(h[:], raw3[:, i], 1.0, None, ALU.mult).then_inc(s3_ws, 1)
                    pool.wait_ge(s3_ws, 2 * i + 1)
                    pool.tensor_tensor(l[:], raw3[:, i], h[:].bitcast(F32), ALU.subtract).then_inc(s3_ws, 1)
                steps(pool, pool3)

            @block.vector
            def _(dve):
                for t in range(G):
                    dve.bn_stats(st3[:, t, :], tok[:, t, :]).then_inc(s3_st, 1)
                for t in range(G):
                    dve.wait_ge(s3_st, t + 1)
                    dve.bn_aggr(mv3[:, t, :], st3[:, t, :]).then_inc(s3_mv, 1)
                dve.wait_ge(s3_sd, 1)
                dve.reciprocal(rs3[:], rs3[:]).then_inc(s3_rs, 1)
                dve.wait_ge(s3_rs, 1)
                dve.wait_ge(s3_z, 2)
                dve.wait_ge(s3_c, 16 * 3 * BPG)
                steps(dve, dve3)

            @block.scalar
            def _(act):
                act.wait_ge(s3_mv, G)
                act.activation(rs3[:], mv3[:, :, 1], ACT.Sqrt, bias=epsb[:]).then_inc(s3_sd, 1)
                act.wait_ge(s3_z, 2)
                steps(act, act3)

            @block.tensor
            def _(pe):
                steps(pe, pe3)

        if stop_after == 3:
            s_dbg = sem("dbg")
            with nc.Block() as block:
                @block.sync
                def _(sp):
                    sp.dma_start(outt, tok[:]).then_inc(s_dbg, 16)
                    sp.wait_ge(s_dbg, 16)
            return

        KEEP = SQ // 2
        FF = w1.shape[0]
        ST = B * KEEP // P
        m = Map(nc, base)
        xs_h, xs_l = m("xs_h", [P, DT, ST * P], F32R), m("xs_l", [P, DT, ST * P], F32R)
        ohT = m("ohT", [P, G, P], F32)
        s_all, w_all = m("s_all", [P, G], F32), m("w_all", [P, G], F32)
        b1_sb, b2_sb = m("b1_sb", [P, FF], F32), m("b2_sb", [P, D], F32)
        after4 = m.at
        xn4 = m("xn4", [P, CH, D], F32)
        router_sb = m("router_sb", [P, D], F32)
        dots = m("dots", [P, D], F32)
        ones = m("ones", [P, P], F32)
        dg = m("dg", [P, CH, P], F32)
        s4, r1, r2, rank = m("s4", [P, CH], F32), m("r1", [P, CH], F32), m("r2", [P, CH], F32), m("rank", [P, CH], F32)
        same, before = m("same", [P, P], F32), m("before", [P, P], F32)
        slot_no = m("slot_no", [P, 2, P], F32)
        junk = m("junk", [P, 2, P], F32)
        oh = m("oh", [P, CH, P], F32)
        assert m.at <= nc.sbuf_usable_end, m.at

        s4_c, s4_on, s4_b = sem("p4_const"), sem("p4_ones"), sem("p4_b")
        s4_st, s4_mv, s4_sd, s4_rs, s4_xn = sem("p4_st"), sem("p4_mv"), sem("p4_sd"), sem("p4_rs"), sem("p4_xn")
        s4_s, s4_dg, s4_R, s4_cp, s4_eq = sem("p4_s"), sem("p4_dg"), sem("p4_R"), sem("p4_cp"), sem("p4_eq")
        s4_rk, s4_oh, s4_G, s4_T = sem("p4_rk"), sem("p4_oh"), sem("p4_G"), sem("p4_T")
        s4_gh, s4_gl, s4_oc, s4_tk, s4_sg = sem("p4_gh"), sem("p4_gl"), sem("p4_oc"), sem("p4_tk"), sem("p4_sg")

        def chunks(eng, chunk):
            chunk(0)
            with eng.Fori(1, NCH) as c:
                chunk(c)

        with nc.Block() as block:
            @block.sync
            def _(sp):
                sp.dma_start(router_sb[:], router.rearrange("(a n) -> a n", a=1).broadcast_to([P, D]))\
                    .then_inc(s4_c, 16)
                sp.dma_start(same[:], same_in).then_inc(s4_c, 16)
                sp.dma_start(before[:], before_in).then_inc(s4_c, 16)
                sp.dma_start(slot_no[:], slot_in).then_inc(s4_c, 16)
                sp.dma_start(b1_sb[:], b1).then_inc(s4_b, 16)
                sp.dma_start(b2_sb[:], b2.rearrange("(a n) -> a n", a=1).broadcast_to([P, D])).then_inc(s4_b, 16)
                sp.wait_ge(s4_b, 32)

            @block.gpsimd
            def _(pool):
                pool.memset(ones[:], 1.0).then_inc(s4_on, 1)
                def chunk(c):
                    pool.wait_ge(s4_xn, CH * c + CH)
                    settle(pool)
                    t = tok[:, bass.ds(CH * c, CH), :]
                    pool.tensor_tensor(t, t, xn4[:], ALU.add).then_inc(s4_tk, 1)
                chunks(pool, chunk)

            @block.vector
            def _(dve):
                dve.wait_ge(s4_c, 64)
                dve.wait_ge(s4_on, 1)
                def chunk(c):
                    for t in range(CH):
                        dve.bn_stats(st3[:, t, :], one_tile(CH * c + t)).then_inc(s4_st, 1)
                    at_least(dve, s4_sd, c)
                    for t in range(CH):
                        dve.wait_ge(s4_st, CH * c + t + 1)
                        settle(dve)
                        dve.bn_aggr(mv[:, t, :], st3[:, t, :]).then_inc(s4_mv, 1)
                    dve.wait_ge(s4_sd, c + 1)
                    dve.reciprocal(rstd[:], rstd[:]).then_inc(s4_rs, 1)
                    dve.wait_ge(s4_rs, c + 1)
                    at_least(dve, s4_G, 2 * c)
                    at_least(dve, s4_tk, c)
                    for t in range(CH):
                        dve.tensor_scalar(xn4[:, t, :], one_tile(CH * c + t), mv[:, t, 0:1], rstd[:, t:t + 1],
                                          ALU.subtract, ALU.mult).then_inc(s4_xn, 1)
                    for t in range(CH):
                        dve.wait_ge(s4_xn, CH * c + t + 1)
                        settle(dve)
                        dve.tensor_tensor_reduce(dots[:], xn4[:, t, :], router_sb[:], 1.0, 0.0, ALU.mult, ALU.add,
                                                 s4[:, t:t + 1]).then_inc(s4_s, 1)
                        dve.wait_ge(s4_s, CH * c + t + 1)
                    dve.tensor_copy(s_all[:, bass.ds(CH * c, CH)], s4[:]).then_inc(s4_cp, 1)
                    at_least(dve, s4_R, c)
                    dve.tensor_tensor(dg[:], ident[:].rearrange("p (a n) -> p a n", a=1).broadcast_to([P, CH, P]),
                                      s4[:].rearrange("p (t a) -> p t a", a=1).broadcast_to([P, CH, P]),
                                      ALU.mult).then_inc(s4_dg, 1)
                    dve.wait_ge(s4_R, c + 1)
                    for t in range(CH):
                        row = bank[0][:, t * P:(t + 1) * P]
                        dve.scalar_tensor_tensor(out=junk[:, 0, :], in0=row, scalar=s4[:, t:t + 1], in1=same[:],
                                                 op0=ALU.is_gt, op1=ALU.mult, accum_out=r1[:, t:t + 1]).then_inc(s4_eq, 1)
                        dve.wait_ge(s4_eq, 2 * CH * c + 2 * t + 1)
                        dve.scalar_tensor_tensor(out=junk[:, 1, :], in0=row, scalar=s4[:, t:t + 1], in1=before[:],
                                                 op0=ALU.is_equal, op1=ALU.mult, accum_out=r2[:, t:t + 1]).then_inc(s4_eq, 1)
                        dve.wait_ge(s4_eq, 2 * CH * c + 2 * t + 2)
                    dve.tensor_tensor(rank[:], r1[:], r2[:], ALU.add).then_inc(s4_rk, 1)
                    dve.wait_ge(s4_rk, c + 1)
                    at_least(dve, s4_T, c)
                    for t in range(CH):
                        dve.tensor_scalar(oh[:, t, :], slot_no[:, t % 2, :], rank[:, t:t + 1], None,
                                          ALU.is_equal).then_inc(s4_oh, 1)
                    for h in range(2):
                        dve.wait_ge(s4_gh, 2 * c + h + 1)
                        at = c * (2 * P) + h * P
                        dve.tensor_tensor(xs_l[:, :, bass.ds(at, P)], bank[1 + h].rearrange("p (k n) -> p k n", k=DT),
                                          xs_h[:, :, bass.ds(at, P)].bitcast(F32), ALU.subtract).then_inc(s4_gl, 1)
                chunks(dve, chunk)

            @block.scalar
            def _(act):
                def chunk(c):
                    act.wait_ge(s4_mv, CH * c + CH)
                    at_least(act, s4_xn, CH * c)
                    act.activation(rstd[:], mv[:, :, 1], ACT.Sqrt, bias=epsb[:]).then_inc(s4_sd, 1)
                    for h in range(2):
                        act.wait_ge(s4_G, 2 * c + h + 1)
                        act.activation(xs_h[:, :, bass.ds(c * (2 * P) + h * P, P)],
                                       bank[1 + h].rearrange("p (k n) -> p k n", k=DT), ACT.Copy).then_inc(s4_gh, 1)
                    act.wait_ge(s4_T, c + 1)
                    act.activation(ohT[:, bass.ds(CH * c, CH), :], bank[3].rearrange("p (k n) -> p k n", k=CH),
                                   ACT.Copy).then_inc(s4_oc, 1)
                chunks(act, chunk)
                act.wait_ge(s4_cp, NCH)
                act.activation(w_all[:], s_all[:], ACT.Sigmoid).then_inc(s4_sg, 1)

            @block.tensor
            def _(pe):
                pe.wait_ge(s4_on, 1)
                def chunk(c):
                    pe.wait_ge(s4_dg, c + 1)
                    at_least(pe, s4_rk, c)
                    pe.matmul(bank[0], ones[:], dg[:].rearrange("p a n -> p (a n)"), start=True, stop=True)\
                        .then_inc(s4_R, 1)
                    pe.wait_ge(s4_oh, CH * c + CH)
                    at_least(pe, s4_gl, 2 * c)
                    for h in range(2):
                        for k in range(DT):
                            for e in range(2):
                                ins = pe.matmul(bank[1 + h][:, k * P:(k + 1) * P],
                                                xn4[:, 2 * h + e, k * P:(k + 1) * P], oh[:, 2 * h + e, :],
                                                start=(e == 0), stop=(e == 1))
                        ins.then_inc(s4_G, 1)
                    at_least(pe, s4_oc, c)
                    for t in range(CH):
                        ins = pe.transpose(bank[3][:, t * P:(t + 1) * P], oh[:, t, :], ident[:])
                    ins.then_inc(s4_T, 1)
                chunks(pe, chunk)

        m = Map(nc, after4)
        DEEP = 4
        w_r = m("w_r", [P, DEEP, 2, D], F32)
        w_h, w_l = m("w_h", [P, DEEP, 2, D], F32R), m("w_l", [P, DEEP, 2, D], F32R)
        hid = m("hid", [P, 2, 4 * P], F32)
        hid_h, hid_l = m("hid_h", [P, 2, 4 * P], F32R), m("hid_l", [P, 2, 4 * P], F32R)
        y_sb = m("y_sb", [P, 4, D], F32)
        assert m.at <= nc.sbuf_usable_end, m.at
        SC = ST // 4
        TPC = G // SC

        s5_w = [sem(f"p5_w{i}") for i in range(DEEP)]
        s5_wh, s5_wl, s5_H, s5_g, s5_gh, s5_gl, s5_Y = (sem("p5_wh"), sem("p5_wl"), sem("p5_H"), sem("p5_g"), sem("p5_gh"), sem("p5_gl"),
                                                 sem("p5_Y"))
        s5_y, s5_Sc, s5_x, s5_out = sem("p5_y"), sem("p5_Sc"), sem("p5_x"), sem("p5_out")
        h_bank, sc_bank, y_bank = bank[0:2], bank[2:4], bank[4:8]

        def ffn_tiles(eng, step, after):
            for q in range(SC):
                for f in range(DEEP):
                    step(f, q * FF + f, f, q)
                with eng.Fori(1, FF // DEEP - 1) as h:
                    for e in range(DEEP):
                        step(DEEP * h + e, q * FF + DEEP * h + e, e, q)
                for f in range(FF - DEEP, FF):
                    step(f, q * FF + f, f % DEEP, q)
                after(q)

        with nc.Block() as block:
            @block.sync
            def _(sp):
                def load(f, n, e, q):
                    at_least(sp, s5_wl, n - DEEP + 1)
                    settle(sp)
                    sp.dma_start(w_r[:, e, 0, :], w1[bass.ds(f, 1), :, :].rearrange("a p n -> p (a n)"))\
                        .then_inc(s5_w[e], 16)
                    sp.dma_start(w_r[:, e, 1, :], w2[bass.ds(f, 1), :, :].rearrange("a p n -> p (a n)"))\
                        .then_inc(s5_w[e], 16)

                def store(q):
                    if q == 0:
                        return
                    for t in range(G):
                        sp.wait_ge(s5_x, t + 1)
                        sp.dma_start(outt[:, t, :], tok[:, t, :]).then_inc(s5_out, 16)
                    sp.wait_ge(s5_out, 16 * G)
                ffn_tiles(sp, load, store)

            @block.gpsimd
            def _(pool):
                def split(f, n, e, q):
                    pool.wait_ge(s5_wh, n + 1)
                    settle(pool)
                    pool.tensor_tensor(w_l[:, e], w_r[:, e], w_h[:, e].bitcast(F32), ALU.subtract).then_inc(s5_wl, 1)
                ffn_tiles(pool, split, lambda q: None)

            @block.scalar
            def _(act):
                def weights_high(n, e):
                    act.wait_ge(s5_w[e], 32 * (n // DEEP + 1) if isinstance(n, int) else (n - e) * (32 // DEEP) + 32)
                    at_least(act, s5_Y, n - DEEP + 1)
                    act.activation(w_h[:, e], w_r[:, e], ACT.Copy).then_inc(s5_wh, 1)

                def gelu(f, n, e, q):
                    if isinstance(n, int) and n == 0:
                        weights_high(0, 0)
                        weights_high(1, 1)
                    if not (isinstance(n, int) and n >= SC * FF - 2):
                        weights_high(n + 2, (e + 2) % DEEP)
                    act.wait_ge(s5_H, n + 1)
                    at_least(act, s5_gl, n - 1)
                    act.activation(hid[:, e % 2, :], h_bank[e % 2], ACT.Gelu_apprx_tanh,
                                   bias=b1_sb[:, bass.ds(f, 1)]).then_inc(s5_g, 1)
                ffn_tiles(act, gelu, lambda q: None)

            @block.vector
            def _(dve):
                def split(f, n, e, q):
                    dve.wait_ge(s5_g, n + 1)
                    at_least(dve, s5_Y, n - 1)
                    e = e % 2
                    dve.tensor_copy(hid_h[:, e, :], hid[:, e, :]).then_inc(s5_gh, 1)
                    dve.wait_ge(s5_gh, n + 1)
                    dve.tensor_tensor(hid_l[:, e, :], hid[:, e, :], hid_h[:, e, :].bitcast(F32),
                                      ALU.subtract).then_inc(s5_gl, 1)

                def update(q):
                    dve.wait_ge(s5_Y, FF * (q + 1))
                    at_least(dve, s5_Sc, TPC * q)
                    for i in range(4):
                        dve.tensor_tensor(y_sb[:, i, :], y_bank[i], b2_sb[:], ALU.add).then_inc(s5_y, 1)
                    for t in range(TPC * q, TPC * (q + 1)):
                        dve.wait_ge(s5_Sc, t + 1)
                        dve.scalar_tensor_tensor(out=tok[:, t, :], in0=sc_bank[t % 2], scalar=w_all[:, t:t + 1],
                                                 in1=tok[:, t, :], op0=ALU.mult, op1=ALU.add).then_inc(s5_x, 1)
                ffn_tiles(dve, split, update)

            @block.tensor
            def _(pe):
                def hidden(n, e, q):
                    pe.wait_ge(s5_wl, n + 1)
                    at_least(pe, s5_g, n - 1)
                    for k in range(DT):
                        cols = slice(q * 4 * P, (q + 1) * 4 * P)
                        for i, (w, y) in enumerate(((w_h, xs_h), (w_l, xs_h), (w_h, xs_l))):
                            ins = pe.matmul(h_bank[e % 2], w[:, e, 0, k * P:(k + 1) * P], y[:, k, cols],
                                            start=(k == 0 and i == 0), stop=(k == DT - 1 and i == PRODUCTS - 1))
                    ins.then_inc(s5_H, 1)

                def step(f, n, e, q):
                    if isinstance(f, int) and f == 0:
                        hidden(n, 0, q)
                        at_least(pe, s5_y, 4 * q)
                    if not (isinstance(f, int) and f == FF - 1):
                        hidden(n + 1, (e + 1) % DEEP, q)
                    pe.wait_ge(s5_gl, n + 1)
                    for t in range(4):
                        for i, (h, w) in enumerate(((hid_h, w_h), (hid_h, w_l), (hid_l, w_h))):
                            ins = pe.matmul(y_bank[t], h[:, e % 2, t * P:(t + 1) * P], w[:, e, 1, :],
                                            start=(isinstance(f, int) and f == 0 and i == 0),
                                            stop=(isinstance(f, int) and f == FF - 1 and i == PRODUCTS - 1))
                    ins.then_inc(s5_Y, 1)

                def scatter(q):
                    pe.wait_ge(s5_y, 4 * q + 4)
                    for t in range(TPC * q, TPC * (q + 1)):
                        at_least(pe, s5_x, t - 1)
                        pe.matmul(sc_bank[t % 2], ohT[:, t, :], y_sb[:, (t % TPC) // 2, :], start=True, stop=True)\
                            .then_inc(s5_Sc, 1)
                ffn_tiles(pe, step, scatter)


_INS = ["x", "ctx_768", "mask_BxS2_bf1", "L0_xattn_Wq", "L0_xattn_Wk", "L0_xattn_Wv", "L0_xattn_Wo",
        "L0_attn_wq", "L0_attn_wk", "L0_attn_wv", "L0_attn_wo", "L0_ffn_w_router", "L0_ffn_W1", "L0_ffn_b1",
        "L0_ffn_W2", "L0_ffn_b2"]
STOP = None


def constants(queries, hd, theta=10000.0):
    freq = np.float32(1.0) / np.float32(theta) ** (np.arange(0, hd, 2, dtype=np.float32) / np.float32(hd))
    ang = np.arange(queries, dtype=np.float32)[:, None] * freq[None, :]
    cos = np.repeat(np.cos(ang), 2, axis=1)
    sin = np.stack([-np.sin(ang), np.sin(ang)], axis=-1).reshape(queries, hd)
    seen = np.tril(np.ones((queries, queries), bool))
    token, batch = np.arange(P), np.arange(P) // queries
    same = batch[:, None] == batch[None, :]
    keep, slot = queries // 2, np.arange(P)
    mine = [(slot // keep)[None, :] == (2 * e + batch)[:, None] for e in (0, 1)]
    return {"cos": cos.astype(np.float32), "sin": sin.astype(np.float32),
            "causal": np.where(seen, 0.0, -BIG).astype(np.float32),
            "same": same.astype(np.float32),
            "before": (same & (token[None, :] < token[:, None])).astype(np.float32),
            "slot": np.stack([np.where(x, slot % keep, -1) for x in mine], axis=1).astype(np.float32)}


def kernel(**inputs):
    from concourse import bacc
    from concourse.bass_utils import run_bass_kernel_spmd

    nc = bacc.Bacc("TRN2", target_bir_lowering=False, num_devices=1)
    arrays, args = {}, []
    for name in _INS:
        a = np.ascontiguousarray(inputs[name])
        if name == "ctx_768":
            a = np.ascontiguousarray(a.transpose(0, 2, 1))
        if name == "mask_BxS2_bf1":
            a = a.view(np.uint8)
        if name == "L0_ffn_W1":
            d, f = a.shape
            a = np.ascontiguousarray(a.reshape(d // P, P, f // P, P).transpose(2, 1, 0, 3)).reshape(f // P, P, d)
        if name == "L0_ffn_W2":
            a = a.reshape(-1, P, a.shape[1])
        if name == "L0_ffn_b1":
            a = np.ascontiguousarray(a.reshape(-1, P).T)
        arrays[f"in_{name}"] = a
        args.append(nc.dram_tensor(f"in_{name}", a.shape, mybir.dt.from_np(a.dtype), kind="ExternalInput").ap())
    for name, a in constants(inputs["x"].shape[1], inputs["x"].shape[2] // HEADS).items():
        arrays[f"in_{name}"] = a
        args.append(nc.dram_tensor(f"in_{name}", a.shape, F32, kind="ExternalInput").ap())
    out = nc.dram_tensor("out", inputs["x"].shape, F32, kind="ExternalOutput").ap()
    perceiver_layer(nc, *args, out, stop_after=STOP)
    r = run_bass_kernel_spmd(nc, [arrays], core_ids=[0])
    return r.results[0]["out"]
```

```python
from contextlib import ExitStack

import numpy as np

import concourse.bass as bass
from concourse import mybir

F32 = mybir.dt.float32
F32R = mybir.dt.float32r
U8 = mybir.dt.uint8
ALU = mybir.AluOpType
ACT = mybir.ActivationFunctionType
AX_X = mybir.AxisListType.X

P = 128
HEADS = 16
BIG = 1.0e30
LN_EPS = 1e-5


class Map:

    def __init__(self, nc, start):
        self.nc, self.at = nc, (start + 63) // 64 * 64

    def __call__(self, name, shape, dt):
        size = 1 if dt == U8 else 4
        for n in shape[1:]:
            size *= n
        t = self.nc.alloc_sbuf_tensor_at(name, shape, dt, offset=self.at)
        self.at += (size + 63) // 64 * 64
        return t


def perceiver_layer(nc, x, ctxT, mask, wq, wk, wv, wo, aq, ak, av, ao, router, w1, b1, w2, b2,
                    cos_tab, sin_tab, causal, same_in, before_in, slot_in, out, stop_after=None):
    B, SQ, D = x.shape
    _, C, SK = ctxT.shape
    HD = D // HEADS
    DT, CT, KT = D // P, C // P, SK // P
    G = B * SQ // P
    BPG = P // SQ
    CH = 4
    NCH = G // CH
    PAIRS = HEADS // 2
    SCALE = float(HD) ** -0.5
    xt = x.rearrange("b s d -> (b s) d").rearrange("(g p) d -> p g d", p=P)
    outt = out.rearrange("b s d -> (b s) d").rearrange("(g p) d -> p g d", p=P)

    stack = ExitStack()
    with stack:
        def sem(name):
            return stack.enter_context(nc.semaphore(name))

        s_stood = sem("stood")

        def settle(eng):
            eng.sem_inc(s_stood, 1)

        psum = stack.enter_context(nc.psum_tensor("psum", [P, 8, 512], F32))
        bank = [psum[:, i, :] for i in range(8)]

        def at_least(eng, sem, value):
            if not isinstance(value, int) or value > 0:
                eng.wait_ge(sem, value)

        always = Map(nc, nc.sbuf_base)
        tok = always("tok", [P, G, D], F32)
        ident = always("ident", [P, P], F32)
        epsb = always("epsb", [P, 1], F32)
        stats = always("stats", [P, CH, 6], F32)
        mv = always("mv", [P, CH, 2], F32)
        rstd = always("rstd", [P, CH], F32)
        st1, mv1 = always("st1", [P, 6], F32), always("mv1", [P, 1, 2], F32)
        mv3, rs3 = always("mv3", [P, G, 2], F32), always("rs3", [P, G], F32)
        base = always.at

        m = Map(nc, base)
        wk_h, wk_l = m("wk_h", [P, CT, D], F32R), m("wk_l", [P, CT, D], F32R)
        wv_h, wv_l = m("wv_h", [P, CT, D], F32R), m("wv_l", [P, CT, D], F32R)
        wo_at = m.at
        wo_h, wo_l = m("wo_h", [P, DT, D], F32R), m("wo_l", [P, DT, D], F32R)
        after_xw = m.at
        wq_r = m("wq_r", [P, DT, D], F32)
        wq_h, wq_l = m("wq_h", [P, DT, D], F32R), m("wq_l", [P, DT, D], F32R)
        wk_r, wv_r = m("wk_r", [P, CT, D], F32), m("wv_r", [P, CT, D], F32)
        wo_r = m("wo_r", [P, DT, D], F32)
        xn = m("xn", [P, CH, D], F32)
        xnT_h, xnT_l = m("xnT_h", [P, DT, CH * P], F32R), m("xnT_l", [P, DT, CH * P], F32R)

        end1 = m.at

        s_w = [sem(f"p1_wq{k}") for k in range(DT)]
        s_wkv = [sem(f"p1_w{i}") for i in range(3)]
        s_x0 = [sem(f"p1_x0_{t}") for t in range(CH)]
        s_x = [sem(f"p1_x{i}") for i in range(NCH)]
        s_id = sem("p1_id")
        s_eps = sem("p1_eps")
        s_st, s_var, s_sd, s_rs, s_xn = sem("p1_st"), sem("p1_var"), sem("p1_sd"), sem("p1_rs"), sem("p1_xn")
        s_tr, s_hi, s_lo, s_q, s_qe = sem("p1_tr"), sem("p1_hi"), sem("p1_lo"), sem("p1_q"), sem("p1_qe")
        s_wh, s_wl = sem("p1_wh"), sem("p1_wl")
        s_pw = sem("p1_pw")


        m = Map(nc, after_xw)
        xres = m("xres", [P, 1, D], F32)
        KK = m("KK", [P, PAIRS, SK], F32R)
        V_h, V_l = m("V_h", [P, 2, KT, D], F32R), m("V_l", [P, 2, KT, D], F32R)
        prob = m("prob", [P, 2, SK], F32)
        PT_h, PT_l = m("PT_h", [P, 2, KT, 2, P], F32R), m("PT_l", [P, 2, KT, 2, P], F32R)
        OT_h, OT_l = m("OT_h", [P, DT, BPG, SQ], F32R), m("OT_l", [P, DT, BPG, SQ], F32R)
        mx, nmx = m("mx", [P, 4], F32), m("nmx", [P, 4], F32)
        rsum, rinv = m("rsum", [P, 4], F32), m("rinv", [P, 4], F32)
        assert m.at >= end1, (m.at, end1)
        qz_h, qz_l = m("qz_h", [P, DT, 2, 2, SQ], F32R), m("qz_l", [P, DT, 2, 2, SQ], F32R)
        mask8 = m("mask8", [P, BPG, SK], U8)
        mbias = m("mbias", [P, BPG, SK], F32)
        ctx_at = m.at
        ctx_r = m("ctx_r", [P, CT, SK], F32)
        ctx_h, ctx_l = m("ctx_h", [P, 2, CT, SK], F32R), m("ctx_l", [P, 2, CT, SK], F32R)
        ctx_end = m.at
        assert m.at <= nc.sbuf_usable_end, m.at

        s_raw = sem("p2_ctx")
        s_mraw = [sem(f"p2_mask{i}") for i in range(BPG)]
        s_xr = sem("p2_xres")
        s_z = sem("p2_zero")
        s_cx = sem("p2_cx")
        s_qz = sem("p2_qz")
        s_qd = sem("p2_qd")
        s_mb = sem("p2_mb")
        s_S, s_KV, s_T, s_PV, s_Wo = sem("p2_S"), sem("p2_KV"), sem("p2_T"), sem("p2_PV"), sem("p2_Wo")
        s_mx, s_nm, s_ex, s_ri, s_pn = sem("p2_mx"), sem("p2_nm"), sem("p2_ex"), sem("p2_ri"), sem("p2_pn")
        s_Th, s_Tl, s_KVh, s_KVl = sem("p2_Th"), sem("p2_Tl"), sem("p2_KVh"), sem("p2_KVl")
        s_Oh, s_Ol = sem("p2_Oh"), sem("p2_Ol")
        s_x1 = sem("p2_x1")
        S_bank, KV_bank, T_bank, PV_bank, Wo_bank = bank[0:2], bank[2:5], bank[5], bank[6], bank[7]

        SPT = BPG * PAIRS
        AHEAD = 6
        TILES = KT + DT
        KV_ORDER = [(kind, t) for t in range(DT) for kind in "KV"]
        GROUPS = BPG * DT
        UPPER, LOWER = slice(0, P // 2), slice(P // 2, P)
        PRODUCTS = 3

        def group(j, lag):
            n = (j - lag) // 2
            return n, n % DT, (n % GROUPS) // DT

        def kv_bank(k):
            return KV_bank[1 if k % SPT == SPT - 1 else k % SPT % 3]

        def high_parts(k):
            kind, t = KV_ORDER[k % TILES]
            if kind == "V":
                return [(slice(0, P), V_h[:, (k // TILES) % 2, t, :])]
            return [(UPPER, KK[UPPER, 2 * t, :]), (LOWER, KK[LOWER, 2 * t + 1, :])]

        def low_parts(k):
            kind, t = KV_ORDER[k % TILES]
            if kind == "V":
                return [V_l[:, (k // TILES) % 2, t, :]]
            return [KK[LOWER, 2 * t, :], KK[UPPER, 2 * t + 1, :]]

        def pt_half(j, low):
            return (PT_l if low else PT_h)[:, (j // 2) % 2, :, j % 2, :]

        def heads_of(psum, r):
            return psum[r * HD:(r + 1) * HD, r * SQ:(r + 1) * SQ]

        def pe_kv(pe, g, k, first):
            b, t = k // TILES, KV_ORDER[k % TILES][1]
            if k % TILES == 0:
                pe.wait_ge(s_cx, g * (2 * BPG) + 2 * b + 2)
            last_use = 2 if k % SPT in (1, SPT - 1) else 4 if k % SPT == 0 else 3
            if not (first and k < 3):
                pe.wait_ge(s_KVl, g * SPT + (k - last_use + 1))
            for c in range(CT):
                if KV_ORDER[k % TILES][0] == "K":
                    parts = ((wk_h, ctx_h), (wk_l, ctx_h), (wk_h, ctx_l))
                    ops = [(w[:, c, t * P:(t + 1) * P], y[:, b % 2, c, :]) for w, y in parts]
                else:
                    parts = ((ctx_h, wv_h), (ctx_h, wv_l), (ctx_l, wv_h))
                    ops = [(y[:, b % 2, c, t * P:(t + 1) * P], w[:, c, :]) for y, w in parts]
                for i, (stat, mov) in enumerate(ops):
                    ins = pe.matmul(kv_bank(k)[:], stat, mov, start=(c == 0 and i == 0),
                                    stop=(c == CT - 1 and i == PRODUCTS - 1))
            ins.then_inc(s_KV, 1)

        def pe_slot(pe, g, j, first=False, last=False, tail=False):
            s = g * SPT + j
            b, p = j // PAIRS, j % PAIRS
            if not tail:
                if p % 4 == 0:
                    pe.wait_ge(s_qz, g * (BPG * 16) + b * 16 + (p // 4 + 1) * 8)
                    pe.wait_ge(s_qd, g * SPT + j + 4)
                if p % 2 == 0:
                    pe.wait_ge(s_KVl, g * SPT + b * TILES + p + 1)
                if not (first and j < 2):
                    pe.wait_ge(s_mx, s - 1)
                for q in (qz_h, qz_l):
                    ins = pe.matmul(S_bank[j % 2][:], q[:, p // 2, p % 2, :, :].rearrange("p a b -> p (a b)"),
                                    KK[:, p, :], start=(q is qz_h), stop=(q is qz_l))
                ins.then_inc(s_S, 1)
                if not (last and j + AHEAD >= SPT):
                    pe_kv(pe, g, j + AHEAD, first)
            if j == 3 and not first:
                pe.wait_ge(s_Ol, g * (4 * GROUPS))
                pe.wait_ge(s_x1, g)
                for n in range(DT):
                    for i, (o, w) in enumerate(((OT_h, wo_h), (OT_l, wo_h), (OT_h, wo_l))):
                        ins = pe.matmul(Wo_bank[:], o[:, n, :, :].rearrange("p a b -> p (a b)"), w[:, n, :],
                                        start=(n == 0 and i == 0), stop=(n == DT - 1 and i == PRODUCTS - 1))
                ins.then_inc(s_Wo, 1)
            if not (first and j == 0) and not (tail and j > 0):
                pe.wait_ge(s_pn, s)
                if not (first and j == 1):
                    pe.wait_ge(s_Tl, s - 1)
                for kt in range(KT):
                    ins = pe.transpose(T_bank[:, kt * P:(kt + 1) * P],
                                       prob[:, (j - 1) % 2, kt * P:(kt + 1) * P], ident[:])
                ins.then_inc(s_T, 1)
            if j % 2 == 1 and not (first and j == 1) and not (tail and j > 1):
                n, quarter, odd = group(j, 3)
                pe.wait_ge(s_Tl, s - 1)
                if j % PAIRS == 3:
                    pe.wait_ge(s_KVl, g * SPT + (j // PAIRS + 1) * TILES)
                if not (first and n == 0):
                    pe.wait_ge(s_Ol, g * (4 * GROUPS) + 4 * n)
                for kt in range(KT):
                    for i, (v, t) in enumerate(((V_h, PT_h), (V_h, PT_l), (V_l, PT_h))):
                        ins = pe.matmul(PV_bank[:, 0:2 * P], v[:, odd, kt, quarter * P:(quarter + 1) * P],
                                        t[:, n % 2, kt, :, :].rearrange("p a b -> p (a b)"),
                                        start=(kt == 0 and i == 0), stop=(kt == KT - 1 and i == PRODUCTS - 1))
                ins.then_inc(s_PV, 1)

        def act_kv(act, g, k):
            act.wait_ge(s_KV, g * SPT + k + 1)
            for rows, place in high_parts(k):
                ins = act.activation(place, kv_bank(k)[rows, :], ACT.Copy)
            ins.then_inc(s_KVh, 1)

        def dve_kv(dve, g, k):
            dve.wait_ge(s_KVh, g * SPT + k + 1)
            for (rows, high), low in zip(high_parts(k), low_parts(k)):
                ins = dve.tensor_tensor(low, kv_bank(k)[rows, :], high.bitcast(F32), ALU.subtract)
            ins.then_inc(s_KVl, 1)

        def dve_q(dve, g, half, heads):
            b, t = half // 2, slice(2 * (half % 2), 2 * (half % 2) + 2)
            qt = tok[:, bass.ds(g, 1), :].rearrange("p a (n b q) -> p (a n) b q", n=DT, b=BPG)
            for r in heads:
                rows, other = slice(r * HD, (r + 1) * HD), slice((r + 2) % 4 * HD, ((r + 2) % 4 + 1) * HD)
                dve.tensor_copy(qz_h[other, t, r // 2, r % 2, :], qt[rows, t, b, :]).then_inc(s_qd, 1)

        def act_slot(act, g, j, first=False, last=False, tail=False):
            s = g * SPT + j
            if not (first and j < 2) and not (tail and j > 1):
                act.wait_ge(s_T, s - 1)
                if not (first and j < 6):
                    act.wait_ge(s_PV, g * GROUPS + (j - 2) // 2 - 1)
                act.activation(pt_half(j - 2, False), T_bank[:].rearrange("p (k n) -> p k n", k=KT),
                               ACT.Copy).then_inc(s_Th, 1)
            if j % 2 == 0 and not (first and j < 4) and not (tail and j > 2):
                n, quarter, odd = group(j, 4)
                act.wait_ge(s_PV, g * GROUPS + n + 1)
                if n == 0 and not first:
                    act.wait_ge(s_Wo, g)
                for r in range(4):
                    act.activation(OT_h[r * HD:(r + 1) * HD, quarter, odd, :], heads_of(PV_bank, r),
                                   ACT.Copy).then_inc(s_Oh, 1)
            if tail:
                return
            if not (last and j - 1 + AHEAD >= SPT) and not (first and j == 0):
                act_kv(act, g, j - 1 + AHEAD)
            c = slice(j % 4, j % 4 + 1)
            act.wait_ge(s_nm, s + 1)
            act.activation(prob[:, j % 2, :], prob[:, j % 2, :], ACT.Exp, bias=nmx[:, c], scale=SCALE,
                           accum_out=rsum[:, c]).then_inc(s_ex, 1)
            act.wait_ge(s_ri, s + 1)
            act.activation(prob[:, j % 2, :], prob[:, j % 2, :], ACT.Copy, scale=rinv[:, c]).then_inc(s_pn, 1)

        def dve_stats(dve, g, tail=False):
            dve.wait_ge(s_x1, g + 1)
            settle(dve)
            dve.bn_stats(st1[:], tok[:, bass.ds(g - 1, 1), :].rearrange("p a n -> p (a n)")).then_inc(s3_st, 1)
            dve.wait_ge(s3_st, g)
            settle(dve)
            dve.bn_aggr(mv1[:, 0, :], st1[:]).then_inc(s3_mv, 1)
            dve.wait_ge(s3_mv, g)
            dve.tensor_copy(mv3[:, bass.ds(g - 1, 1), :], mv1[:])

        def dve_slot(dve, g, j, first=False, last=False, tail=False):
            s = g * SPT + j
            c = slice(j % 4, j % 4 + 1)
            if not tail:
                dve.wait_ge(s_S, s + 1)
                if not (first and j < 2):
                    dve.wait_ge(s_T, s - 1)
                if j % PAIRS == 0:
                    dve.wait_ge(s_mb, g * BPG + j // PAIRS + 1)
                settle(dve)
                dve.tensor_tensor_reduce(prob[:, j % 2, :], S_bank[j % 2][:], mbias[:, j // PAIRS, :], 1.0,
                                         -3.0e38, ALU.add, ALU.max, mx[:, c]).then_inc(s_mx, 1)
                dve.wait_ge(s_mx, s + 1)
                dve.tensor_scalar(nmx[:, c], mx[:, c], -SCALE, None, ALU.mult).then_inc(s_nm, 1)
            if not (first and j < 2) and not (tail and j > 1):
                dve.wait_ge(s_Th, s - 1)
                dve.tensor_tensor(pt_half(j - 2, True), T_bank[:].rearrange("p (k n) -> p k n", k=KT),
                                  pt_half(j - 2, False).bitcast(F32), ALU.subtract).then_inc(s_Tl, 1)
            if j % 2 == 0 and not (first and j < 4) and not (tail and j > 2):
                n, quarter, odd = group(j, 4)
                dve.wait_ge(s_Oh, g * (4 * GROUPS) + 4 * n + 4)
                for r in range(4):
                    rows = slice(r * HD, (r + 1) * HD)
                    dve.tensor_tensor(OT_l[rows, quarter, odd, :], heads_of(PV_bank, r),
                                      OT_h[rows, quarter, odd, :].bitcast(F32), ALU.subtract).then_inc(s_Ol, 1)
            if j == 5 and not first:
                dve.wait_ge(s_Wo, g)
                dve.wait_ge(s_xr, g * 16)
                dve.tensor_tensor(tok[:, bass.ds(g - 1, 1), :], Wo_bank[:].rearrange("p (a n) -> p a n", a=1),
                                  xres[:], ALU.add).then_inc(s_x1, 1)
            if tail:
                return
            dve.wait_ge(s_ex, s + 1)
            dve.reciprocal(rinv[:, c], rsum[:, c]).then_inc(s_ri, 1)
            if not (last and j - 1 + AHEAD >= SPT) and not (first and j == 0):
                dve_kv(dve, g, j - 1 + AHEAD)
            if j == 11 and not first:
                dve_stats(dve, g)
            if j % 4 < 3 and not (last and j >= SPT - 4):
                half = (j // 4 + 1) % 4
                dve_q(dve, g if half else g + 1, half, ((0,), (1, 2), (3,))[j % 4])

        def sp_contexts(sp, g, first):
            for b in range(BPG):
                n = g * BPG + b
                if not (first and b == 0):
                    sp.wait_ge(s_cx, n * 2)
                settle(sp)
                sp.dma_start(ctx_r[:], ctxT[bass.ds(n, 1), :, :].rearrange("a (t p) n -> p (a t) n", p=P))\
                    .then_inc(s_raw, 16)
                if not first:
                    sp.wait_ge(s_mb, n - 1)
                settle(sp)
                sp.dma_start(mask8[:, b, :], mask[bass.ds(n, 1), :].broadcast_to([P, SK])).then_inc(s_mraw[b], 16)

        def sp_tile(sp, g, first=False, last=False):
            if not first:
                sp_contexts(sp, g, first)
                sp.wait_ge(s_x1, g + 1)
            settle(sp)
            sp.dma_start(xres[:], xt[:, bass.ds(g, 1), :]).then_inc(s_xr, 16)

        def pool_ctx(pool, g, b, first):
            n = g * BPG + b
            pool.wait_ge(s_raw, n * 16 + 16)
            if not (first and b == 0):
                pool.wait_ge(s_qz, (n - 1) * 16 + 8)
            if not (first and b < 2):
                pool.wait_ge(s_KV, (n - 1) * TILES)
            settle(pool)
            pool.tensor_scalar(ctx_h[:, b % 2, :, :], ctx_r[:], 1.0, None, ALU.mult).then_inc(s_cx, 1)
            pool.wait_ge(s_cx, n * 2 + 1)
            settle(pool)
            pool.tensor_tensor(ctx_l[:, b % 2, :, :], ctx_r[:], ctx_h[:, b % 2, :, :].bitcast(F32),
                               ALU.subtract).then_inc(s_cx, 1)

        def pool_q(pool, g, b, half, first, last):
            n = g * BPG + b
            if not (first and b == 0):
                pool.wait_ge(s_S, n * PAIRS - 4 + 4 * half)
            qt = tok[:, bass.ds(g, 1), :].rearrange("p a (n b q) -> p (a n) b q", n=DT, b=BPG)
            t = slice(2 * half, 2 * half + 2)
            for low in (0, 1):
                for r in range(4):
                    rows = slice(r * HD, (r + 1) * HD)
                    src, dst = qt[rows, t, b, :], qz_h[rows, t, r // 2, r % 2, :]
                    if low or r:
                        pool.wait_ge(s_qz, n * 16 + half * 8 + 4 * low + r)
                    elif half == 0:
                        pool.wait_ge(s_mb, n + 1)
                    elif not last or b < BPG - 1:
                        pool.wait_ge(s_cx, n * 2 + 4)
                    settle(pool)
                    if low:
                        ins = pool.tensor_tensor(qz_l[rows, t, r // 2, r % 2, :], src, dst.bitcast(F32), ALU.subtract)
                    else:
                        ins = pool.tensor_copy(dst, src)
                    ins.then_inc(s_qz, 1)

        def pool_mask(pool, g, b, first):
            n = g * BPG + b
            pool.wait_ge(s_mraw[b], g * 16 + 16)
            if not first:
                pool.wait_ge(s_mx, (n - 1) * PAIRS)
            if not (first and b == 0):
                pool.wait_ge(s_qz, n * 16)
            settle(pool)
            pool.tensor_scalar(mbias[:, b, :], mask8[:, b, :], -1.0, BIG, ALU.add, ALU.mult).then_inc(s_mb, 1)

        def pool_tile(pool, g, first=False, last=False):
            for b in range(BPG):
                if not (first and b == 0):
                    pool_mask(pool, g, b, first)
                    pool_q(pool, g, b, 0, first, last)
                if not (last and b == BPG - 1):
                    pool_ctx(pool, g, b + 1, first)
                pool_q(pool, g, b, 1, first, last)

        def tiles(eng, tile):
            tile(0, True, False)
            with eng.Fori(1, G - 1) as g:
                tile(g, False, False)
            tile(G - 1, False, True)

        m = Map(nc, base)
        raw3 = m("raw3", [P, 3, DT, D], F32)
        assert m.at <= wo_at
        m = Map(nc, ctx_at)
        qw_h, qw_l = m("aq_h", [P, DT, D], F32R), m("aq_l", [P, DT, D], F32R)
        kw_h = m("ak_h", [P, DT, D], F32R)
        rope = m("rope", [P, 2, HD], F32)
        cmask = m("cmask", [P, SQ], F32)
        assert m.at <= ctx_end
        s3_w = [sem(f"p3_w{i}") for i in range(4)]
        s3_c = sem("p3_const")
        s3_ws = sem("p3_ws")
        s3_st, s3_mv = sem("p3_st"), sem("p3_mv")

        with nc.Block() as block:
            @block.sync
            def _(sp):
                for t in range(CH):
                    sp.dma_start(tok[:, t, :], xt[:, t, :]).then_inc(s_x0[t], 16)
                for c in range(1, NCH):
                    sp.dma_start(tok[:, c * CH:(c + 1) * CH, :], xt[:, c * CH:(c + 1) * CH, :]).then_inc(s_x[c], 16)
                for i, (r, w) in enumerate(((wk_r, wk), (wv_r, wv), (wo_r, wo))):
                    sp.dma_start(r[:], w.rearrange("(t p) n -> p t n", p=P)).then_inc(s_wkv[i], 16)
                sp_contexts(sp, 0, True)

            @block.gpsimd
            def _(pool):
                pool.memset(ident[:], 0.0).then_inc(s_id, 1)
                pool.memset(epsb[:], LN_EPS).then_inc(s_eps, 1)
                pool.wait_ge(s_id, 1)
                pool.affine_select(out=ident[:], in_=ident[:], compare_op=ALU.not_equal, fill=1.0, base=0,
                                   pattern=[[-1, P]], channel_multiplier=1).then_inc(s_id, 1)
                pool.memset(qz_h[:].bitcast(F32), 0.0).then_inc(s_z, 1)
                pool.memset(qz_l[:].bitcast(F32), 0.0).then_inc(s_z, 1)

                def split(i, r, h, l):
                    pool.wait_ge(s_wkv[i], 16)
                    pool.tensor_scalar(h[:], r[:], 1.0, None, ALU.mult).then_inc(s_pw, 1)
                    pool.wait_ge(s_pw, 2 * i + 1)
                    pool.tensor_tensor(l[:], r[:], h[:].bitcast(F32), ALU.subtract).then_inc(s_pw, 1)
                    pool.wait_ge(s_pw, 2 * i + 2)

                split(0, wk_r, wk_h, wk_l)
                split(1, wv_r, wv_h, wv_l)
                pool_ctx(pool, 0, 0, True)
                pool.wait_ge(s_cx, 2)
                pool_mask(pool, 0, 0, True)
                split(2, wo_r, wo_h, wo_l)
                pool.wait_ge(s_z, 2)
                pool.wait_ge(s_qe, DT)
                pool_q(pool, 0, 0, 0, True, False)

            @block.vector
            def _(dve):
                def deviations(c):
                    for t in range(CH):
                        dve.wait_ge(s_x[c] if c else s_x0[t], 16)
                        dve.bn_stats(stats[:, t, :], tok[:, c * CH + t, :]).then_inc(s_st, 1)
                    if c >= 1:
                        dve.wait_ge(s_xn, CH * c)
                    for t in range(CH):
                        dve.wait_ge(s_st, CH * c + t + 1)
                        dve.bn_aggr(mv[:, t, :], stats[:, t, :]).then_inc(s_var, 1)
                    dve.wait_ge(s_sd, c + 1)
                    dve.reciprocal(rstd[:], rstd[:]).then_inc(s_rs, 1)
                    dve.wait_ge(s_rs, c + 1)

                def normalize(c):
                    if c >= 1:
                        dve.wait_ge(s_tr, DT * c)
                    for t in range(CH):
                        dve.tensor_scalar(xn[:, t, :], tok[:, c * CH + t, :], mv[:, t, 0:1], rstd[:, t:t + 1],
                                          ALU.subtract, ALU.mult).then_inc(s_xn, 1)

                def low(c, k):
                    dve.wait_ge(s_hi, DT * c + k + 1)
                    dve.tensor_tensor(xnT_l[:, k, :], bank[k][:], xnT_h[:, k, :].bitcast(F32),
                                      ALU.subtract).then_inc(s_lo, 1)

                deviations(0)
                normalize(0)
                for k in range(DT):
                    dve.wait_ge(s_wh, k + 1)
                    dve.tensor_tensor(wq_l[:, k, :], wq_r[:, k, :], wq_h[:, k, :].bitcast(F32),
                                      ALU.subtract).then_inc(s_wl, 1)
                    low(0, k)
                deviations(1)
                normalize(1)
                for c in range(1, NCH):
                    low(c, 0)
                    low(c, 1)
                    if c + 1 < NCH:
                        deviations(c + 1)
                        normalize(c + 1)
                    low(c, 2)
                    low(c, 3)
                dve.wait_ge(s_qe, DT)
                dve.wait_ge(s_z, 1)
                dve_q(dve, 0, 0, range(4))

            @block.scalar
            def _(act):
                for k in range(DT):
                    act.dma_start(wq_r[:, k, :], wq[k * P:(k + 1) * P, :]).then_inc(s_w[k], 16)
                act.wait_ge(s_eps, 1)

                def deviation(c):
                    act.wait_ge(s_var, CH * (c + 1))
                    act.activation(rstd[:], mv[:, :, 1], ACT.Sqrt, bias=epsb[:]).then_inc(s_sd, 1)

                def high(c, k):
                    act.wait_ge(s_tr, DT * c + k + 1)
                    if c >= 1:
                        act.wait_ge(s_q, DT * (c - 1) + k + 1)
                    act.activation(xnT_h[:, k, :], bank[k][:], ACT.Copy).then_inc(s_hi, 1)

                deviation(0)
                for k in range(DT):
                    act.wait_ge(s_w[k], 16)
                    act.activation(wq_h[:, k, :], wq_r[:, k, :], ACT.Copy).then_inc(s_wh, 1)
                for k in range(DT):
                    high(0, k)
                deviation(1)
                for c in range(NCH):
                    if c + 1 < NCH:
                        high(c + 1, 0)
                        high(c + 1, 1)
                    if c + 2 < NCH:
                        deviation(c + 2)
                    act.wait_ge(s_q, DT * (c + 1))
                    for mt in range(DT):
                        act.activation(
                            tok[:, c * CH:(c + 1) * CH, mt * P:(mt + 1) * P],
                            bank[4 + mt][:].rearrange("p (t n) -> p t n", t=CH), ACT.Copy).then_inc(s_qe, 1)
                    if c + 1 < NCH:
                        high(c + 1, 2)
                        high(c + 1, 3)
                act.wait_ge(s_qe, DT * NCH)

            @block.tensor
            def _(pe):
                def transpose(c, k):
                    pe.wait_ge(s_xn, CH * (c + 1))
                    if c >= 1:
                        pe.wait_ge(s_lo, DT * (c - 1) + k + 1)
                    for t in range(CH):
                        ins = pe.transpose(bank[k][:, t * P:(t + 1) * P], xn[:, t, k * P:(k + 1) * P], ident[:])
                    ins.then_inc(s_tr, 1)

                pe.wait_ge(s_id, 2)
                for k in range(DT):
                    transpose(0, k)
                for c in range(NCH):
                    for k in range(DT):
                        if c == 0:
                            pe.wait_ge(s_wl, k + 1)
                        pe.wait_ge(s_lo, DT * c + k + 1)
                        for mt in range(DT):
                            if c >= 1 and k == 0:
                                pe.wait_ge(s_qe, DT * (c - 1) + mt + 1)
                            for w, y in ((wq_h, xnT_h), (wq_h, xnT_l), (wq_l, xnT_h)):
                                ins = pe.matmul(bank[4 + mt][:], w[:, k, mt * P:(mt + 1) * P], y[:, k, :],
                                                start=(k == 0 and w is wq_h and y is xnT_h),
                                                stop=(k == DT - 1 and w is wq_l))
                        ins.then_inc(s_q, 1)
                        if c + 1 < NCH and k >= 1:
                            transpose(c + 1, k - 1)
                    if c + 1 < NCH:
                        transpose(c + 1, DT - 1)

        with nc.Block() as block:
            @block.sync
            def _(sp):
                tiles(sp, lambda g, first, last: sp_tile(sp, g, first, last))
                sp.wait_ge(s_KV, B * TILES)
                for i, w in enumerate((aq, ak, av)):
                    sp.dma_start(raw3[:, i], w.rearrange("(t p) n -> p t n", p=P)).then_inc(s3_w[i], 16)
                for i in range(BPG):
                    rows = slice(i * SQ, (i + 1) * SQ)
                    sp.dma_start(rope[rows, 0, :], cos_tab).then_inc(s3_c, 16)
                    sp.dma_start(rope[rows, 1, :], sin_tab).then_inc(s3_c, 16)
                    sp.dma_start(cmask[rows, :], causal).then_inc(s3_c, 16)

            @block.gpsimd
            def _(pool):
                tiles(pool, lambda g, first, last: pool_tile(pool, g, first, last))
                pool.wait_ge(s_KV, B * TILES)
                pool.wait_ge(s_qz, B * 16)
                pool.wait_ge(s3_w[0], 16)
                pool.tensor_scalar(qw_h[:], raw3[:, 0], 1.0, None, ALU.mult).then_inc(s3_ws, 1)
                pool.wait_ge(s3_ws, 1)
                pool.tensor_tensor(qw_l[:], raw3[:, 0], qw_h[:].bitcast(F32), ALU.subtract).then_inc(s3_ws, 1)
                pool.wait_ge(s3_w[1], 16)
                pool.wait_ge(s3_ws, 2)
                pool.tensor_scalar(kw_h[:], raw3[:, 1], 1.0, None, ALU.mult).then_inc(s3_ws, 1)

            @block.tensor
            def _(pe):
                def tile(g, first, last):
                    for j in range(SPT):
                        pe_slot(pe, g, j, first, last)
                for k in range(AHEAD):
                    pe_kv(pe, 0, k, True)
                tiles(pe, tile)
                for j in range(4):
                    pe_slot(pe, G, j, tail=True)

            @block.scalar
            def _(act):
                def tile(g, first, last):
                    for j in range(SPT):
                        act_slot(act, g, j, first, last)
                for k in range(AHEAD):
                    act_kv(act, 0, k)
                tiles(act, tile)
                for j in range(4):
                    act_slot(act, G, j, tail=True)

            @block.vector
            def _(dve):
                def tile(g, first, last):
                    for j in range(SPT):
                        dve_slot(dve, g, j, first, last)
                dve.sem_inc(s_x1, 1)
                for k in range(AHEAD):
                    dve_kv(dve, 0, k)
                tiles(dve, tile)
                for j in range(6):
                    dve_slot(dve, G, j, tail=True)
                dve_stats(dve, G, tail=True)

        if stop_after == 2:
            s_dbg = sem("dbg")
            with nc.Block() as block:
                @block.sync
                def _(sp):
                    sp.dma_start(outt, tok[:]).then_inc(s_dbg, 16)
                    sp.wait_ge(s_dbg, 16)
            return

        m = Map(nc, wo_at)
        kw_l = m("ak_l", [P, DT, D], F32R)
        vw_h, vw_l = m("av_h", [P, DT, D], F32R), m("av_l", [P, DT, D], F32R)
        ow = m("ao_sb", [P, DT, D], F32)
        qb = m("qb", [P, DT, BPG, 4, SQ], F32)
        pb = m("pb", [P, DT, BPG, 2, P], F32)
        sm = m("sm", [P, 2, DT, 2, BPG, SQ], F32)
        x3_h, x3_l = m("x3_h", [P, 2, DT, P], F32R), m("x3_l", [P, 2, DT, P], F32R)
        cur = m("cur", [P, 3], F32)
        xn3 = m("xn3", [P, D], F32)
        r_cos, r_sin = m("r_cos", [P, D], F32), m("r_sin", [P, D], F32)
        q_r, k_r = m("q_r", [P, D], F32), m("k_r", [P, D], F32)
        v_sb = m("v_sb", [P, 2, D], F32)
        k_T = m("k_T", [P, DT, P], F32)
        mx3, rc3 = m("mx3", [P, HEADS], F32), m("rc3", [P, 2, HEADS], F32)
        o_T = m("o_T", [P, DT, BPG, SQ], F32)
        assert m.at <= ctx_at, (m.at, ctx_at)

        s3_wa, s3_wd = sem("p3_wa"), sem("p3_wd")
        s3_z = sem("p3_z")
        s3_sd, s3_rs = sem("p3_sd"), sem("p3_rs")
        s3_cu, s3_xn, s3_XT, s3_xh, s3_xl = sem("p3_cu"), sem("p3_xn"), sem("p3_XT"), sem("p3_xh"), sem("p3_xl")
        s3_Q, s3_K, s3_V, s3_Tq, s3_Tk = sem("p3_Q"), sem("p3_K"), sem("p3_V"), sem("p3_Tq"), sem("p3_Tk")
        s3_rq, s3_rk, s3_aq, s3_ak = sem("p3_rq"), sem("p3_rk"), sem("p3_aq"), sem("p3_ak")
        s3_v = sem("p3_v")
        s3_qa, s3_qd, s3_kT = sem("p3_qa"), sem("p3_qd"), sem("p3_kT")
        s3_S, s3_ms, s3_mx, s3_su, s3_ex = sem("p3_S"), sem("p3_ms"), sem("p3_mx"), sem("p3_su"), sem("p3_ex")
        s3_sm, s3_rc, s3_pn = sem("p3_sum"), sem("p3_rc"), sem("p3_pn")
        s3_PT, s3_pa, s3_pd = sem("p3_PT"), sem("p3_pa"), sem("p3_pd")
        s3_PV, s3_oa, s3_od, s3_Wo, s3_x = sem("p3_PV"), sem("p3_oa"), sem("p3_od"), sem("p3_Wo"), sem("p3_x")

        def has(t):
            return not isinstance(t, int) or 0 <= t < G

        def one_tile(t):
            return tok[:, bass.ds(t, 1), :].rearrange("p a n -> p (a n)")

        def project(pe, b, y_h, y_l, w_h, w_l):
            for k in range(DT):
                for i, (y, w) in enumerate(((y_h, w_h), (y_h, w_l), (y_l, w_h))):
                    ins = pe.matmul(b, y[:, k, :], w[:, k, :], start=(k == 0 and i == 0),
                                    stop=(k == DT - 1 and i == PRODUCTS - 1))
            return ins

        def pe3(pe, t, par):
            nxt = 1 - par
            if has(t):
                pe.wait_ge(s3_aq, t + 1)
                at_least(pe, s3_xl, t + 2 if not isinstance(t, int) else min(t + 2, G))
                for n in range(DT):
                    ins = pe.transpose(bank[0][:, n * P:(n + 1) * P], q_r[:, n * P:(n + 1) * P], ident[:])
                ins.then_inc(s3_Tq, 1)
                pe.wait_ge(s3_ak, t + 1)
                for n in range(DT):
                    ins = pe.transpose(bank[1][:, n * P:(n + 1) * P], k_r[:, n * P:(n + 1) * P], ident[:])
                ins.then_inc(s3_Tk, 1)
            if has(t + 1):
                at_least(pe, s3_xl, t + 2)
                at_least(pe, s3_v, t + 1)
                if isinstance(t, int) and t == -1:
                    pe.wait_ge(s3_ws, 2)
                project(pe, bank[2], x3_h[:, nxt, :, :], x3_l[:, nxt, :, :], qw_h, qw_l).then_inc(s3_Q, 1)
            if has(t):
                pe.wait_ge(s3_kT, t + 1)
                pe.wait_ge(s3_qa, 2 * t + 2)
                pe.wait_ge(s3_qd, 2 * t + 2)
                for n in range(DT):
                    if n < 2:
                        at_least(pe, s3_oa, 4 * t - 4)
                        at_least(pe, s3_od, 4 * t - 4)
                    else:
                        pe.wait_ge(s3_ms, 4 * t + n - 1)
                    for b in range(BPG):
                        for pl in range(2):
                            at = pl * 2 * P + b * SQ
                            ins = pe.matmul(bank[4 + n % 2][:, at:at + P],
                                            qb[:, n, b, 2 * pl:2 * pl + 2, :].rearrange("p a b -> p (a b)"), k_T[:, n, :],
                                            start=True, stop=True)
                    ins.then_inc(s3_S, 1)
            if has(t + 1):
                at_least(pe, s3_x, t - 1)
                if isinstance(t, int) and t == -1:
                    pe.wait_ge(s3_ws, 3)
                    pe.wait_ge(s3_wd, 1)
                project(pe, bank[3], x3_h[:, nxt, :, :], x3_l[:, nxt, :, :], kw_h, kw_l).then_inc(s3_K, 1)
            if has(t - 1):
                pe.wait_ge(s3_pn, t)
                for h in range(2):
                    for i in range(4):
                        n, pl = 2 * h + i // 2, i % 2
                        ins = pe.transpose(bank[h][:, i * P:(i + 1) * P],
                                           sm[:, nxt, n, pl, :, :].rearrange("p b k -> p (b k)"), ident[:])
                    ins.then_inc(s3_PT, 1)
            if has(t + 1):
                pe.wait_ge(s3_rq, 2 * t + 4)
                if isinstance(t, int) and t == -1:
                    pe.wait_ge(s3_wa, 1)
                    pe.wait_ge(s3_wd, 2)
                project(pe, bank[2], x3_h[:, nxt, :, :], x3_l[:, nxt, :, :], vw_h, vw_l).then_inc(s3_V, 1)
            if has(t - 1):
                pe.wait_ge(s3_v, t)
                for n in range(DT):
                    if n % 2 == 0:
                        pe.wait_ge(s3_pa, 2 * t - 1 + n // 2)
                        pe.wait_ge(s3_pd, 2 * t - 1 + n // 2)
                    if n == 0:
                        at_least(pe, s3_oa, 4 * (t - 1) - 2)
                        at_least(pe, s3_od, 4 * (t - 1) - 2)
                    if n == 2 and has(t):
                        pe.wait_ge(s3_ms, 4 * t + 4)
                    ins = pe.matmul(bank[(6, 7, 4, 5)[n]], v_sb[:, nxt, n * P:(n + 1) * P],
                                    pb[:, n, :, :, :].rearrange("p a b c -> p (a b c)"), start=True, stop=True)
                    if n % 2:
                        ins.then_inc(s3_PV, 1)
            if has(t + 2):
                at_least(pe, s3_xn, t + 3)
                if has(t - 1):
                    pe.wait_ge(s3_pa, 2 * t)
                    pe.wait_ge(s3_pd, 2 * t)
                for k in range(DT):
                    ins = pe.transpose(bank[0][:, k * P:(k + 1) * P], xn3[:, k * P:(k + 1) * P], ident[:])
                ins.then_inc(s3_XT, 1)
            if has(t - 1):
                if has(t + 1):
                    pe.wait_ge(s3_rk, 2 * t + 4)
                if isinstance(t, int) and t == 1:
                    pe.wait_ge(s3_w[3], 16)
                for n in range(DT):
                    if n % 2 == 0:
                        pe.wait_ge(s3_oa, 4 * t - 2 + n)
                        pe.wait_ge(s3_od, 4 * t - 2 + n)
                    ins = pe.matmul(bank[3], o_T[:, n, :, :].rearrange("p b q -> p (b q)"), ow[:, n, :],
                                    start=(n == 0), stop=(n == DT - 1))
                ins.then_inc(s3_Wo, 1)

        def head_rows(r):
            return slice(r * HD, (r + 1) * HD)

        def q_blocks(eng_copy, r):
            return eng_copy(qb[head_rows(r), :, :, r, :],
                            bank[0][head_rows(r), :].rearrange("p (n b q) -> p n b q", n=DT, b=BPG))

        def o_blocks(eng_copy, pair, r):
            src = (psum[:, 6:8, :] if pair == 0 else psum[:, 4:6, :])[head_rows(r), :, :]
            src = src.rearrange("p n (b h q) -> p n b h q", b=BPG, h=4)[:, :, :, r, :]
            return eng_copy(o_T[head_rows(r), 2 * pair:2 * pair + 2, :, :], src)

        def p_block(eng_copy, h, b):
            rows = slice(b * SQ, (b + 1) * SQ)
            return eng_copy(pb[rows, 2 * h:2 * h + 2, b, :, :],
                            bank[h][rows, :].rearrange("p (n l c) -> p n l c", n=2, l=2))

        def act3(act, t, par):
            nxt = 1 - par
            copy = lambda o, i: act.activation(o, i, ACT.Copy)
            if has(t):
                act.wait_ge(s3_Tq, t + 1)
                at_least(act, s3_S, 4 * t)
                for r in range(2):
                    q_blocks(copy, r).then_inc(s3_qa, 1)
                act.wait_ge(s3_Tk, t + 1)
                copy(k_T[:].rearrange("p n c -> p (n c)"), bank[1]).then_inc(s3_kT, 1)
            if has(t - 1):
                at_least(act, s3_PV, 2 * t - 2)
                for h in range(2):
                    act.wait_ge(s3_PT, 2 * t - 1 + h)
                    p_block(copy, h, 0).then_inc(s3_pa, 1)
            if has(t):
                act.wait_ge(s3_su, t + 1)
                s_ = sm[:, par].rearrange("p a b c d -> p (a b c d)")
                act.activation(s_, s_, ACT.Exp).then_inc(s3_ex, 1)
            if has(t - 1):
                at_least(act, s3_Wo, t - 1)
                for pair in range(2):
                    act.wait_ge(s3_PV, 2 * t - 1 + pair)
                    for r in range(2):
                        o_blocks(copy, pair, r).then_inc(s3_oa, 1)
            if has(t + 2):
                act.wait_ge(s3_XT, t + 3)
                at_least(act, s3_V, t + 1)
                copy(x3_h[:, par].rearrange("p n c -> p (n c)"), bank[0]).then_inc(s3_xh, 1)
            if has(t + 1):
                act.wait_ge(s3_V, t + 2)
                at_least(act, s3_PV, 2 * t)
                copy(v_sb[:, nxt, :], bank[2]).then_inc(s3_v, 1)

        def rotate_parts(dve, psum_bank, done, pool_sem, pool_count):
            at_least(dve, pool_sem, pool_count)
            p4 = psum_bank.rearrange("p (h i) -> p h i", h=HEADS)
            dve.tensor_tensor(r_cos[:].rearrange("p (h i) -> p h i", h=HEADS), p4,
                              rope[:, 0:1, :].broadcast_to([P, HEADS, HD]), ALU.mult).then_inc(done, 1)
            for e in range(2):
                swapped = psum_bank.rearrange("p (h i e) -> p h i e", h=HEADS, e=2)[:, :, :, 1 - e]
                o = r_sin[:].rearrange("p (h i e) -> p h i e", h=HEADS, e=2)[:, :, :, e]
                w = rope[:, 1:2, e::2].broadcast_to([P, HEADS, HD // 2])
                ins = dve.tensor_tensor(o, swapped, w, ALU.mult)
            ins.then_inc(done, 1)

        def dve3(dve, t, par):
            nxt = 1 - par
            copy = dve.tensor_copy
            if has(t):
                dve.wait_ge(s3_Tq, t + 1)
                at_least(dve, s3_S, 4 * t)
                for r in range(2, 4):
                    q_blocks(copy, r).then_inc(s3_qd, 1)
            if has(t + 2):
                at_least(dve, s3_xn, t + 2)
                dve.tensor_copy(cur[:, 0:2], mv3[:, bass.ds(t + 2, 1), :].rearrange("p a b -> p (a b)"))
                dve.tensor_copy(cur[:, 2:3], rs3[:, bass.ds(t + 2, 1)]).then_inc(s3_cu, 1)
                dve.wait_ge(s3_cu, t + 3)
                at_least(dve, s3_XT, t + 2)
                dve.tensor_scalar(xn3[:], one_tile(t + 2), cur[:, 0:1], cur[:, 2:3],
                                  ALU.subtract, ALU.mult).then_inc(s3_xn, 1)
            if has(t):
                at_least(dve, s3_PT, 2 * t - 2)
                for n in range(DT):
                    dve.wait_ge(s3_S, 4 * t + n + 1)
                    src = bank[4 + n % 2].rearrange("p (u w) -> p u w", w=P)[:, :, 0:SQ]
                    dve.scalar_tensor_tensor(out=sm[:, par, n].rearrange("p l b k -> p (l b) k"), in0=src,
                                             scalar=SCALE, in1=cmask[:].rearrange("p (a k) -> p a k", a=1)
                                             .broadcast_to([P, 4, SQ]), op0=ALU.mult, op1=ALU.add).then_inc(s3_ms, 1)
            if has(t + 1):
                dve.wait_ge(s3_Q, t + 2)
                rotate_parts(dve, bank[2], s3_rq, s3_ak, t + 1)
            if has(t):
                dve.wait_ge(s3_ms, 4 * t + 4)
                at_least(dve, s3_su, t)
                dve.tensor_reduce(mx3[:], sm[:, par].rearrange("p n l b k -> p (n l b) k"), AX_X,
                                  ALU.max).then_inc(s3_mx, 1)
            if has(t + 1):
                dve.wait_ge(s3_K, t + 2)
                rotate_parts(dve, bank[3], s3_rk, s3_aq, t + 2)
            if has(t - 1):
                at_least(dve, s3_PV, 2 * t - 2)
                for h in range(2):
                    dve.wait_ge(s3_PT, 2 * t - 1 + h)
                    p_block(copy, h, 1).then_inc(s3_pd, 1)
                at_least(dve, s3_Wo, t - 1)
                for pair in range(2):
                    dve.wait_ge(s3_PV, 2 * t - 1 + pair)
                    for r in range(2, 4):
                        o_blocks(copy, pair, r).then_inc(s3_od, 1)
            if has(t):
                dve.wait_ge(s3_ex, t + 1)
                dve.tensor_reduce(rc3[:, 0, :], sm[:, par].rearrange("p n l b k -> p (n l b) k"), AX_X,
                                  ALU.add).then_inc(s3_sm, 1)
                dve.wait_ge(s3_sm, t + 1)
                at_least(dve, s3_pn, t)
                dve.reciprocal(rc3[:, 1, :], rc3[:, 0, :]).then_inc(s3_rc, 1)
            if has(t + 2):
                dve.wait_ge(s3_xh, t + 3)
                dve.tensor_tensor(x3_l[:, par].rearrange("p n c -> p (n c)"), bank[0],
                                  x3_h[:, par].rearrange("p n c -> p (n c)").bitcast(F32),
                                  ALU.subtract).then_inc(s3_xl, 1)
            if has(t - 1):
                dve.wait_ge(s3_Wo, t)
                dve.tensor_tensor(one_tile(t - 1), bank[3], one_tile(t - 1), ALU.add).then_inc(s3_x, 1)

        def pool3(pool, t, par):
            if has(t + 1):
                pool.wait_ge(s3_rq, 2 * t + 4)
                at_least(pool, s3_Tq, t + 1)
                settle(pool)
                pool.tensor_tensor(q_r[:], r_cos[:], r_sin[:], ALU.add).then_inc(s3_aq, 1)
            if has(t):
                pool.wait_ge(s3_mx, t + 1)
                settle(pool)
                s_ = sm[:, par].rearrange("p n l b k -> p (n l b) k")
                pool.tensor_tensor(s_, s_, mx3[:].rearrange("p (u a) -> p u a", a=1).broadcast_to([P, HEADS, SQ]),
                                   ALU.subtract).then_inc(s3_su, 1)
            if has(t + 1):
                pool.wait_ge(s3_rk, 2 * t + 4)
                at_least(pool, s3_Tk, t + 1)
                settle(pool)
                pool.tensor_tensor(k_r[:], r_cos[:], r_sin[:], ALU.add).then_inc(s3_ak, 1)
            if has(t):
                pool.wait_ge(s3_rc, t + 1)
                settle(pool)
                s_ = sm[:, par].rearrange("p n l b k -> p (n l b) k")
                pool.tensor_tensor(s_, s_, rc3[:, 1, :].rearrange("p (u a) -> p u a", a=1)
                                   .broadcast_to([P, HEADS, SQ]), ALU.mult).then_inc(s3_pn, 1)

        def steps(eng, step, start=-2):
            for t in range(start, 2):
                step(eng, t, t % 2)
            with eng.Fori(1, G // 2 - 1) as h:
                step(eng, 2 * h, 0)
                step(eng, 2 * h + 1, 1)
            for t in range(G - 2, G + 1):
                step(eng, t, t % 2)

        with nc.Block() as block:
            @block.sync
            def _(sp):
                sp.dma_start(ow[:], ao.rearrange("(t p) n -> p t n", p=P)).then_inc(s3_w[3], 16)
                sp.wait_ge(s3_w[3], 16)

            @block.gpsimd
            def _(pool):
                pool.memset(qb[:], 0.0).then_inc(s3_z, 1)
                pool.memset(pb[:], 0.0).then_inc(s3_z, 1)
                steps(pool, pool3)

            @block.vector
            def _(dve):
                def low(weights, h, l):
                    dve.tensor_tensor(l[:], raw3[:, weights], h[:].bitcast(F32), ALU.subtract).then_inc(s3_wd, 1)

                dve.wait_ge(s3_sd, 1)
                dve.reciprocal(rs3[:], rs3[:]).then_inc(s3_rs, 1)
                dve.wait_ge(s3_rs, 1)
                dve3(dve, -2, 0)
                dve.wait_ge(s3_ws, 3)
                low(1, kw_h, kw_l)
                dve.wait_ge(s3_wa, 1)
                low(2, vw_h, vw_l)
                dve.wait_ge(s3_z, 2)
                dve.wait_ge(s3_c, 16 * 3 * BPG)
                steps(dve, dve3, -1)

            @block.scalar
            def _(act):
                act.activation(rs3[:], mv3[:, :, 1], ACT.Sqrt, bias=epsb[:]).then_inc(s3_sd, 1)
                act.wait_ge(s3_w[2], 16)
                act.activation(vw_h[:], raw3[:, 2], ACT.Copy).then_inc(s3_wa, 1)
                act.wait_ge(s3_z, 2)
                steps(act, act3)

            @block.tensor
            def _(pe):
                steps(pe, pe3)

        if stop_after == 3:
            s_dbg = sem("dbg")
            with nc.Block() as block:
                @block.sync
                def _(sp):
                    sp.dma_start(outt, tok[:]).then_inc(s_dbg, 16)
                    sp.wait_ge(s_dbg, 16)
            return

        KEEP = SQ // 2
        FF = w1.shape[0]
        ST = B * KEEP // P
        m = Map(nc, base)
        xs_h, xs_l = m("xs_h", [P, DT, ST * P], F32R), m("xs_l", [P, DT, ST * P], F32R)
        ohT = m("ohT", [P, G, P], F32)
        s_all, w_all = m("s_all", [P, G], F32), m("w_all", [P, G], F32)
        b1_sb, b2_sb = m("b1_sb", [P, FF], F32), m("b2_sb", [P, D], F32)
        after4 = m.at
        xn4 = m("xn4", [P, CH, D], F32)
        router_sb = m("router_sb", [P, D], F32)
        dots = m("dots", [P, D], F32)
        ones = m("ones", [P, P], F32)
        dg = m("dg", [P, CH, P], F32)
        s4, r1, r2, rank = m("s4", [P, CH], F32), m("r1", [P, CH], F32), m("r2", [P, CH], F32), m("rank", [P, CH], F32)
        same, before = m("same", [P, P], F32), m("before", [P, P], F32)
        slot_no = m("slot_no", [P, 2, P], F32)
        junk = m("junk", [P, 2, P], F32)
        oh = m("oh", [P, CH, P], F32)
        assert m.at <= nc.sbuf_usable_end, m.at

        s4_c, s4_on, s4_b = sem("p4_const"), sem("p4_ones"), sem("p4_b")
        s4_st, s4_mv, s4_sd, s4_rs, s4_xn = sem("p4_st"), sem("p4_mv"), sem("p4_sd"), sem("p4_rs"), sem("p4_xn")
        s4_s, s4_dg, s4_R, s4_cp, s4_eq = sem("p4_s"), sem("p4_dg"), sem("p4_R"), sem("p4_cp"), sem("p4_eq")
        s4_rk, s4_oh, s4_G, s4_T = sem("p4_rk"), sem("p4_oh"), sem("p4_G"), sem("p4_T")
        s4_gh, s4_gl, s4_oc, s4_tk, s4_sg = sem("p4_gh"), sem("p4_gl"), sem("p4_oc"), sem("p4_tk"), sem("p4_sg")

        def chunks(eng, chunk):
            chunk(0)
            with eng.Fori(1, NCH) as c:
                chunk(c)

        with nc.Block() as block:
            @block.sync
            def _(sp):
                sp.dma_start(router_sb[:], router.rearrange("(a n) -> a n", a=1).broadcast_to([P, D]))\
                    .then_inc(s4_c, 16)
                sp.dma_start(same[:], same_in).then_inc(s4_c, 16)
                sp.dma_start(before[:], before_in).then_inc(s4_c, 16)
                sp.dma_start(slot_no[:], slot_in).then_inc(s4_c, 16)
                sp.dma_start(b1_sb[:], b1).then_inc(s4_b, 16)
                sp.dma_start(b2_sb[:], b2.rearrange("(a n) -> a n", a=1).broadcast_to([P, D])).then_inc(s4_b, 16)
                sp.wait_ge(s4_b, 32)

            @block.gpsimd
            def _(pool):
                pool.memset(ones[:], 1.0).then_inc(s4_on, 1)
                def chunk(c):
                    pool.wait_ge(s4_xn, CH * c + CH)
                    settle(pool)
                    t = tok[:, bass.ds(CH * c, CH), :]
                    pool.tensor_tensor(t, t, xn4[:], ALU.add).then_inc(s4_tk, 1)
                chunks(pool, chunk)

            @block.vector
            def _(dve):
                dve.wait_ge(s4_c, 64)
                dve.wait_ge(s4_on, 1)
                def chunk(c):
                    for t in range(CH):
                        dve.bn_stats(stats[:, t, :], one_tile(CH * c + t)).then_inc(s4_st, 1)
                    at_least(dve, s4_sd, c)
                    for t in range(CH):
                        dve.wait_ge(s4_st, CH * c + t + 1)
                        settle(dve)
                        dve.bn_aggr(mv[:, t, :], stats[:, t, :]).then_inc(s4_mv, 1)
                    dve.wait_ge(s4_sd, c + 1)
                    dve.reciprocal(rstd[:], rstd[:]).then_inc(s4_rs, 1)
                    dve.wait_ge(s4_rs, c + 1)
                    at_least(dve, s4_G, 2 * c)
                    at_least(dve, s4_tk, c)
                    for t in range(CH):
                        dve.tensor_scalar(xn4[:, t, :], one_tile(CH * c + t), mv[:, t, 0:1], rstd[:, t:t + 1],
                                          ALU.subtract, ALU.mult).then_inc(s4_xn, 1)
                    for t in range(CH):
                        dve.wait_ge(s4_xn, CH * c + t + 1)
                        settle(dve)
                        dve.tensor_tensor_reduce(dots[:], xn4[:, t, :], router_sb[:], 1.0, 0.0, ALU.mult, ALU.add,
                                                 s4[:, t:t + 1]).then_inc(s4_s, 1)
                        dve.wait_ge(s4_s, CH * c + t + 1)
                    dve.tensor_copy(s_all[:, bass.ds(CH * c, CH)], s4[:]).then_inc(s4_cp, 1)
                    at_least(dve, s4_R, c)
                    dve.tensor_tensor(dg[:], ident[:].rearrange("p (a n) -> p a n", a=1).broadcast_to([P, CH, P]),
                                      s4[:].rearrange("p (t a) -> p t a", a=1).broadcast_to([P, CH, P]),
                                      ALU.mult).then_inc(s4_dg, 1)
                    dve.wait_ge(s4_R, c + 1)
                    for t in range(CH):
                        row = bank[0][:, t * P:(t + 1) * P]
                        dve.scalar_tensor_tensor(out=junk[:, 0, :], in0=row, scalar=s4[:, t:t + 1], in1=same[:],
                                                 op0=ALU.is_gt, op1=ALU.mult, accum_out=r1[:, t:t + 1]).then_inc(s4_eq, 1)
                        dve.wait_ge(s4_eq, 2 * CH * c + 2 * t + 1)
                        dve.scalar_tensor_tensor(out=junk[:, 1, :], in0=row, scalar=s4[:, t:t + 1], in1=before[:],
                                                 op0=ALU.is_equal, op1=ALU.mult, accum_out=r2[:, t:t + 1]).then_inc(s4_eq, 1)
                        dve.wait_ge(s4_eq, 2 * CH * c + 2 * t + 2)
                    dve.tensor_tensor(rank[:], r1[:], r2[:], ALU.add).then_inc(s4_rk, 1)
                    dve.wait_ge(s4_rk, c + 1)
                    at_least(dve, s4_T, c)
                    for t in range(CH):
                        dve.tensor_scalar(oh[:, t, :], slot_no[:, t % 2, :], rank[:, t:t + 1], None,
                                          ALU.is_equal).then_inc(s4_oh, 1)
                    for h in range(2):
                        dve.wait_ge(s4_gh, 2 * c + h + 1)
                        at = c * (2 * P) + h * P
                        dve.tensor_tensor(xs_l[:, :, bass.ds(at, P)], bank[1 + h].rearrange("p (k n) -> p k n", k=DT),
                                          xs_h[:, :, bass.ds(at, P)].bitcast(F32), ALU.subtract).then_inc(s4_gl, 1)
                chunks(dve, chunk)

            @block.scalar
            def _(act):
                def chunk(c):
                    act.wait_ge(s4_mv, CH * c + CH)
                    at_least(act, s4_xn, CH * c)
                    act.activation(rstd[:], mv[:, :, 1], ACT.Sqrt, bias=epsb[:]).then_inc(s4_sd, 1)
                    for h in range(2):
                        act.wait_ge(s4_G, 2 * c + h + 1)
                        act.activation(xs_h[:, :, bass.ds(c * (2 * P) + h * P, P)],
                                       bank[1 + h].rearrange("p (k n) -> p k n", k=DT), ACT.Copy).then_inc(s4_gh, 1)
                    act.wait_ge(s4_T, c + 1)
                    act.activation(ohT[:, bass.ds(CH * c, CH), :], bank[3].rearrange("p (k n) -> p k n", k=CH),
                                   ACT.Copy).then_inc(s4_oc, 1)
                chunks(act, chunk)
                act.wait_ge(s4_cp, NCH)
                act.activation(w_all[:], s_all[:], ACT.Sigmoid).then_inc(s4_sg, 1)

            @block.tensor
            def _(pe):
                pe.wait_ge(s4_on, 1)
                def chunk(c):
                    pe.wait_ge(s4_dg, c + 1)
                    at_least(pe, s4_rk, c)
                    pe.matmul(bank[0], ones[:], dg[:].rearrange("p a n -> p (a n)"), start=True, stop=True)\
                        .then_inc(s4_R, 1)
                    pe.wait_ge(s4_oh, CH * c + CH)
                    at_least(pe, s4_gl, 2 * c)
                    for h in range(2):
                        for k in range(DT):
                            for e in range(2):
                                ins = pe.matmul(bank[1 + h][:, k * P:(k + 1) * P],
                                                xn4[:, 2 * h + e, k * P:(k + 1) * P], oh[:, 2 * h + e, :],
                                                start=(e == 0), stop=(e == 1))
                        ins.then_inc(s4_G, 1)
                    at_least(pe, s4_oc, c)
                    for t in range(CH):
                        ins = pe.transpose(bank[3][:, t * P:(t + 1) * P], oh[:, t, :], ident[:])
                    ins.then_inc(s4_T, 1)
                chunks(pe, chunk)

        m = Map(nc, after4)
        DEEP = 4
        w_r = m("w_r", [P, DEEP, 2, D], F32)
        w_h, w_l = m("w_h", [P, DEEP, 2, D], F32R), m("w_l", [P, DEEP, 2, D], F32R)
        hid = m("hid", [P, 2, 4 * P], F32)
        hid_h, hid_l = m("hid_h", [P, 2, 4 * P], F32R), m("hid_l", [P, 2, 4 * P], F32R)
        y_sb = m("y_sb", [P, 4, D], F32)
        assert m.at <= nc.sbuf_usable_end, m.at
        SC = ST // 4
        TPC = G // SC

        s5_w = [sem(f"p5_w{i}") for i in range(DEEP)]
        s5_wh, s5_wl, s5_H, s5_g, s5_gh, s5_gl, s5_Y = (sem("p5_wh"), sem("p5_wl"), sem("p5_H"), sem("p5_g"), sem("p5_gh"), sem("p5_gl"),
                                                 sem("p5_Y"))
        s5_y, s5_Sc, s5_x, s5_out = sem("p5_y"), sem("p5_Sc"), sem("p5_x"), sem("p5_out")
        h_bank, sc_bank, y_bank = bank[0:2], bank[2:4], bank[4:8]

        def ffn_tiles(eng, step, after):
            for q in range(SC):
                for f in range(DEEP):
                    step(f, q * FF + f, f, q)
                with eng.Fori(1, FF // DEEP - 1) as h:
                    for e in range(DEEP):
                        step(DEEP * h + e, q * FF + DEEP * h + e, e, q)
                for f in range(FF - DEEP, FF):
                    step(f, q * FF + f, f % DEEP, q)
                after(q)

        with nc.Block() as block:
            @block.sync
            def _(sp):
                def load(f, n, e, q):
                    at_least(sp, s5_wl, n - DEEP + 1)
                    settle(sp)
                    sp.dma_start(w_r[:, e, 0, :], w1[bass.ds(f, 1), :, :].rearrange("a p n -> p (a n)"))\
                        .then_inc(s5_w[e], 16)
                    sp.dma_start(w_r[:, e, 1, :], w2[bass.ds(f, 1), :, :].rearrange("a p n -> p (a n)"))\
                        .then_inc(s5_w[e], 16)

                def store(q):
                    if q == 0:
                        return
                    for t in range(G):
                        sp.wait_ge(s5_x, t + 1)
                        sp.dma_start(outt[:, t, :], tok[:, t, :]).then_inc(s5_out, 16)
                    sp.wait_ge(s5_out, 16 * G)
                ffn_tiles(sp, load, store)

            @block.gpsimd
            def _(pool):
                def split(f, n, e, q):
                    pool.wait_ge(s5_wh, n + 1)
                    settle(pool)
                    pool.tensor_tensor(w_l[:, e], w_r[:, e], w_h[:, e].bitcast(F32), ALU.subtract).then_inc(s5_wl, 1)
                ffn_tiles(pool, split, lambda q: None)

            @block.scalar
            def _(act):
                def weights_high(n, e):
                    act.wait_ge(s5_w[e], 32 * (n // DEEP + 1) if isinstance(n, int) else (n - e) * (32 // DEEP) + 32)
                    at_least(act, s5_Y, n - DEEP + 1)
                    act.activation(w_h[:, e], w_r[:, e], ACT.Copy).then_inc(s5_wh, 1)

                def gelu(f, n, e, q):
                    if isinstance(n, int) and n == 0:
                        weights_high(0, 0)
                        weights_high(1, 1)
                    if not (isinstance(n, int) and n >= SC * FF - 2):
                        weights_high(n + 2, (e + 2) % DEEP)
                    act.wait_ge(s5_H, n + 1)
                    at_least(act, s5_gl, n - 1)
                    act.activation(hid[:, e % 2, :], h_bank[e % 2], ACT.Gelu_apprx_tanh,
                                   bias=b1_sb[:, bass.ds(f, 1)]).then_inc(s5_g, 1)
                ffn_tiles(act, gelu, lambda q: None)

            @block.vector
            def _(dve):
                def split(f, n, e, q):
                    dve.wait_ge(s5_g, n + 1)
                    at_least(dve, s5_Y, n - 1)
                    e = e % 2
                    dve.tensor_copy(hid_h[:, e, :], hid[:, e, :]).then_inc(s5_gh, 1)
                    dve.wait_ge(s5_gh, n + 1)
                    dve.tensor_tensor(hid_l[:, e, :], hid[:, e, :], hid_h[:, e, :].bitcast(F32),
                                      ALU.subtract).then_inc(s5_gl, 1)

                def update(q):
                    dve.wait_ge(s5_Y, FF * (q + 1))
                    at_least(dve, s5_Sc, TPC * q)
                    for i in range(4):
                        dve.tensor_tensor(y_sb[:, i, :], y_bank[i], b2_sb[:], ALU.add).then_inc(s5_y, 1)
                    for t in range(TPC * q, TPC * (q + 1)):
                        dve.wait_ge(s5_Sc, t + 1)
                        dve.scalar_tensor_tensor(out=tok[:, t, :], in0=sc_bank[t % 2], scalar=w_all[:, t:t + 1],
                                                 in1=tok[:, t, :], op0=ALU.mult, op1=ALU.add).then_inc(s5_x, 1)
                ffn_tiles(dve, split, update)

            @block.tensor
            def _(pe):
                def hidden(n, e, q):
                    pe.wait_ge(s5_wl, n + 1)
                    at_least(pe, s5_g, n - 1)
                    for k in range(DT):
                        cols = slice(q * 4 * P, (q + 1) * 4 * P)
                        for i, (w, y) in enumerate(((w_h, xs_h), (w_l, xs_h), (w_h, xs_l))):
                            ins = pe.matmul(h_bank[e % 2], w[:, e, 0, k * P:(k + 1) * P], y[:, k, cols],
                                            start=(k == 0 and i == 0), stop=(k == DT - 1 and i == PRODUCTS - 1))
                    ins.then_inc(s5_H, 1)

                def step(f, n, e, q):
                    if isinstance(f, int) and f == 0:
                        hidden(n, 0, q)
                        at_least(pe, s5_y, 4 * q)
                    if not (isinstance(f, int) and f == FF - 1):
                        hidden(n + 1, (e + 1) % DEEP, q)
                    pe.wait_ge(s5_gl, n + 1)
                    for t in range(4):
                        for i, (h, w) in enumerate(((hid_h, w_h), (hid_h, w_l), (hid_l, w_h))):
                            ins = pe.matmul(y_bank[t], h[:, e % 2, t * P:(t + 1) * P], w[:, e, 1, :],
                                            start=(isinstance(f, int) and f == 0 and i == 0),
                                            stop=(isinstance(f, int) and f == FF - 1 and i == PRODUCTS - 1))
                    ins.then_inc(s5_Y, 1)

                def scatter(q):
                    pe.wait_ge(s5_y, 4 * q + 4)
                    for t in range(TPC * q, TPC * (q + 1)):
                        at_least(pe, s5_x, t - 1)
                        pe.matmul(sc_bank[t % 2], ohT[:, t, :], y_sb[:, (t % TPC) // 2, :], start=True, stop=True)\
                            .then_inc(s5_Sc, 1)
                ffn_tiles(pe, step, scatter)


_INS = ["x", "ctx_768", "mask_BxS2_bf1", "L0_xattn_Wq", "L0_xattn_Wk", "L0_xattn_Wv", "L0_xattn_Wo",
        "L0_attn_wq", "L0_attn_wk", "L0_attn_wv", "L0_attn_wo", "L0_ffn_w_router", "L0_ffn_W1", "L0_ffn_b1",
        "L0_ffn_W2", "L0_ffn_b2"]
STOP = None


def constants(queries, hd, theta=10000.0):
    freq = np.float32(1.0) / np.float32(theta) ** (np.arange(0, hd, 2, dtype=np.float32) / np.float32(hd))
    ang = np.arange(queries, dtype=np.float32)[:, None] * freq[None, :]
    cos = np.repeat(np.cos(ang), 2, axis=1)
    sin = np.stack([-np.sin(ang), np.sin(ang)], axis=-1).reshape(queries, hd)
    seen = np.tril(np.ones((queries, queries), bool))
    token, batch = np.arange(P), np.arange(P) // queries
    same = batch[:, None] == batch[None, :]
    keep, slot = queries // 2, np.arange(P)
    mine = [(slot // keep)[None, :] == (2 * e + batch)[:, None] for e in (0, 1)]
    return {"cos": cos.astype(np.float32), "sin": sin.astype(np.float32),
            "causal": np.where(seen, 0.0, -BIG).astype(np.float32),
            "same": same.astype(np.float32),
            "before": (same & (token[None, :] < token[:, None])).astype(np.float32),
            "slot": np.stack([np.where(x, slot % keep, -1) for x in mine], axis=1).astype(np.float32)}


def kernel(**inputs):
    from concourse import bacc
    from concourse.bass_utils import run_bass_kernel_spmd

    nc = bacc.Bacc("TRN2", target_bir_lowering=False, num_devices=1)
    arrays, args = {}, []
    for name in _INS:
        a = np.ascontiguousarray(inputs[name])
        if name == "ctx_768":
            a = np.ascontiguousarray(a.transpose(0, 2, 1))
        if name == "mask_BxS2_bf1":
            a = a.view(np.uint8)
        if name == "L0_ffn_W1":
            d, f = a.shape
            a = np.ascontiguousarray(a.reshape(d // P, P, f // P, P).transpose(2, 1, 0, 3)).reshape(f // P, P, d)
        if name == "L0_ffn_W2":
            a = a.reshape(-1, P, a.shape[1])
        if name == "L0_ffn_b1":
            a = np.ascontiguousarray(a.reshape(-1, P).T)
        arrays[f"in_{name}"] = a
        args.append(nc.dram_tensor(f"in_{name}", a.shape, mybir.dt.from_np(a.dtype), kind="ExternalInput").ap())
    for name, a in constants(inputs["x"].shape[1], inputs["x"].shape[2] // HEADS).items():
        arrays[f"in_{name}"] = a
        args.append(nc.dram_tensor(f"in_{name}", a.shape, F32, kind="ExternalInput").ap())
    out = nc.dram_tensor("out", inputs["x"].shape, F32, kind="ExternalOutput").ap()
    perceiver_layer(nc, *args, out, stop_after=STOP)
    r = run_bass_kernel_spmd(nc, [arrays], core_ids=[0])
    return r.results[0]["out"]
```

```python
from contextlib import ExitStack

import numpy as np

import concourse.bass as bass
from concourse import mybir

F32 = mybir.dt.float32
F32R = mybir.dt.float32r
U8 = mybir.dt.uint8
ALU = mybir.AluOpType
ACT = mybir.ActivationFunctionType
AX_X = mybir.AxisListType.X

P = 128
HEADS = 16
BIG = 1.0e30
LN_EPS = 1e-5


class Map:

    def __init__(self, nc, start):
        self.nc, self.at = nc, (start + 63) // 64 * 64

    def __call__(self, name, shape, dt):
        size = 1 if dt == U8 else 4
        for n in shape[1:]:
            size *= n
        t = self.nc.alloc_sbuf_tensor_at(name, shape, dt, offset=self.at)
        self.at += (size + 63) // 64 * 64
        return t


def perceiver_layer(nc, x, ctxT, mask, wq, wk, wv, wo, aq, ak, av, ao, router, w1, b1, w2, b2,
                    cos_tab, sin_tab, causal, same_in, before_in, slot_in, out):
    B, SQ, D = x.shape
    _, C, SK = ctxT.shape
    HD = D // HEADS
    DT, CT, KT = D // P, C // P, SK // P
    G = B * SQ // P
    BPG = P // SQ
    CH = 4
    NCH = G // CH
    PAIRS = HEADS // 2
    SCALE = float(HD) ** -0.5
    xt = x.rearrange("b s d -> (b s) d").rearrange("(g p) d -> p g d", p=P)
    outt = out.rearrange("b s d -> (b s) d").rearrange("(g p) d -> p g d", p=P)

    stack = ExitStack()
    with stack:
        def sem(name):
            return stack.enter_context(nc.semaphore(name))

        s_stood = sem("stood")

        def settle(eng):
            eng.sem_inc(s_stood, 1)

        psum = stack.enter_context(nc.psum_tensor("psum", [P, 8, 512], F32))
        bank = [psum[:, i, :] for i in range(8)]

        def at_least(eng, sem, value):
            if not isinstance(value, int) or value > 0:
                eng.wait_ge(sem, value)

        always = Map(nc, nc.sbuf_base)
        tok = always("tok", [P, G, D], F32)
        ident = always("ident", [P, P], F32)
        epsb = always("epsb", [P, 1], F32)
        stats = always("stats", [P, CH, 6], F32)
        mv = always("mv", [P, CH, 2], F32)
        rstd = always("rstd", [P, CH], F32)
        st1, mv1 = always("st1", [P, 6], F32), always("mv1", [P, 1, 2], F32)
        mv3, rs3 = always("mv3", [P, G, 2], F32), always("rs3", [P, G], F32)
        base = always.at

        m = Map(nc, base)
        wk_h, wk_l = m("wk_h", [P, CT, D], F32R), m("wk_l", [P, CT, D], F32R)
        wv_h, wv_l = m("wv_h", [P, CT, D], F32R), m("wv_l", [P, CT, D], F32R)
        wo_at = m.at
        wo_h, wo_l = m("wo_h", [P, DT, D], F32R), m("wo_l", [P, DT, D], F32R)
        after_xw = m.at
        wq_r = m("wq_r", [P, DT, D], F32)
        wq_h, wq_l = m("wq_h", [P, DT, D], F32R), m("wq_l", [P, DT, D], F32R)
        wk_r, wv_r = m("wk_r", [P, CT, D], F32), m("wv_r", [P, CT, D], F32)
        wo_r = m("wo_r", [P, DT, D], F32)
        xn = m("xn", [P, CH, D], F32)
        xnT_h, xnT_l = m("xnT_h", [P, DT, CH * P], F32R), m("xnT_l", [P, DT, CH * P], F32R)

        end1 = m.at

        s_w = [sem(f"p1_wq{k}") for k in range(DT)]
        s_wkv = [sem(f"p1_w{i}") for i in range(3)]
        s_x0 = [sem(f"p1_x0_{t}") for t in range(CH)]
        s_x = [sem(f"p1_x{i}") for i in range(NCH)]
        s_id = sem("p1_id")
        s_eps = sem("p1_eps")
        s_st, s_var, s_sd, s_rs, s_xn = sem("p1_st"), sem("p1_var"), sem("p1_sd"), sem("p1_rs"), sem("p1_xn")
        s_tr, s_hi, s_lo, s_q, s_qe = sem("p1_tr"), sem("p1_hi"), sem("p1_lo"), sem("p1_q"), sem("p1_qe")
        s_wh, s_wl = sem("p1_wh"), sem("p1_wl")
        s_pw = sem("p1_pw")


        m = Map(nc, after_xw)
        xres = m("xres", [P, 1, D], F32)
        KK = m("KK", [P, PAIRS, SK], F32R)
        V_h, V_l = m("V_h", [P, 2, KT, D], F32R), m("V_l", [P, 2, KT, D], F32R)
        prob = m("prob", [P, 2, SK], F32)
        PT_h, PT_l = m("PT_h", [P, 2, KT, 2, P], F32R), m("PT_l", [P, 2, KT, 2, P], F32R)
        PT_end = m.at
        OT_h, OT_l = m("OT_h", [P, DT, BPG, SQ], F32R), m("OT_l", [P, DT, BPG, SQ], F32R)
        mx, nmx = m("mx", [P, 4], F32), m("nmx", [P, 4], F32)
        rsum, rinv = m("rsum", [P, 4], F32), m("rinv", [P, 4], F32)
        assert m.at >= end1, (m.at, end1)
        qz_h, qz_l = m("qz_h", [P, DT, 2, 2, SQ], F32R), m("qz_l", [P, DT, 2, 2, SQ], F32R)
        mask8 = m("mask8", [P, BPG, SK], U8)
        mbias = m("mbias", [P, BPG, SK], F32)
        ctx_at = m.at
        ctx_r = m("ctx_r", [P, CT, SK], F32)
        ctx_h, ctx_l = m("ctx_h", [P, 2, CT, SK], F32R), m("ctx_l", [P, 2, CT, SK], F32R)
        ctx_end = m.at
        assert m.at <= nc.sbuf_usable_end, m.at

        s_raw = sem("p2_ctx")
        s_mraw = [sem(f"p2_mask{i}") for i in range(BPG)]
        s_xr = sem("p2_xres")
        s_z = sem("p2_zero")
        s_cx = sem("p2_cx")
        s_qz = sem("p2_qz")
        s_qd = sem("p2_qd")
        s_mb = sem("p2_mb")
        s_S, s_KV, s_T, s_PV, s_Wo = sem("p2_S"), sem("p2_KV"), sem("p2_T"), sem("p2_PV"), sem("p2_Wo")
        s_mx, s_nm, s_ex, s_ri, s_pn = sem("p2_mx"), sem("p2_nm"), sem("p2_ex"), sem("p2_ri"), sem("p2_pn")
        s_Th, s_Tl, s_KVh, s_KVl = sem("p2_Th"), sem("p2_Tl"), sem("p2_KVh"), sem("p2_KVl")
        s_Oh, s_Ol = sem("p2_Oh"), sem("p2_Ol")
        s_x1 = sem("p2_x1")
        S_bank, KV_bank, T_bank, PV_bank, Wo_bank = bank[0:2], bank[2:5], bank[5], bank[6], bank[7]

        SPT = BPG * PAIRS
        AHEAD = 6
        TILES = KT + DT
        KV_ORDER = [(kind, t) for t in range(DT) for kind in "KV"]
        GROUPS = BPG * DT
        UPPER, LOWER = slice(0, P // 2), slice(P // 2, P)
        PRODUCTS = 3

        def group(j, lag):
            n = (j - lag) // 2
            return n, n % DT, (n % GROUPS) // DT

        def kv_bank(k):
            return KV_bank[1 if k % SPT == SPT - 1 else k % SPT % 3]

        def high_parts(k):
            kind, t = KV_ORDER[k % TILES]
            if kind == "V":
                return [(slice(0, P), V_h[:, (k // TILES) % 2, t, :])]
            return [(UPPER, KK[UPPER, 2 * t, :]), (LOWER, KK[LOWER, 2 * t + 1, :])]

        def low_parts(k):
            kind, t = KV_ORDER[k % TILES]
            if kind == "V":
                return [V_l[:, (k // TILES) % 2, t, :]]
            return [KK[LOWER, 2 * t, :], KK[UPPER, 2 * t + 1, :]]

        def pt_half(j, low):
            return (PT_l if low else PT_h)[:, (j // 2) % 2, :, j % 2, :]

        def heads_of(psum, r):
            return psum[r * HD:(r + 1) * HD, r * SQ:(r + 1) * SQ]

        def pe_kv(pe, g, k, first):
            b, t = k // TILES, KV_ORDER[k % TILES][1]
            if k % TILES == 0:
                pe.wait_ge(s_cx, g * (2 * BPG) + 2 * b + 2)
            last_use = 2 if k % SPT in (1, SPT - 1) else 4 if k % SPT == 0 else 3
            if not (first and k < 3):
                pe.wait_ge(s_KVl, g * SPT + (k - last_use + 1))
            for c in range(CT):
                if KV_ORDER[k % TILES][0] == "K":
                    parts = ((wk_h, ctx_h), (wk_l, ctx_h), (wk_h, ctx_l))
                    ops = [(w[:, c, t * P:(t + 1) * P], y[:, b % 2, c, :]) for w, y in parts]
                else:
                    parts = ((ctx_h, wv_h), (ctx_h, wv_l), (ctx_l, wv_h))
                    ops = [(y[:, b % 2, c, t * P:(t + 1) * P], w[:, c, :]) for y, w in parts]
                for i, (stat, mov) in enumerate(ops):
                    ins = pe.matmul(kv_bank(k)[:], stat, mov, start=(c == 0 and i == 0),
                                    stop=(c == CT - 1 and i == PRODUCTS - 1))
            ins.then_inc(s_KV, 1)

        def pe_slot(pe, g, j, first=False, last=False, tail=False):
            s = g * SPT + j
            b, p = j // PAIRS, j % PAIRS
            if not tail:
                if p % 4 == 0:
                    pe.wait_ge(s_qz, g * (BPG * 16) + b * 16 + (p // 4 + 1) * 8)
                    pe.wait_ge(s_qd, g * SPT + j + 4)
                if p % 2 == 0:
                    pe.wait_ge(s_KVl, g * SPT + b * TILES + p + 1)
                if not (first and j < 2):
                    pe.wait_ge(s_mx, s - 1)
                for q in (qz_h, qz_l):
                    ins = pe.matmul(S_bank[j % 2][:], q[:, p // 2, p % 2, :, :].rearrange("p a b -> p (a b)"),
                                    KK[:, p, :], start=(q is qz_h), stop=(q is qz_l))
                ins.then_inc(s_S, 1)
                if not (last and j + AHEAD >= SPT):
                    pe_kv(pe, g, j + AHEAD, first)
            if j == 3 and not first:
                pe.wait_ge(s_Ol, g * (4 * GROUPS))
                pe.wait_ge(s_x1, g)
                for n in range(DT):
                    for i, (o, w) in enumerate(((OT_h, wo_h), (OT_l, wo_h), (OT_h, wo_l))):
                        ins = pe.matmul(Wo_bank[:], o[:, n, :, :].rearrange("p a b -> p (a b)"), w[:, n, :],
                                        start=(n == 0 and i == 0), stop=(n == DT - 1 and i == PRODUCTS - 1))
                ins.then_inc(s_Wo, 1)
            if not (first and j == 0) and not (tail and j > 0):
                pe.wait_ge(s_pn, s)
                if not (first and j == 1):
                    pe.wait_ge(s_Tl, s - 1)
                for kt in range(KT):
                    ins = pe.transpose(T_bank[:, kt * P:(kt + 1) * P],
                                       prob[:, (j - 1) % 2, kt * P:(kt + 1) * P], ident[:])
                ins.then_inc(s_T, 1)
            if j % 2 == 1 and not (first and j == 1) and not (tail and j > 1):
                n, quarter, odd = group(j, 3)
                pe.wait_ge(s_Tl, s - 1)
                if j % PAIRS == 3:
                    pe.wait_ge(s_KVl, g * SPT + (j // PAIRS + 1) * TILES)
                if not (first and n == 0):
                    pe.wait_ge(s_Ol, g * (4 * GROUPS) + 4 * n)
                for kt in range(KT):
                    for i, (v, t) in enumerate(((V_h, PT_h), (V_h, PT_l), (V_l, PT_h))):
                        ins = pe.matmul(PV_bank[:, 0:2 * P], v[:, odd, kt, quarter * P:(quarter + 1) * P],
                                        t[:, n % 2, kt, :, :].rearrange("p a b -> p (a b)"),
                                        start=(kt == 0 and i == 0), stop=(kt == KT - 1 and i == PRODUCTS - 1))
                ins.then_inc(s_PV, 1)

        def act_kv(act, g, k):
            act.wait_ge(s_KV, g * SPT + k + 1)
            for rows, place in high_parts(k):
                ins = act.activation(place, kv_bank(k)[rows, :], ACT.Copy)
            ins.then_inc(s_KVh, 1)

        def dve_kv(dve, g, k):
            dve.wait_ge(s_KVh, g * SPT + k + 1)
            for (rows, high), low in zip(high_parts(k), low_parts(k)):
                ins = dve.tensor_tensor(low, kv_bank(k)[rows, :], high.bitcast(F32), ALU.subtract)
            ins.then_inc(s_KVl, 1)

        def dve_q(dve, g, half, heads):
            b, t = half // 2, slice(2 * (half % 2), 2 * (half % 2) + 2)
            qt = tok[:, bass.ds(g, 1), :].rearrange("p a (n b q) -> p (a n) b q", n=DT, b=BPG)
            for r in heads:
                rows, other = slice(r * HD, (r + 1) * HD), slice((r + 2) % 4 * HD, ((r + 2) % 4 + 1) * HD)
                dve.tensor_copy(qz_h[other, t, r // 2, r % 2, :], qt[rows, t, b, :]).then_inc(s_qd, 1)

        def act_slot(act, g, j, first=False, last=False, tail=False):
            s = g * SPT + j
            if not (first and j < 2) and not (tail and j > 1):
                act.wait_ge(s_T, s - 1)
                if not (first and j < 6):
                    act.wait_ge(s_PV, g * GROUPS + (j - 2) // 2 - 1)
                act.activation(pt_half(j - 2, False), T_bank[:].rearrange("p (k n) -> p k n", k=KT),
                               ACT.Copy).then_inc(s_Th, 1)
            if j % 2 == 0 and not (first and j < 4) and not (tail and j > 2):
                n, quarter, odd = group(j, 4)
                act.wait_ge(s_PV, g * GROUPS + n + 1)
                if n == 0 and not first:
                    act.wait_ge(s_Wo, g)
                for r in range(4):
                    act.activation(OT_h[r * HD:(r + 1) * HD, quarter, odd, :], heads_of(PV_bank, r),
                                   ACT.Copy).then_inc(s_Oh, 1)
            if tail:
                return
            if not (last and j - 1 + AHEAD >= SPT) and not (first and j == 0):
                act_kv(act, g, j - 1 + AHEAD)
            c = slice(j % 4, j % 4 + 1)
            act.wait_ge(s_nm, s + 1)
            act.activation(prob[:, j % 2, :], prob[:, j % 2, :], ACT.Exp, bias=nmx[:, c], scale=SCALE,
                           accum_out=rsum[:, c]).then_inc(s_ex, 1)
            act.wait_ge(s_ri, s + 1)
            act.activation(prob[:, j % 2, :], prob[:, j % 2, :], ACT.Copy, scale=rinv[:, c]).then_inc(s_pn, 1)

        def dve_stats(dve, g):
            dve.wait_ge(s_x1, g + 1)
            settle(dve)
            dve.bn_stats(st1[:], tok[:, bass.ds(g - 1, 1), :].rearrange("p a n -> p (a n)")).then_inc(s3_st, 1)
            dve.wait_ge(s3_st, g)
            settle(dve)
            dve.bn_aggr(mv1[:, 0, :], st1[:]).then_inc(s3_ag, 1)
            dve.wait_ge(s3_ag, g)
            dve.tensor_copy(mv3[:, bass.ds(g - 1, 1), :], mv1[:]).then_inc(s3_mv, 1)

        def layer_norm(dve, t):
            at_least(dve, s3_xn, t)
            dve.tensor_copy(cur[:, 0:2], mv3[:, bass.ds(t, 1), :].rearrange("p a b -> p (a b)"))
            dve.tensor_copy(cur[:, 2:3], rs3[:, bass.ds(t, 1)]).then_inc(s3_cu, 1)
            dve.wait_ge(s3_cu, t + 1)
            dve.tensor_scalar(xn3[:], tok[:, bass.ds(t, 1), :].rearrange("p a n -> p (a n)"), cur[:, 0:1],
                              cur[:, 2:3], ALU.subtract, ALU.mult).then_inc(s3_xn, 1)

        def dve_slot(dve, g, j, first=False, last=False, tail=False):
            s = g * SPT + j
            c = slice(j % 4, j % 4 + 1)
            if not tail:
                dve.wait_ge(s_S, s + 1)
                if not (first and j < 2):
                    dve.wait_ge(s_T, s - 1)
                if j % PAIRS == 0:
                    dve.wait_ge(s_mb, g * BPG + j // PAIRS + 1)
                settle(dve)
                dve.tensor_tensor_reduce(prob[:, j % 2, :], S_bank[j % 2][:], mbias[:, j // PAIRS, :], 1.0,
                                         -3.0e38, ALU.add, ALU.max, mx[:, c]).then_inc(s_mx, 1)
                dve.wait_ge(s_mx, s + 1)
                dve.tensor_scalar(nmx[:, c], mx[:, c], -SCALE, None, ALU.mult).then_inc(s_nm, 1)
            if not (first and j < 2) and not (tail and j > 1):
                dve.wait_ge(s_Th, s - 1)
                dve.tensor_tensor(pt_half(j - 2, True), T_bank[:].rearrange("p (k n) -> p k n", k=KT),
                                  pt_half(j - 2, False).bitcast(F32), ALU.subtract).then_inc(s_Tl, 1)
            if j % 2 == 0 and not (first and j < 4) and not (tail and j > 2):
                n, quarter, odd = group(j, 4)
                dve.wait_ge(s_Oh, g * (4 * GROUPS) + 4 * n + 4)
                for r in range(4):
                    rows = slice(r * HD, (r + 1) * HD)
                    dve.tensor_tensor(OT_l[rows, quarter, odd, :], heads_of(PV_bank, r),
                                      OT_h[rows, quarter, odd, :].bitcast(F32), ALU.subtract).then_inc(s_Ol, 1)
            if j == 5 and not first:
                dve.wait_ge(s_Wo, g)
                dve.wait_ge(s_xr, g * 16)
                dve.tensor_tensor(tok[:, bass.ds(g - 1, 1), :], Wo_bank[:].rearrange("p (a n) -> p a n", a=1),
                                  xres[:], ALU.add).then_inc(s_x1, 1)
            if tail:
                return
            dve.wait_ge(s_ex, s + 1)
            dve.reciprocal(rinv[:, c], rsum[:, c]).then_inc(s_ri, 1)
            if not (last and j - 1 + AHEAD >= SPT) and not (first and j == 0):
                dve_kv(dve, g, j - 1 + AHEAD)
            if j == 11 and not first:
                dve_stats(dve, g)
            if j % 4 < 3 and not (last and j >= SPT - 4):
                half = (j // 4 + 1) % 4
                dve_q(dve, g if half else g + 1, half, ((0,), (1, 2), (3,))[j % 4])

        def sp_contexts(sp, g, first):
            for b in range(BPG):
                n = g * BPG + b
                if not (first and b == 0):
                    sp.wait_ge(s_cx, n * 2)
                settle(sp)
                sp.dma_start(ctx_r[:], ctxT[bass.ds(n, 1), :, :].rearrange("a (t p) n -> p (a t) n", p=P))\
                    .then_inc(s_raw, 16)
                if not first:
                    sp.wait_ge(s_mb, n - 1)
                settle(sp)
                sp.dma_start(mask8[:, b, :], mask[bass.ds(n, 1), :].broadcast_to([P, SK])).then_inc(s_mraw[b], 16)

        def sp_tile(sp, g, first):
            if not first:
                sp_contexts(sp, g, first)
                sp.wait_ge(s_x1, g + 1)
            settle(sp)
            sp.dma_start(xres[:], xt[:, bass.ds(g, 1), :]).then_inc(s_xr, 16)

        def pool_ctx(pool, g, b, first):
            n = g * BPG + b
            pool.wait_ge(s_raw, n * 16 + 16)
            if not (first and b == 0):
                pool.wait_ge(s_qz, (n - 1) * 16 + 8)
            if not (first and b < 2):
                pool.wait_ge(s_KV, (n - 1) * TILES)
            settle(pool)
            pool.tensor_scalar(ctx_h[:, b % 2, :, :], ctx_r[:], 1.0, None, ALU.mult).then_inc(s_cx, 1)
            pool.wait_ge(s_cx, n * 2 + 1)
            settle(pool)
            pool.tensor_tensor(ctx_l[:, b % 2, :, :], ctx_r[:], ctx_h[:, b % 2, :, :].bitcast(F32),
                               ALU.subtract).then_inc(s_cx, 1)

        def pool_q(pool, g, b, half, first, last):
            n = g * BPG + b
            if not (first and b == 0):
                pool.wait_ge(s_S, n * PAIRS - 4 + 4 * half)
            qt = tok[:, bass.ds(g, 1), :].rearrange("p a (n b q) -> p (a n) b q", n=DT, b=BPG)
            t = slice(2 * half, 2 * half + 2)
            for low in (0, 1):
                for r in range(4):
                    rows = slice(r * HD, (r + 1) * HD)
                    src, dst = qt[rows, t, b, :], qz_h[rows, t, r // 2, r % 2, :]
                    if low or r:
                        pool.wait_ge(s_qz, n * 16 + half * 8 + 4 * low + r)
                    elif half == 0:
                        pool.wait_ge(s_mb, n + 1)
                    elif not last or b < BPG - 1:
                        pool.wait_ge(s_cx, n * 2 + 4)
                    settle(pool)
                    if low:
                        ins = pool.tensor_tensor(qz_l[rows, t, r // 2, r % 2, :], src, dst.bitcast(F32), ALU.subtract)
                    else:
                        ins = pool.tensor_copy(dst, src)
                    ins.then_inc(s_qz, 1)

        def pool_mask(pool, g, b, first):
            n = g * BPG + b
            pool.wait_ge(s_mraw[b], g * 16 + 16)
            if not first:
                pool.wait_ge(s_mx, (n - 1) * PAIRS)
            if not (first and b == 0):
                pool.wait_ge(s_qz, n * 16)
            settle(pool)
            pool.tensor_scalar(mbias[:, b, :], mask8[:, b, :], -1.0, BIG, ALU.add, ALU.mult).then_inc(s_mb, 1)

        def pool_tile(pool, g, first=False, last=False):
            for b in range(BPG):
                if not (first and b == 0):
                    pool_mask(pool, g, b, first)
                    pool_q(pool, g, b, 0, first, last)
                if not (last and b == BPG - 1):
                    pool_ctx(pool, g, b + 1, first)
                pool_q(pool, g, b, 1, first, last)

        def tiles(eng, tile):
            tile(0, True, False)
            with eng.Fori(1, G - 1) as g:
                tile(g, False, False)
            tile(G - 1, False, True)

        m = Map(nc, base)
        raw3 = m("raw3", [P, 3, DT, D], F32)
        assert m.at <= wo_at
        m = Map(nc, ctx_at)
        qw_h, qw_l = m("aq_h", [P, DT, D], F32R), m("aq_l", [P, DT, D], F32R)
        kw_h = m("ak_h", [P, DT, D], F32R)
        rope = m("rope", [P, 2, HD], F32)
        cmask = m("cmask", [P, SQ], F32)
        assert m.at <= ctx_end
        s3_w = [sem(f"p3_w{i}") for i in range(4)]
        s3_c = sem("p3_const")
        s3_ws = sem("p3_ws")
        s3_st, s3_ag, s3_mv = sem("p3_st"), sem("p3_ag"), sem("p3_mv")
        s3_sd, s3_rs, s3_cu, s3_xn = sem("p3_sd"), sem("p3_rs"), sem("p3_cu"), sem("p3_xn")
        xn_at = PT_end - 4 * (D + 16)
        m = Map(nc, xn_at)
        cur = m("cur", [P, 3], F32)
        xn3 = m("xn3", [P, D], F32)
        xn_end = m.at
        assert m.at <= PT_end

        with nc.Block() as block:
            @block.sync
            def _(sp):
                for t in range(CH):
                    sp.dma_start(tok[:, t, :], xt[:, t, :]).then_inc(s_x0[t], 16)
                for c in range(1, NCH):
                    sp.dma_start(tok[:, c * CH:(c + 1) * CH, :], xt[:, c * CH:(c + 1) * CH, :]).then_inc(s_x[c], 16)
                for i, (r, w) in enumerate(((wk_r, wk), (wv_r, wv), (wo_r, wo))):
                    sp.dma_start(r[:], w.rearrange("(t p) n -> p t n", p=P)).then_inc(s_wkv[i], 16)
                sp_contexts(sp, 0, True)

            @block.gpsimd
            def _(pool):
                pool.memset(ident[:], 0.0).then_inc(s_id, 1)
                pool.memset(epsb[:], LN_EPS).then_inc(s_eps, 1)
                pool.wait_ge(s_id, 1)
                pool.affine_select(out=ident[:], in_=ident[:], compare_op=ALU.not_equal, fill=1.0, base=0,
                                   pattern=[[-1, P]], channel_multiplier=1).then_inc(s_id, 1)
                pool.memset(qz_h[:].bitcast(F32), 0.0).then_inc(s_z, 1)
                pool.memset(qz_l[:].bitcast(F32), 0.0).then_inc(s_z, 1)

                def split(i, r, h, l):
                    pool.wait_ge(s_wkv[i], 16)
                    pool.tensor_scalar(h[:], r[:], 1.0, None, ALU.mult).then_inc(s_pw, 1)
                    pool.wait_ge(s_pw, 2 * i + 1)
                    pool.tensor_tensor(l[:], r[:], h[:].bitcast(F32), ALU.subtract).then_inc(s_pw, 1)
                    pool.wait_ge(s_pw, 2 * i + 2)

                split(0, wk_r, wk_h, wk_l)
                split(1, wv_r, wv_h, wv_l)
                pool_ctx(pool, 0, 0, True)
                pool.wait_ge(s_cx, 2)
                pool_mask(pool, 0, 0, True)
                split(2, wo_r, wo_h, wo_l)
                pool.wait_ge(s_z, 2)
                pool.wait_ge(s_qe, DT)
                pool_q(pool, 0, 0, 0, True, False)

            @block.vector
            def _(dve):
                def deviations(c):
                    for t in range(CH):
                        dve.wait_ge(s_x[c] if c else s_x0[t], 16)
                        dve.bn_stats(stats[:, t, :], tok[:, c * CH + t, :]).then_inc(s_st, 1)
                    if c >= 1:
                        dve.wait_ge(s_xn, CH * c)
                    for t in range(CH):
                        dve.wait_ge(s_st, CH * c + t + 1)
                        dve.bn_aggr(mv[:, t, :], stats[:, t, :]).then_inc(s_var, 1)
                    dve.wait_ge(s_sd, c + 1)
                    dve.reciprocal(rstd[:], rstd[:]).then_inc(s_rs, 1)
                    dve.wait_ge(s_rs, c + 1)

                def normalize(c):
                    if c >= 1:
                        dve.wait_ge(s_tr, DT * c)
                    for t in range(CH):
                        dve.tensor_scalar(xn[:, t, :], tok[:, c * CH + t, :], mv[:, t, 0:1], rstd[:, t:t + 1],
                                          ALU.subtract, ALU.mult).then_inc(s_xn, 1)

                def low(c, k):
                    dve.wait_ge(s_hi, DT * c + k + 1)
                    dve.tensor_tensor(xnT_l[:, k, :], bank[k][:], xnT_h[:, k, :].bitcast(F32),
                                      ALU.subtract).then_inc(s_lo, 1)

                deviations(0)
                normalize(0)
                for k in range(DT):
                    dve.wait_ge(s_wh, k + 1)
                    dve.tensor_tensor(wq_l[:, k, :], wq_r[:, k, :], wq_h[:, k, :].bitcast(F32),
                                      ALU.subtract).then_inc(s_wl, 1)
                    low(0, k)
                deviations(1)
                normalize(1)
                for c in range(1, NCH):
                    low(c, 0)
                    low(c, 1)
                    if c + 1 < NCH:
                        deviations(c + 1)
                        normalize(c + 1)
                    low(c, 2)
                    low(c, 3)
                dve.wait_ge(s_qe, DT)
                dve.wait_ge(s_z, 1)
                dve_q(dve, 0, 0, range(4))

            @block.scalar
            def _(act):
                for k in range(DT):
                    act.dma_start(wq_r[:, k, :], wq[k * P:(k + 1) * P, :]).then_inc(s_w[k], 16)
                act.wait_ge(s_eps, 1)

                def deviation(c):
                    act.wait_ge(s_var, CH * (c + 1))
                    act.activation(rstd[:], mv[:, :, 1], ACT.Sqrt, bias=epsb[:]).then_inc(s_sd, 1)

                def high(c, k):
                    act.wait_ge(s_tr, DT * c + k + 1)
                    if c >= 1:
                        act.wait_ge(s_q, DT * (c - 1) + k + 1)
                    act.activation(xnT_h[:, k, :], bank[k][:], ACT.Copy).then_inc(s_hi, 1)

                deviation(0)
                for k in range(DT):
                    act.wait_ge(s_w[k], 16)
                    act.activation(wq_h[:, k, :], wq_r[:, k, :], ACT.Copy).then_inc(s_wh, 1)
                for k in range(DT):
                    high(0, k)
                deviation(1)
                for c in range(NCH):
                    if c + 1 < NCH:
                        high(c + 1, 0)
                        high(c + 1, 1)
                    if c + 2 < NCH:
                        deviation(c + 2)
                    act.wait_ge(s_q, DT * (c + 1))
                    for mt in range(DT):
                        act.activation(
                            tok[:, c * CH:(c + 1) * CH, mt * P:(mt + 1) * P],
                            bank[4 + mt][:].rearrange("p (t n) -> p t n", t=CH), ACT.Copy).then_inc(s_qe, 1)
                    if c + 1 < NCH:
                        high(c + 1, 2)
                        high(c + 1, 3)
                act.wait_ge(s_qe, DT * NCH)

            @block.tensor
            def _(pe):
                def transpose(c, k):
                    pe.wait_ge(s_xn, CH * (c + 1))
                    if c >= 1:
                        pe.wait_ge(s_lo, DT * (c - 1) + k + 1)
                    for t in range(CH):
                        ins = pe.transpose(bank[k][:, t * P:(t + 1) * P], xn[:, t, k * P:(k + 1) * P], ident[:])
                    ins.then_inc(s_tr, 1)

                pe.wait_ge(s_id, 2)
                for k in range(DT):
                    transpose(0, k)
                for c in range(NCH):
                    for k in range(DT):
                        if c == 0:
                            pe.wait_ge(s_wl, k + 1)
                        pe.wait_ge(s_lo, DT * c + k + 1)
                        for mt in range(DT):
                            if c >= 1 and k == 0:
                                pe.wait_ge(s_qe, DT * (c - 1) + mt + 1)
                            for w, y in ((wq_h, xnT_h), (wq_h, xnT_l), (wq_l, xnT_h)):
                                ins = pe.matmul(bank[4 + mt][:], w[:, k, mt * P:(mt + 1) * P], y[:, k, :],
                                                start=(k == 0 and w is wq_h and y is xnT_h),
                                                stop=(k == DT - 1 and w is wq_l))
                        ins.then_inc(s_q, 1)
                        if c + 1 < NCH and k >= 1:
                            transpose(c + 1, k - 1)
                    if c + 1 < NCH:
                        transpose(c + 1, DT - 1)
                pe.wait_ge(s_pw, 4)
                pe_kv(pe, 0, 0, True)
                pe_kv(pe, 0, 1, True)

        with nc.Block() as block:
            @block.sync
            def _(sp):
                tiles(sp, lambda g, first, last: sp_tile(sp, g, first))
                sp.wait_ge(s_KV, B * TILES)
                for i, w in enumerate((aq, ak, av)):
                    sp.dma_start(raw3[:, i], w.rearrange("(t p) n -> p t n", p=P)).then_inc(s3_w[i], 16)
                for i in range(BPG):
                    rows = slice(i * SQ, (i + 1) * SQ)
                    sp.dma_start(rope[rows, 0, :], cos_tab).then_inc(s3_c, 16)
                    sp.dma_start(rope[rows, 1, :], sin_tab).then_inc(s3_c, 16)
                    sp.dma_start(cmask[rows, :], causal).then_inc(s3_c, 16)

            @block.gpsimd
            def _(pool):
                tiles(pool, lambda g, first, last: pool_tile(pool, g, first, last))
                pool.wait_ge(s_KV, B * TILES)
                pool.wait_ge(s_qz, B * 16)
                pool.wait_ge(s3_w[0], 16)
                pool.tensor_scalar(qw_h[:], raw3[:, 0], 1.0, None, ALU.mult).then_inc(s3_ws, 1)
                pool.wait_ge(s3_ws, 1)
                pool.tensor_tensor(qw_l[:], raw3[:, 0], qw_h[:].bitcast(F32), ALU.subtract).then_inc(s3_ws, 1)
                pool.wait_ge(s3_w[1], 16)
                pool.wait_ge(s3_ws, 2)
                pool.tensor_scalar(kw_h[:], raw3[:, 1], 1.0, None, ALU.mult).then_inc(s3_ws, 1)

            @block.tensor
            def _(pe):
                def tile(g, first, last):
                    for j in range(SPT):
                        pe_slot(pe, g, j, first, last)
                for k in range(2, AHEAD):
                    pe_kv(pe, 0, k, True)
                tiles(pe, tile)
                for j in range(4):
                    pe_slot(pe, G, j, tail=True)

            @block.scalar
            def _(act):
                def tile(g, first, last):
                    for j in range(SPT):
                        act_slot(act, g, j, first, last)
                for k in range(AHEAD):
                    act_kv(act, 0, k)
                tiles(act, tile)
                for j in range(4):
                    act_slot(act, G, j, tail=True)
                act.wait_ge(s3_mv, G - 1)
                act.activation(rs3[:, 0:G - 1], mv3[:, 0:G - 1, 1], ACT.Sqrt, bias=epsb[:]).then_inc(s3_sd, 1)

            @block.vector
            def _(dve):
                def tile(g, first, last):
                    for j in range(SPT):
                        dve_slot(dve, g, j, first, last)
                dve.sem_inc(s_x1, 1)
                for k in range(AHEAD):
                    dve_kv(dve, 0, k)
                tiles(dve, tile)
                for j in range(6):
                    if j == 5:
                        dve.wait_ge(s3_sd, 1)
                        dve.reciprocal(rs3[:, 0:G - 1], rs3[:, 0:G - 1]).then_inc(s3_rs, 1)
                        dve.wait_ge(s3_rs, 1)
                        dve.wait_ge(s_PV, G * GROUPS)
                        layer_norm(dve, 0)
                    dve_slot(dve, G, j, tail=True)

        KEEP = SQ // 2
        FF = w1.shape[0]
        ST = B * KEEP // P
        m = Map(nc, ctx_end)
        b1_sb, b2_sb = m("b1_sb", [P, FF], F32), m("b2_sb", [P, D], F32)
        router_sb = m("router_sb", [P, D], F32)
        ones = m("ones", [P, P], F32)
        same, before = m("same", [P, P], F32), m("before", [P, P], F32)
        slot_no = m("slot_no", [P, 2, P], F32)
        assert m.at <= nc.sbuf_usable_end, m.at
        s4_c, s4_on = sem("p4_const"), sem("p4_ones")
        nmr = m("nmr", [P, G], F32)
        s4_st, s4_ag, s4_mv = sem("p4_st"), sem("p4_ag"), sem("p4_mv")
        s4_sd, s4_rs, s4_nm = sem("p4_sd"), sem("p4_rs"), sem("p4_nm")

        m = Map(nc, wo_at)
        kw_l = m("ak_l", [P, DT, D], F32R)
        vw_h, vw_l = m("av_h", [P, DT, D], F32R), m("av_l", [P, DT, D], F32R)
        ow_r = m("ao_r", [P, DT, D], F32)
        ow_h, ow_l = m("ao_h", [P, DT, D], F32R), m("ao_l", [P, DT, D], F32R)
        qb = m("qb", [P, DT, BPG, 4, SQ], F32)
        pb_h = m("pb_h", [P, DT, BPG, 2, P], F32R)
        sm = m("sm", [P, 2, DT, 2, BPG, SQ], F32)
        x3_h, x3_l = m("x3_h", [P, 2, DT, P], F32R), m("x3_l", [P, 2, DT, P], F32R)
        k_T = m("k_T", [P, DT, P], F32)
        assert m.at <= xn_at, (m.at, xn_at)
        m = Map(nc, xn_end)
        v_h = m("v_h", [P, 2, D], F32R)
        r_cos, r_sin = m("r_cos", [P, D], F32), m("r_sin", [P, D], F32)
        q_r, k_r = m("q_r", [P, D], F32), m("k_r", [P, D], F32)
        mx3, rc3 = m("mx3", [P, HEADS], F32), m("rc3", [P, 2, HEADS], F32)
        o_h, o_l = m("o_h", [P, DT, BPG, SQ], F32R), m("o_l", [P, DT, BPG, SQ], F32R)
        assert m.at <= ctx_at, (m.at, ctx_at)

        m = Map(nc, base)
        pb_l, v_l = m("pb_l", [P, DT, BPG, 2, P], F32R), m("v_l", [P, 2, D], F32R)
        assert m.at <= wo_at

        s3_wa, s3_wd = sem("p3_wa"), sem("p3_wd")
        s3_z = sem("p3_z")
        s3_XT, s3_xh, s3_xl = sem("p3_XT"), sem("p3_xh"), sem("p3_xl")
        s3_Q, s3_K, s3_V, s3_Tq, s3_Tk = sem("p3_Q"), sem("p3_K"), sem("p3_V"), sem("p3_Tq"), sem("p3_Tk")
        s3_rq, s3_rk, s3_aq, s3_ak = sem("p3_rq"), sem("p3_rk"), sem("p3_aq"), sem("p3_ak")
        s3_vh, s3_v = sem("p3_vh"), sem("p3_v")
        s3_qa, s3_kT = sem("p3_qa"), sem("p3_kT")
        s3_S, s3_ms, s3_mx, s3_su, s3_ex = sem("p3_S"), sem("p3_ms"), sem("p3_mx"), sem("p3_su"), sem("p3_ex")
        s3_sm, s3_rc, s3_pn = sem("p3_sum"), sem("p3_rc"), sem("p3_pn")
        s3_PT, s3_pa, s3_pd = sem("p3_PT"), sem("p3_pa"), sem("p3_pd")
        s3_PV, s3_oa, s3_od, s3_Wo, s3_x = sem("p3_PV"), sem("p3_oa"), sem("p3_od"), sem("p3_Wo"), sem("p3_x")

        def has(t):
            return not isinstance(t, int) or 0 <= t < G

        def one_tile(t):
            return tok[:, bass.ds(t, 1), :].rearrange("p a n -> p (a n)")

        def project(pe, b, y_h, y_l, w_h, w_l):
            for k in range(DT):
                for i, (y, w) in enumerate(((y_h, w_h), (y_h, w_l), (y_l, w_h))):
                    ins = pe.matmul(b, y[:, k, :], w[:, k, :], start=(k == 0 and i == 0),
                                    stop=(k == DT - 1 and i == PRODUCTS - 1))
            return ins

        def pe3(pe, t, par):
            nxt = 1 - par
            if has(t):
                pe.wait_ge(s3_aq, t + 1)
                at_least(pe, s3_xl, t + 2 if not isinstance(t, int) else min(t + 2, G))
                for n in range(DT):
                    ins = pe.transpose(bank[0][:, n * P:(n + 1) * P], q_r[:, n * P:(n + 1) * P], ident[:])
                ins.then_inc(s3_Tq, 1)
                pe.wait_ge(s3_ak, t + 1)
                for n in range(DT):
                    ins = pe.transpose(bank[1][:, n * P:(n + 1) * P], k_r[:, n * P:(n + 1) * P], ident[:])
                ins.then_inc(s3_Tk, 1)
            if has(t + 1):
                at_least(pe, s3_xl, t + 2)
                at_least(pe, s3_v, t + 1)
                if isinstance(t, int) and t == -1:
                    pe.wait_ge(s3_ws, 2)
                project(pe, bank[2], x3_h[:, nxt, :, :], x3_l[:, nxt, :, :], qw_h, qw_l).then_inc(s3_Q, 1)
            if has(t):
                pe.wait_ge(s3_kT, t + 1)
                pe.wait_ge(s3_qa, 4 * t + 4)
                for n in range(DT):
                    if n < 2:
                        at_least(pe, s3_od, 8 * t - 8)
                    else:
                        pe.wait_ge(s3_ms, 4 * t + n - 1)
                    for b in range(BPG):
                        for pl in range(2):
                            at = pl * 2 * P + b * SQ
                            ins = pe.matmul(bank[4 + n % 2][:, at:at + P],
                                            qb[:, n, b, 2 * pl:2 * pl + 2, :].rearrange("p a b -> p (a b)"), k_T[:, n, :],
                                            start=True, stop=True)
                    ins.then_inc(s3_S, 1)
            if has(t + 1):
                at_least(pe, s3_x, t - 1)
                if isinstance(t, int) and t == -1:
                    pe.wait_ge(s3_ws, 3)
                    pe.wait_ge(s3_wd, 1)
                project(pe, bank[3], x3_h[:, nxt, :, :], x3_l[:, nxt, :, :], kw_h, kw_l).then_inc(s3_K, 1)
            if has(t - 1):
                pe.wait_ge(s3_pn, t)
                for h in range(2):
                    for i in range(4):
                        n, pl = 2 * h + i // 2, i % 2
                        ins = pe.transpose(bank[h][:, i * P:(i + 1) * P],
                                           sm[:, nxt, n, pl, :, :].rearrange("p b k -> p (b k)"), ident[:])
                    ins.then_inc(s3_PT, 1)
            if has(t + 1):
                pe.wait_ge(s3_rq, 2 * t + 4)
                if isinstance(t, int) and t == -1:
                    pe.wait_ge(s3_wa, 1)
                    pe.wait_ge(s3_wd, 2)
                project(pe, bank[2], x3_h[:, nxt, :, :], x3_l[:, nxt, :, :], vw_h, vw_l).then_inc(s3_V, 1)
            if has(t - 1):
                pe.wait_ge(s3_v, t)
                for n in range(DT):
                    if n % 2 == 0:
                        pe.wait_ge(s3_pd, 4 * t - 2 + n)
                    if n == 0:
                        at_least(pe, s3_od, 8 * (t - 1) - 4)
                    if n == 2 and has(t):
                        pe.wait_ge(s3_ms, 4 * t + 4)
                    for i, (v, p) in enumerate(((v_h, pb_h), (v_l, pb_h), (v_h, pb_l))):
                        ins = pe.matmul(bank[(6, 7, 4, 5)[n]], v[:, nxt, n * P:(n + 1) * P],
                                        p[:, n, :, :, :].rearrange("p a b c -> p (a b c)"),
                                        start=(i == 0), stop=(i == PRODUCTS - 1))
                    if n % 2:
                        ins.then_inc(s3_PV, 1)
            if has(t + 2):
                at_least(pe, s3_xn, t + 3)
                if has(t - 1):
                    pe.wait_ge(s3_pd, 4 * t)
                for k in range(DT):
                    ins = pe.transpose(bank[0][:, k * P:(k + 1) * P], xn3[:, k * P:(k + 1) * P], ident[:])
                ins.then_inc(s3_XT, 1)
            if has(t - 1):
                if has(t + 1):
                    pe.wait_ge(s3_rk, 2 * t + 4)
                if isinstance(t, int) and t == 1:
                    pe.wait_ge(s3_wd, 3)
                for n in range(DT):
                    if n % 2 == 0:
                        pe.wait_ge(s3_od, 8 * t - 4 + 2 * n)
                    for i, (o, w) in enumerate(((o_h, ow_h), (o_h, ow_l), (o_l, ow_h))):
                        ins = pe.matmul(bank[3], o[:, n, :, :].rearrange("p b q -> p (b q)"), w[:, n, :],
                                        start=(n == 0 and i == 0), stop=(n == DT - 1 and i == PRODUCTS - 1))
                ins.then_inc(s3_Wo, 1)

        def head_rows(r):
            return slice(r * HD, (r + 1) * HD)

        def q_blocks(eng_copy, r):
            return eng_copy(qb[head_rows(r), :, :, r, :],
                            bank[0][head_rows(r), :].rearrange("p (n b q) -> p n b q", n=DT, b=BPG))

        def o_block(pair, r):
            src = (psum[:, 6:8, :] if pair == 0 else psum[:, 4:6, :])[head_rows(r), :, :]
            src = src.rearrange("p n (b h q) -> p n b h q", b=BPG, h=4)[:, :, :, r, :]
            quarters = slice(2 * pair, 2 * pair + 2)
            return src, o_h[head_rows(r), quarters, :, :], o_l[head_rows(r), quarters, :, :]

        def p_block(h, b):
            rows, heads = slice(b * SQ, (b + 1) * SQ), slice(2 * h, 2 * h + 2)
            return (bank[h][rows, :].rearrange("p (n l c) -> p n l c", n=2, l=2),
                    pb_h[rows, heads, b, :, :], pb_l[rows, heads, b, :, :])

        def act3(act, t, par):
            nxt = 1 - par
            copy = lambda o, i: act.activation(o, i, ACT.Copy)
            if has(t):
                act.wait_ge(s3_Tq, t + 1)
                at_least(act, s3_S, 4 * t)
                for r in range(4):
                    q_blocks(copy, r).then_inc(s3_qa, 1)
                act.wait_ge(s3_Tk, t + 1)
                copy(k_T[:].rearrange("p n c -> p (n c)"), bank[1]).then_inc(s3_kT, 1)
            if has(t - 1):
                at_least(act, s3_PV, 2 * t - 2)
                for h in range(2):
                    act.wait_ge(s3_PT, 2 * t - 1 + h)
                    for b in range(BPG):
                        src, high, _ = p_block(h, b)
                        copy(high, src).then_inc(s3_pa, 1)
            if has(t):
                act.wait_ge(s3_su, t + 1)
                s_ = sm[:, par].rearrange("p a b c d -> p (a b c d)")
                act.activation(s_, s_, ACT.Exp).then_inc(s3_ex, 1)
            if has(t - 1):
                at_least(act, s3_Wo, t - 1)
                for pair in range(2):
                    act.wait_ge(s3_PV, 2 * t - 1 + pair)
                    for r in range(4):
                        src, high, _ = o_block(pair, r)
                        copy(high, src).then_inc(s3_oa, 1)
            if has(t + 2):
                act.wait_ge(s3_XT, t + 3)
                at_least(act, s3_V, t + 1)
                copy(x3_h[:, par].rearrange("p n c -> p (n c)"), bank[0]).then_inc(s3_xh, 1)
            if has(t + 1):
                act.wait_ge(s3_V, t + 2)
                if isinstance(t, int) and t == 0:
                    act.wait_ge(s3_w[3], 16)
                    copy(ow_h[:], ow_r[:]).then_inc(s3_wa, 1)
                at_least(act, s3_PV, 2 * t)
                copy(v_h[:, nxt, :], bank[2]).then_inc(s3_vh, 1)

        def rotate_parts(dve, psum_bank, done, pool_sem, pool_count):
            at_least(dve, pool_sem, pool_count)
            p4 = psum_bank.rearrange("p (h i) -> p h i", h=HEADS)
            dve.tensor_tensor(r_cos[:].rearrange("p (h i) -> p h i", h=HEADS), p4,
                              rope[:, 0:1, :].broadcast_to([P, HEADS, HD]), ALU.mult).then_inc(done, 1)
            for e in range(2):
                swapped = psum_bank.rearrange("p (h i e) -> p h i e", h=HEADS, e=2)[:, :, :, 1 - e]
                o = r_sin[:].rearrange("p (h i e) -> p h i e", h=HEADS, e=2)[:, :, :, e]
                w = rope[:, 1:2, e::2].broadcast_to([P, HEADS, HD // 2])
                ins = dve.tensor_tensor(o, swapped, w, ALU.mult)
            ins.then_inc(done, 1)

        def next_stats(dve, t):
            dve.wait_ge(s3_x, t + 1)
            settle(dve)
            dve.bn_stats(st1[:], one_tile(t)).then_inc(s4_st, 1)
            dve.wait_ge(s4_st, t + 1)
            settle(dve)
            dve.bn_aggr(mv1[:, 0, :], st1[:]).then_inc(s4_ag, 1)
            dve.wait_ge(s4_ag, t + 1)
            dve.tensor_copy(mv3[:, bass.ds(t, 1), :], mv1[:]).then_inc(s4_mv, 1)

        def act_deviations(act, tiles):
            act.wait_ge(s4_mv, tiles.stop)
            act.activation(rs3[:, tiles], mv3[:, tiles, 1], ACT.Sqrt, bias=epsb[:]).then_inc(s4_sd, 1)

        def dve_deviations(dve, tiles, done):
            dve.wait_ge(s4_sd, done + 1)
            dve.reciprocal(rs3[:, tiles], rs3[:, tiles]).then_inc(s4_rs, 1)
            dve.wait_ge(s4_rs, done + 1)
            dve.scalar_tensor_tensor(out=nmr[:, tiles], in0=mv3[:, tiles, 0], scalar=-1.0, in1=rs3[:, tiles],
                                     op0=ALU.mult, op1=ALU.mult).then_inc(s4_nm, 1)

        MOST, REST = slice(0, G - CH), slice(G - CH, G)

        def dve3(dve, t, par):
            nxt = 1 - par
            if has(t - 2):
                next_stats(dve, t - 2)
            if has(t + 2) and not (isinstance(t, int) and t == -2):
                at_least(dve, s3_XT, t + 2)
                layer_norm(dve, t + 2)
            if has(t):
                at_least(dve, s3_PT, 2 * t - 2)
                for n in range(DT):
                    dve.wait_ge(s3_S, 4 * t + n + 1)
                    src = bank[4 + n % 2].rearrange("p (u w) -> p u w", w=P)[:, :, 0:SQ]
                    dve.scalar_tensor_tensor(out=sm[:, par, n].rearrange("p l b k -> p (l b) k"), in0=src,
                                             scalar=SCALE, in1=cmask[:].rearrange("p (a k) -> p a k", a=1)
                                             .broadcast_to([P, 4, SQ]), op0=ALU.mult, op1=ALU.add).then_inc(s3_ms, 1)
            if has(t + 1):
                dve.wait_ge(s3_Q, t + 2)
                rotate_parts(dve, bank[2], s3_rq, s3_ak, t + 1)
            if has(t):
                dve.wait_ge(s3_ms, 4 * t + 4)
                at_least(dve, s3_su, t)
                dve.tensor_reduce(mx3[:], sm[:, par].rearrange("p n l b k -> p (n l b) k"), AX_X,
                                  ALU.max).then_inc(s3_mx, 1)
            if has(t + 1):
                dve.wait_ge(s3_K, t + 2)
                rotate_parts(dve, bank[3], s3_rk, s3_aq, t + 2)
            if has(t - 1):
                at_least(dve, s3_PV, 2 * t - 2)
                for h in range(2):
                    for b in range(BPG):
                        src, high, low = p_block(h, b)
                        dve.wait_ge(s3_pa, 4 * (t - 1) + 2 * h + b + 1)
                        dve.tensor_tensor(low, src, high.bitcast(F32), ALU.subtract).then_inc(s3_pd, 1)
            if has(t - 1):
                at_least(dve, s3_Wo, t - 1)
                for pair in range(2):
                    for r in range(4):
                        src, high, low = o_block(pair, r)
                        dve.wait_ge(s3_oa, 8 * (t - 1) + 4 * pair + r + 1)
                        dve.tensor_tensor(low, src, high.bitcast(F32), ALU.subtract).then_inc(s3_od, 1)
            if has(t + 2):
                dve.wait_ge(s3_xh, t + 3)
                dve.tensor_tensor(x3_l[:, par].rearrange("p n c -> p (n c)"), bank[0],
                                  x3_h[:, par].rearrange("p n c -> p (n c)").bitcast(F32),
                                  ALU.subtract).then_inc(s3_xl, 1)
            if has(t + 1):
                dve.wait_ge(s3_vh, t + 2)
                dve.tensor_tensor(v_l[:, nxt, :], bank[2], v_h[:, nxt, :].bitcast(F32), ALU.subtract).then_inc(s3_v, 1)
            if has(t):
                dve.wait_ge(s3_ex, t + 1)
                dve.tensor_reduce(rc3[:, 0, :], sm[:, par].rearrange("p n l b k -> p (n l b) k"), AX_X,
                                  ALU.add).then_inc(s3_sm, 1)
                dve.wait_ge(s3_sm, t + 1)
                at_least(dve, s3_pn, t)
                dve.reciprocal(rc3[:, 1, :], rc3[:, 0, :]).then_inc(s3_rc, 1)
            if isinstance(t, int) and t == 0:
                dve.wait_ge(s3_z, 3)
                dve.wait_ge(s3_wa, 2)
                dve.tensor_tensor(ow_l[:], ow_r[:], ow_h[:].bitcast(F32), ALU.subtract).then_inc(s3_wd, 1)
            if isinstance(t, int) and t == G:
                dve_deviations(dve, MOST, 0)
            if has(t - 1):
                dve.wait_ge(s3_Wo, t)
                dve.tensor_tensor(one_tile(t - 1), bank[3], one_tile(t - 1), ALU.add).then_inc(s3_x, 1)

        def pool3(pool, t, par):
            if has(t + 1):
                pool.wait_ge(s3_rq, 2 * t + 4)
                at_least(pool, s3_Tq, t + 1)
                settle(pool)
                pool.tensor_tensor(q_r[:], r_cos[:], r_sin[:], ALU.add).then_inc(s3_aq, 1)
            if has(t):
                pool.wait_ge(s3_mx, t + 1)
                settle(pool)
                s_ = sm[:, par].rearrange("p n l b k -> p (n l b) k")
                pool.tensor_tensor(s_, s_, mx3[:].rearrange("p (u a) -> p u a", a=1).broadcast_to([P, HEADS, SQ]),
                                   ALU.subtract).then_inc(s3_su, 1)
            if has(t + 1):
                pool.wait_ge(s3_rk, 2 * t + 4)
                at_least(pool, s3_Tk, t + 1)
                settle(pool)
                pool.tensor_tensor(k_r[:], r_cos[:], r_sin[:], ALU.add).then_inc(s3_ak, 1)
            if has(t):
                pool.wait_ge(s3_rc, t + 1)
                settle(pool)
                s_ = sm[:, par].rearrange("p n l b k -> p (n l b) k")
                pool.tensor_tensor(s_, s_, rc3[:, 1, :].rearrange("p (u a) -> p u a", a=1)
                                   .broadcast_to([P, HEADS, SQ]), ALU.mult).then_inc(s3_pn, 1)

        def steps(eng, step, start=-2):
            for t in range(start, 2):
                step(eng, t, t % 2)
            with eng.Fori(1, G // 2 - 1) as h:
                step(eng, 2 * h, 0)
                step(eng, 2 * h + 1, 1)
            for t in range(G - 2, G + 1):
                step(eng, t, t % 2)

        with nc.Block() as block:
            @block.sync
            def _(sp):
                sp.dma_start(ow_r[:], ao.rearrange("(t p) n -> p t n", p=P)).then_inc(s3_w[3], 16)
                sp.dma_start(router_sb[:], router.rearrange("(a n) -> a n", a=1).broadcast_to([P, D]))\
                    .then_inc(s4_c, 16)
                sp.dma_start(same[:], same_in).then_inc(s4_c, 16)
                sp.dma_start(before[:], before_in).then_inc(s4_c, 16)
                sp.dma_start(slot_no[:], slot_in).then_inc(s4_c, 16)
                sp.dma_start(b1_sb[:], b1).then_inc(s4_c, 16)
                sp.dma_start(b2_sb[:], b2.rearrange("(a n) -> a n", a=1).broadcast_to([P, D])).then_inc(s4_c, 16)

            @block.gpsimd
            def _(pool):
                pool.memset(qb[:], 0.0).then_inc(s3_z, 1)
                pool.memset(pb_h[:].bitcast(F32), 0.0).then_inc(s3_z, 1)
                pool.memset(ones[:], 1.0).then_inc(s4_on, 1)
                pool.wait_ge(s3_wd, 2)
                pool.memset(pb_l[:].bitcast(F32), 0.0).then_inc(s3_z, 1)
                steps(pool, pool3)

            @block.vector
            def _(dve):
                def low(weights, h, l):
                    dve.tensor_tensor(l[:], raw3[:, weights], h[:].bitcast(F32), ALU.subtract).then_inc(s3_wd, 1)

                dve3(dve, -2, 0)
                dve_stats(dve, G)
                dve.wait_ge(s3_sd, 2)
                dve.reciprocal(rs3[:, G - 1:G], rs3[:, G - 1:G]).then_inc(s3_rs, 1)
                dve.wait_ge(s3_ws, 3)
                low(1, kw_h, kw_l)
                dve.wait_ge(s3_wa, 1)
                low(2, vw_h, vw_l)
                dve.wait_ge(s3_z, 2)
                dve.wait_ge(s3_c, 16 * 3 * BPG)
                steps(dve, dve3, -1)

            @block.scalar
            def _(act):
                act3(act, -2, 0)
                act.wait_ge(s3_w[2], 16)
                act.activation(vw_h[:], raw3[:, 2], ACT.Copy).then_inc(s3_wa, 1)
                act.wait_ge(s3_mv, G)
                act.activation(rs3[:, G - 1:G], mv3[:, G - 1, 1:2], ACT.Sqrt, bias=epsb[:]).then_inc(s3_sd, 1)
                act.wait_ge(s3_z, 2)
                steps(act, act3, -1)
                act_deviations(act, MOST)

            @block.tensor
            def _(pe):
                steps(pe, pe3)

        m = Map(nc, base)
        xs_h, xs_l = m("xs_h", [P, DT, ST * P], F32R), m("xs_l", [P, DT, ST * P], F32R)
        ohT = m("ohT", [P, G, P], F32)
        s_all, w_all = m("s_all", [P, G], F32), m("w_all", [P, G], F32)
        XN = 3
        xn4 = m("xn4", [P, XN, CH, D], F32)
        dots = m("dots", [P, CH, D], F32)
        dg = m("dg", [P, 2, CH, P], F32)
        r1, r2, rank = m("r1", [P, CH], F32), m("r2", [P, CH], F32), m("rank", [P, CH], F32)
        junk = m("junk", [P, 2 * CH, P], F32)
        oh = m("oh", [P, 2, CH, P], F32)

        s4_xn = sem("p4_xn")
        s4_s, s4_dg, s4_R, s4_eq = sem("p4_s"), sem("p4_dg"), sem("p4_R"), sem("p4_eq")
        s4_rk, s4_oh, s4_G, s4_T = sem("p4_rk"), sem("p4_oh"), sem("p4_G"), sem("p4_T")
        s4_gh, s4_gl, s4_oc, s4_tk, s4_sg = sem("p4_gh"), sem("p4_gl"), sem("p4_oc"), sem("p4_tk"), sem("p4_sg")

        DEEP = 4
        w_r = m("w_r", [P, DEEP, 2, D], F32)
        w_h, w_l = m("w_h", [P, DEEP, 2, D], F32R), m("w_l", [P, DEEP, 2, D], F32R)
        hid = m("hid", [P, 2, 4 * P], F32)
        hid_h, hid_l = m("hid_h", [P, 2, 4 * P], F32R), m("hid_l", [P, 2, 4 * P], F32R)
        y_sb = m("y_sb", [P, 4, D], F32)
        assert m.at <= nc.sbuf_usable_end, m.at
        SC = ST // 4
        TPC = G // SC

        s5_w = [sem(f"p5_w{i}") for i in range(DEEP)]
        s5_wh, s5_wl, s5_H, s5_Y = sem("p5_wh"), sem("p5_wl"), sem("p5_H"), sem("p5_Y")
        s5_g, s5_gh, s5_gl = sem("p5_g"), sem("p5_gh"), sem("p5_gl")
        s5_y, s5_Sc, s5_x, s5_out = sem("p5_y"), sem("p5_Sc"), sem("p5_x"), sem("p5_out")
        h_bank, sc_bank, y_bank = bank[0:2], bank[2:4], bank[4:8]

        EARLY = 2

        def load(sp, f, n, e):
            at_least(sp, s5_wl, n - DEEP + 1)
            settle(sp)
            sp.dma_start(w_r[:, e, 0, :], w1[bass.ds(f, 1), :, :].rearrange("a p n -> p (a n)")).then_inc(s5_w[e], 16)
            sp.dma_start(w_r[:, e, 1, :], w2[bass.ds(f, 1), :, :].rearrange("a p n -> p (a n)")).then_inc(s5_w[e], 16)

        def split_high(act, n, e):
            act.wait_ge(s5_w[e], 32 * (n // DEEP + 1) if isinstance(n, int) else (n - e) * (32 // DEEP) + 32)
            at_least(act, s5_Y, n - DEEP + 1)
            act.activation(w_h[:, e], w_r[:, e], ACT.Copy).then_inc(s5_wh, 1)

        def split_low(pool, n, e):
            pool.wait_ge(s5_wh, n + 1)
            settle(pool)
            pool.tensor_tensor(w_l[:, e], w_r[:, e], w_h[:, e].bitcast(F32), ALU.subtract).then_inc(s5_wl, 1)

        def ffn_tiles(eng, step, after):
            for q in range(SC):
                for f in range(DEEP):
                    step(f, q * FF + f, f, q)
                with eng.Fori(1, FF // DEEP - 1) as h:
                    for e in range(DEEP):
                        step(DEEP * h + e, q * FF + DEEP * h + e, e, q)
                for f in range(FF - DEEP, FF):
                    step(f, q * FF + f, f % DEEP, q)
                after(q)

        BANKS_OF = [(4, 5, 6, 7), (0, 1, 3, 2), (2, 3, 2, 3), (2, 3, 2, 3)]

        def bank4(c, i):
            return bank[BANKS_OF[c][i]]

        with nc.Block() as block:
            @block.sync
            def _(sp):
                for f in range(DEEP):
                    load(sp, f, f, f)
                def store(q):
                    if q == 0:
                        return
                    for t in range(G):
                        sp.wait_ge(s5_x, t + 1)
                        sp.dma_start(outt[:, t, :], tok[:, t, :]).then_inc(s5_out, 16)
                    sp.wait_ge(s5_out, 16 * G)
                ffn_tiles(sp, lambda f, n, e, q: None if isinstance(n, int) and n < DEEP else load(sp, f, n, e), store)

            @block.gpsimd
            def _(pool):
                def add(c):
                    pool.wait_ge(s4_xn, CH * c + CH)
                    t = tok[:, c * CH:(c + 1) * CH, :]
                    pool.tensor_tensor(t, t, xn4[:, c % XN], ALU.add).then_inc(s4_tk, 1)

                def split(f, n, e, q):
                    if isinstance(n, int) and n < NCH:
                        add(n)
                    split_low(pool, n, e)
                ffn_tiles(pool, split, lambda q: None)

            @block.vector
            def _(dve):
                def scores(c):
                    for t in range(CH):
                        dve.wait_ge(s4_xn, CH * c + t + 1)
                        n = CH * c + t
                        dve.tensor_tensor_reduce(dots[:, t, :], xn4[:, c % XN, t, :], router_sb[:], 1.0, 0.0,
                                                 ALU.mult, ALU.add, s_all[:, n:n + 1]).then_inc(s4_s, 1)
                    dve.wait_ge(s4_s, CH * c + CH)
                    if c >= 2:
                        dve.wait_ge(s4_R, c - 1)
                    dve.tensor_tensor(dg[:, c % 2], ident[:].rearrange("p (a n) -> p a n", a=1).broadcast_to([P, CH, P]),
                                      s_all[:, c * CH:(c + 1) * CH].rearrange("p (t a) -> p t a", a=1)
                                      .broadcast_to([P, CH, P]), ALU.mult).then_inc(s4_dg, 1)

                def compare(c):
                    dve.wait_ge(s4_R, c + 1)
                    for t in range(CH):
                        row, own = bank4(c, 0)[:, t * P:(t + 1) * P], s_all[:, c * CH + t:c * CH + t + 1]
                        dve.scalar_tensor_tensor(out=junk[:, 2 * t, :], in0=row, scalar=own, in1=same[:],
                                                 op0=ALU.is_gt, op1=ALU.mult, accum_out=r1[:, t:t + 1]).then_inc(s4_eq, 1)
                        dve.scalar_tensor_tensor(out=junk[:, 2 * t + 1, :], in0=row, scalar=own, in1=before[:],
                                                 op0=ALU.is_equal, op1=ALU.mult, accum_out=r2[:, t:t + 1]).then_inc(s4_eq, 1)

                def one_hot(c):
                    dve.wait_ge(s4_eq, 2 * CH * (c + 1))
                    dve.tensor_tensor(rank[:], r1[:], r2[:], ALU.add).then_inc(s4_rk, 1)
                    dve.wait_ge(s4_rk, c + 1)
                    if c >= 2:
                        dve.wait_ge(s4_T, c - 1)
                    for t in range(CH):
                        dve.tensor_scalar(oh[:, c % 2, t, :], slot_no[:, t % 2, :], rank[:, t:t + 1], None,
                                          ALU.is_equal).then_inc(s4_oh, 1)

                def low(c, h):
                    dve.wait_ge(s4_gh, 2 * c + h + 1)
                    at = slice((2 * c + h) * P, (2 * c + h + 1) * P)
                    dve.tensor_tensor(xs_l[:, :, at], bank4(c, 1 + h).rearrange("p (k n) -> p k n", k=DT),
                                      xs_h[:, :, at].bitcast(F32), ALU.subtract).then_inc(s4_gl, 1)

                dve.wait_ge(s4_c, 96)
                dve.wait_ge(s4_on, 1)
                scores(0)
                scores(1)
                compare(0)
                one_hot(0)
                compare(1)
                one_hot(1)
                next_stats(dve, G - 1)
                low(0, 0)
                low(0, 1)
                dve_deviations(dve, REST, 1)
                scores(2)
                low(1, 0)
                low(1, 1)
                scores(3)

                between = {0: lambda: (compare(2), one_hot(2)), 1: lambda: (low(2, 0), low(2, 1)),
                           2: lambda: (compare(3), one_hot(3)), 3: lambda: (low(3, 0), low(3, 1))}

                def split(f, n, e, q):
                    dve.wait_ge(s5_g, n + 1)
                    at_least(dve, s5_Y, n - 1)
                    e = e % 2
                    dve.tensor_copy(hid_h[:, e, :], hid[:, e, :]).then_inc(s5_gh, 1)
                    dve.wait_ge(s5_gh, n + 1)
                    dve.tensor_tensor(hid_l[:, e, :], hid[:, e, :], hid_h[:, e, :].bitcast(F32),
                                      ALU.subtract).then_inc(s5_gl, 1)
                    if isinstance(n, int) and n in between:
                        between[n]()

                def update(q):
                    dve.wait_ge(s5_Y, FF * (q + 1))
                    at_least(dve, s5_Sc, TPC * q)
                    for i in range(4):
                        dve.tensor_tensor(y_sb[:, i, :], y_bank[i], b2_sb[:], ALU.add).then_inc(s5_y, 1)
                    if q == 0:
                        dve.wait_ge(s4_sg, 1)
                        dve.wait_ge(s4_tk, NCH)
                    for t in range(TPC * q, TPC * (q + 1)):
                        dve.wait_ge(s5_Sc, t + 1)
                        dve.scalar_tensor_tensor(out=tok[:, t, :], in0=sc_bank[t % 2], scalar=w_all[:, t:t + 1],
                                                 in1=tok[:, t, :], op0=ALU.mult, op1=ALU.add).then_inc(s5_x, 1)
                ffn_tiles(dve, split, update)

            @block.scalar
            def _(act):
                def normalize(c):
                    if c >= XN:
                        act.wait_ge(s4_G, 2 * (c - XN + 1))
                        act.wait_ge(s4_tk, c - XN + 1)
                        act.wait_ge(s4_s, CH * (c - XN + 1))
                    for t in range(CH):
                        n = CH * c + t
                        act.activation(xn4[:, c % XN, t, :], tok[:, n, :], ACT.Identity, bias=nmr[:, n:n + 1],
                                       scale=rs3[:, n:n + 1]).then_inc(s4_xn, 1)

                def high(c, h):
                    act.wait_ge(s4_G, 2 * c + h + 1)
                    at = slice((2 * c + h) * P, (2 * c + h + 1) * P)
                    act.activation(xs_h[:, :, at], bank4(c, 1 + h).rearrange("p (k n) -> p k n", k=DT),
                                   ACT.Copy).then_inc(s4_gh, 1)

                def one_hots(c):
                    act.wait_ge(s4_T, c + 1)
                    act.activation(ohT[:, c * CH:(c + 1) * CH, :], bank4(c, 3).rearrange("p (k n) -> p k n", k=CH),
                                   ACT.Copy).then_inc(s4_oc, 1)

                for c in range(XN):
                    normalize(c)
                for f in range(EARLY):
                    split_high(act, f, f)
                high(0, 0)
                high(0, 1)
                one_hots(0)
                act_deviations(act, REST)
                act.wait_ge(s4_nm, 2)
                normalize(3)
                high(1, 0)
                high(1, 1)
                one_hots(1)

                def weights():
                    act.wait_ge(s4_s, G)
                    act.activation(w_all[:], s_all[:], ACT.Sigmoid).then_inc(s4_sg, 1)

                between = {0: weights, 2: lambda: (high(2, 0), high(2, 1), one_hots(2)),
                           3: lambda: (high(3, 0), high(3, 1), one_hots(3))}

                def gelu(f, n, e, q):
                    if not (isinstance(n, int) and n >= SC * FF - EARLY):
                        split_high(act, n + EARLY, (e + EARLY) % DEEP)
                    act.wait_ge(s5_H, n + 1)
                    at_least(act, s5_gl, n - 1)
                    act.activation(hid[:, e % 2, :], h_bank[e % 2], ACT.Gelu_apprx_tanh,
                                   bias=b1_sb[:, bass.ds(f, 1)]).then_inc(s5_g, 1)
                    if isinstance(n, int) and n in between:
                        between[n]()

                ffn_tiles(act, gelu, lambda q: None)

            @block.tensor
            def _(pe):
                def spread(c):
                    pe.wait_ge(s4_dg, c + 1)
                    if c >= 2:
                        pe.wait_ge(s4_oc, 2)
                        pe.wait_ge(s4_gl, 2 * c)
                    pe.matmul(bank4(c, 0), ones[:], dg[:, c % 2].rearrange("p a n -> p (a n)"), start=True, stop=True)\
                        .then_inc(s4_R, 1)

                def gather(c, h):
                    pe.wait_ge(s4_oh, CH * c + CH)
                    if c >= 2:
                        pe.wait_ge(s4_gl, 2 * c)
                        pe.wait_ge(s4_oc, c)
                    for k in range(DT):
                        for e in range(2):
                            ins = pe.matmul(bank4(c, 1 + h)[:, k * P:(k + 1) * P],
                                            xn4[:, c % XN, 2 * h + e, k * P:(k + 1) * P], oh[:, c % 2, 2 * h + e, :],
                                            start=(e == 0), stop=(e == 1))
                    ins.then_inc(s4_G, 1)

                def transpose(c):
                    pe.wait_ge(s4_oh, CH * c + CH)
                    if c >= 2:
                        pe.wait_ge(s4_gl, 2 * c + 1)
                    for t in range(CH):
                        ins = pe.transpose(bank4(c, 3)[:, t * P:(t + 1) * P], oh[:, c % 2, t, :], ident[:])
                    ins.then_inc(s4_T, 1)

                pe.wait_ge(s4_on, 1)
                spread(0)
                spread(1)
                for c in range(2):
                    gather(c, 0)
                    gather(c, 1)
                    transpose(c)
                spread(2)

                between = {1: lambda: (gather(2, 0), gather(2, 1), transpose(2)), 2: lambda: spread(3)}

                def hidden(n, e, q):
                    pe.wait_ge(s5_wl, n + 1)
                    at_least(pe, s5_g, n - 1)
                    for k in range(DT):
                        cols = slice(q * 4 * P, (q + 1) * 4 * P)
                        for i, (w, y) in enumerate(((w_h, xs_h), (w_l, xs_h), (w_h, xs_l))):
                            ins = pe.matmul(h_bank[e % 2], w[:, e, 0, k * P:(k + 1) * P], y[:, k, cols],
                                            start=(k == 0 and i == 0), stop=(k == DT - 1 and i == PRODUCTS - 1))
                    ins.then_inc(s5_H, 1)

                def scatter(q):
                    pe.wait_ge(s4_oc, NCH)
                    for t in range(TPC * q, TPC * (q + 1)):
                        pe.wait_ge(s5_y, 4 * q + t % TPC // 2 + 1)
                        at_least(pe, s5_x, t - 1)
                        pe.matmul(sc_bank[t % 2], ohT[:, t, :], y_sb[:, (t % TPC) // 2, :], start=True, stop=True)\
                            .then_inc(s5_Sc, 1)
                def step(f, n, e, q):
                    if isinstance(f, int) and f == 0:
                        if q == 0:
                            pe.wait_ge(s4_gl, 2 * NCH // SC)
                        else:
                            pe.wait_ge(s4_gl, 2 * NCH)
                        hidden(n, 0, q)
                        if q:
                            scatter(q - 1)
                    if not (isinstance(f, int) and f == FF - 1):
                        hidden(n + 1, (e + 1) % DEEP, q)
                    if isinstance(n, int) and n in between:
                        between[n]()
                    pe.wait_ge(s5_gl, n + 1)
                    for t in range(4):
                        for i, (h, w) in enumerate(((hid_h, w_h), (hid_h, w_l), (hid_l, w_h))):
                            ins = pe.matmul(y_bank[t], h[:, e % 2, t * P:(t + 1) * P], w[:, e, 1, :],
                                            start=(isinstance(f, int) and f == 0 and i == 0),
                                            stop=(isinstance(f, int) and f == FF - 1 and i == PRODUCTS - 1))
                    ins.then_inc(s5_Y, 1)
                    if isinstance(n, int) and n == 3:
                        gather(3, 0)
                        gather(3, 1)
                        transpose(3)

                ffn_tiles(pe, step, lambda q: scatter(q) if q == SC - 1 else None)


_INS = ["x", "ctx_768", "mask_BxS2_bf1", "L0_xattn_Wq", "L0_xattn_Wk", "L0_xattn_Wv", "L0_xattn_Wo",
        "L0_attn_wq", "L0_attn_wk", "L0_attn_wv", "L0_attn_wo", "L0_ffn_w_router", "L0_ffn_W1", "L0_ffn_b1",
        "L0_ffn_W2", "L0_ffn_b2"]


def constants(queries, hd, theta=10000.0):
    freq = np.float32(1.0) / np.float32(theta) ** (np.arange(0, hd, 2, dtype=np.float32) / np.float32(hd))
    ang = np.arange(queries, dtype=np.float32)[:, None] * freq[None, :]
    cos = np.repeat(np.cos(ang), 2, axis=1)
    sin = np.stack([-np.sin(ang), np.sin(ang)], axis=-1).reshape(queries, hd)
    seen = np.tril(np.ones((queries, queries), bool))
    token, batch = np.arange(P), np.arange(P) // queries
    same = batch[:, None] == batch[None, :]
    keep, slot = queries // 2, np.arange(P)
    mine = [(slot // keep)[None, :] == (2 * e + batch)[:, None] for e in (0, 1)]
    return {"cos": cos.astype(np.float32), "sin": sin.astype(np.float32),
            "causal": np.where(seen, 0.0, -BIG).astype(np.float32),
            "same": same.astype(np.float32),
            "before": (same & (token[None, :] < token[:, None])).astype(np.float32),
            "slot": np.stack([np.where(x, slot % keep, -1) for x in mine], axis=1).astype(np.float32)}


def kernel(**inputs):
    from concourse import bacc
    from concourse.bass_utils import run_bass_kernel_spmd

    nc = bacc.Bacc("TRN2", target_bir_lowering=False, num_devices=1)
    arrays, args = {}, []
    for name in _INS:
        a = np.ascontiguousarray(inputs[name])
        if name == "ctx_768":
            a = np.ascontiguousarray(a.transpose(0, 2, 1))
        if name == "mask_BxS2_bf1":
            a = a.view(np.uint8)
        if name == "L0_ffn_W1":
            d, f = a.shape
            a = np.ascontiguousarray(a.reshape(d // P, P, f // P, P).transpose(2, 1, 0, 3)).reshape(f // P, P, d)
        if name == "L0_ffn_W2":
            a = a.reshape(-1, P, a.shape[1])
        if name == "L0_ffn_b1":
            a = np.ascontiguousarray(a.reshape(-1, P).T)
        arrays[f"in_{name}"] = a
        args.append(nc.dram_tensor(f"in_{name}", a.shape, mybir.dt.from_np(a.dtype), kind="ExternalInput").ap())
    for name, a in constants(inputs["x"].shape[1], inputs["x"].shape[2] // HEADS).items():
        arrays[f"in_{name}"] = a
        args.append(nc.dram_tensor(f"in_{name}", a.shape, F32, kind="ExternalInput").ap())
    out = nc.dram_tensor("out", inputs["x"].shape, F32, kind="ExternalOutput").ap()
    perceiver_layer(nc, *args, out)
    r = run_bass_kernel_spmd(nc, [arrays], core_ids=[0])
    return r.results[0]["out"]
```
